# Optimizing a Trainium2 kernel written in Bass

```python
import numpy as np
import jax
import jax.numpy as jnp

def _softmax(x, axis=-1):
    return jax.nn.softmax(x, axis=axis)

def _gelu(x):
    return jax.nn.gelu(x, approximate=True)

def _silu(x):
    return jax.nn.silu(x)

def _sigmoid(x):
    return jax.nn.sigmoid(x)

def _layernorm(x, axis=-1, eps=1e-05):
    m = jnp.mean(x, axis=axis, keepdims=True)
    v = jnp.var(x, axis=axis, keepdims=True)
    return (x - m) / jnp.sqrt(v + eps)

def _scatter_add(tgt, idx, src, axis=0):
    return tgt.at[idx].add(src)

def _segment_sum(src, seg, n):
    return jax.ops.segment_sum(src, seg, n)
kernel_name = 'mk_decoder_preln_d4_seqx_r8_58a208'

def setup_inputs(seed: int=0):
    np.random.seed(seed)
    _w = jnp.asarray

    def _rec_inputs():
        import jax
        import jax.numpy as jnp
        _rk = jax.random.key(seed)
        x = 7.22e-05 + 1 * jax.random.normal(jax.random.fold_in(_rk, 1), (16, 256, 128), jnp.float32)
        _lenS = 256 - jax.random.randint(jax.random.fold_in(_rk, 7), (16,), 0, max(1, 256 // 4) + 1, jnp.int32)
        _lenS2 = 64 - jax.random.randint(jax.random.fold_in(_rk, 8), (16,), 0, max(1, 64 // 4) + 1, jnp.int32)
        _ctx_1024P = jax.random.normal(jax.random.fold_in(_rk, 11), (16, 16, 128), jnp.float32)
        _ctx_1024c = jax.random.dirichlet(jax.random.fold_in(_rk, 511), 0.3 * jnp.ones((16,), jnp.float32), (16, 64))
        _ctx_1024t = jnp.einsum('bsk,bkd->bsd', _ctx_1024c, _ctx_1024P)
        _ctx_1024t = _ctx_1024t * jax.lax.rsqrt(jnp.mean(jnp.square(_ctx_1024t)) + 1e-12) * 0.953939
        ctx_1024 = 4.13588e-05 + 0.999923 * (_ctx_1024t + 0.3 * jax.random.normal(jax.random.fold_in(_rk, 611), (16, 64, 128), jnp.float32))
        _validS = jnp.arange(256)[None, :] < _lenS[:, None]
        _validS2 = jnp.arange(64)[None, :] < _lenS2[:, None]
        _causal = jnp.tril(jnp.ones((256, 256), dtype=bool))
        mask_BxS2_bf1 = jnp.ones((16, 64), dtype=bool)
        return (x, ctx_1024, mask_BxS2_bf1)
    x, ctx_1024, mask_BxS2_bf1 = _rec_inputs()

    def _L0_attn_setup():
        import jax, jax.numpy as jnp
        import numpy as np
        EMBED = 128
        HEADS = 16
        HEAD_DIM = EMBED // HEADS
        RANK = 8
        ALPHA = 16
        SCALING = ALPHA / RANK

        def _lora_linear(x, W, b, A, Bm):
            return x @ W + b + x @ A @ Bm * SCALING
        key = jax.random.key(seed)
        ks = jax.random.split(key, 9)
        s = 0.02
        x = jax.random.normal(ks[0], (4, 256, EMBED), dtype=jnp.float32)
        W_qkv = jax.random.normal(ks[1], (EMBED, 3 * EMBED), dtype=jnp.float32) * s
        b_qkv = jax.random.normal(ks[2], (3 * EMBED,), dtype=jnp.float32) * s
        A_qkv = jax.random.normal(ks[3], (EMBED, RANK), dtype=jnp.float32) * s
        B_qkv = jax.random.normal(ks[4], (RANK, 3 * EMBED), dtype=jnp.float32) * s
        W_proj = jax.random.normal(ks[5], (EMBED, EMBED), dtype=jnp.float32) * s
        b_proj = jax.random.normal(ks[6], (EMBED,), dtype=jnp.float32) * s
        A_proj = jax.random.normal(ks[7], (EMBED, RANK), dtype=jnp.float32) * s
        B_proj = jax.random.normal(ks[8], (RANK, EMBED), dtype=jnp.float32) * s
        return dict(x=x, W_qkv=W_qkv, b_qkv=b_qkv, A_qkv=A_qkv, B_qkv=B_qkv, W_proj=W_proj, b_proj=b_proj, A_proj=A_proj, B_proj=B_proj)
    _L0_attn_all = _L0_attn_setup()
    _L0_attn_in = {k: v for k, v in _L0_attn_all.items() if k in ('W_qkv', 'b_qkv', 'A_qkv', 'B_qkv', 'W_proj', 'b_proj', 'A_proj', 'B_proj')}
    del _L0_attn_all

    def _L0_xattn_setup():
        import jax, jax.numpy as jnp
        import numpy as np
        B, S, D = (4, 256, 128)
        key = jax.random.key(seed)
        ks = jax.random.split(key, 10)
        sc = 1.0 / np.sqrt(D)
        return {'x': jax.random.normal(ks[0], (B, S, D), dtype=jnp.float32), 'y': jax.random.normal(ks[1], (B, S, D), dtype=jnp.float32), 'Wq': jax.random.normal(ks[2], (D, D), dtype=jnp.float32) * sc, 'bq': jnp.zeros((D,), dtype=jnp.float32), 'Wk': jax.random.normal(ks[3], (D, D), dtype=jnp.float32) * sc, 'bk': jnp.zeros((D,), dtype=jnp.float32), 'Wv': jax.random.normal(ks[4], (D, D), dtype=jnp.float32) * sc, 'bv': jnp.zeros((D,), dtype=jnp.float32), 'Wr': jax.random.normal(ks[5], (D, D), dtype=jnp.float32) * sc, 'br': jnp.zeros((D,), dtype=jnp.float32)}
    _L0_xattn_all = _L0_xattn_setup()
    _L0_xattn_in = {k: v for k, v in _L0_xattn_all.items() if k in ('Wq', 'bq', 'Wk', 'bk', 'Wv', 'bv', 'Wr', 'br')}
    del _L0_xattn_all

    def _L0_ffn_setup():
        import jax, jax.numpy as jnp
        import numpy as np
        H = 128
        I = 128
        E = 16
        K = 4
        LIMIT = 7.0
        ALPHA = 1.702
        EPS = 1e-05
        key = jax.random.key(seed)
        ks = jax.random.split(key, 8)
        x = jax.random.normal(ks[0], (2, 64, H), dtype=jnp.float32)
        norm_scale = jnp.ones((H,), dtype=jnp.float32)
        wg = jax.random.normal(ks[1], (H, E), dtype=jnp.float32) * 0.02
        bg = jax.random.normal(ks[2], (E,), dtype=jnp.float32) * 0.02
        w1 = jax.random.normal(ks[3], (E, H, 2 * I), dtype=jnp.float32) * 0.02
        b1 = jax.random.normal(ks[4], (E, 2 * I), dtype=jnp.float32) * 0.02
        w2 = jax.random.normal(ks[5], (E, I, H), dtype=jnp.float32) * 0.02
        b2 = jax.random.normal(ks[6], (E, H), dtype=jnp.float32) * 0.02
        return {'x': x, 'norm_scale': norm_scale, 'wg': wg, 'bg': bg, 'w1': w1, 'b1': b1, 'w2': w2, 'b2': b2}
    _L0_ffn_all = _L0_ffn_setup()
    _L0_ffn_in = {k: v for k, v in _L0_ffn_all.items() if k in ('norm_scale', 'wg', 'bg', 'w1', 'b1', 'w2', 'b2')}
    del _L0_ffn_all

    def _L1_attn_setup():
        import jax, jax.numpy as jnp
        import numpy as np
        import math
        N_EMBD = 128
        NUM_HEADS = 16
        HEAD_DIM = N_EMBD // NUM_HEADS

        def alibi_slopes(num_heads):
            x = (2 ** 8) ** (1.0 / num_heads)
            return jnp.array([1.0 / x ** (i + 1) for i in range(num_heads)], dtype=jnp.float32)
        key = jax.random.key(seed)
        k1, k2 = jax.random.split(key)
        x = jax.random.normal(k1, (2, 256, N_EMBD), dtype=jnp.float32)
        W_kqv = jax.random.normal(k2, (3 * N_EMBD, N_EMBD), dtype=jnp.float32) * (1.0 / math.sqrt(N_EMBD))
        return {'x': x, 'W_kqv': W_kqv}
    _L1_attn_all = _L1_attn_setup()
    _L1_attn_in = {k: v for k, v in _L1_attn_all.items() if k in ('W_kqv',)}
    del _L1_attn_all

    def _L1_xattn_setup():
        import jax, jax.numpy as jnp
        import numpy as np
        B, L_ENC, L_DEC, D = (16, 64, 128, 128)
        key = jax.random.key(seed)
        k1, k2, k3, k4, k5, k6 = jax.random.split(key, 6)
        encoder_hc = jax.random.normal(k1, (B, L_ENC, D), dtype=jnp.float32)
        decoder_hq = jax.random.normal(k2, (B, L_DEC, D), dtype=jnp.float32)
        w_sim = jax.random.normal(k3, (3 * D,), dtype=jnp.float32) * 0.02
        b_sim = jax.random.normal(k4, (1,), dtype=jnp.float32) * 0.02
        W_qv = jax.random.normal(k5, (4 * D, D), dtype=jnp.float32) * 0.02
        b_qv = jax.random.normal(k6, (D,), dtype=jnp.float32) * 0.02
        return {'encoder_hc': encoder_hc, 'decoder_hq': decoder_hq, 'w_sim': w_sim, 'b_sim': b_sim, 'W_qv': W_qv, 'b_qv': b_qv}
    _L1_xattn_all = _L1_xattn_setup()
    _L1_xattn_in = {k: v for k, v in _L1_xattn_all.items() if k in ('w_sim', 'b_sim', 'W_qv', 'b_qv')}
    del _L1_xattn_all

    def _L1_ffn_setup():
        import jax, jax.numpy as jnp
        import numpy as np
        B, T, D, H = (4, 256, 128, 256)
        E, S, K = (8, 2, 2)

        def _swiglu_stacked(x, w1, b1, w2, b2, w3, b3):
            p1 = jnp.einsum('btd,ndh->nbth', x, w1) + b1[:, None, None, :]
            p2 = jnp.einsum('btd,ndh->nbth', x, w2) + b2[:, None, None, :]
            glu = jax.nn.silu(p1) * p2
            return jnp.einsum('nbth,nhd->nbtd', glu, w3) + b3[:, None, None, :]
        key = jax.random.key(seed)
        ks = jax.random.split(key, 10)
        s = 0.02
        return {'x': jax.random.normal(ks[0], (B, T, D), jnp.float32), 'gate_w': jax.random.normal(ks[1], (D, E), jnp.float32) * s, 'gate_b': jnp.zeros((E,), jnp.float32), 'rw1': jax.random.normal(ks[2], (E, D, H), jnp.float32) * s, 'rb1': jnp.zeros((E, H), jnp.float32), 'rw2': jax.random.normal(ks[3], (E, D, H), jnp.float32) * s, 'rb2': jnp.zeros((E, H), jnp.float32), 'rw3': jax.random.normal(ks[4], (E, H, D), jnp.float32) * s, 'rb3': jnp.zeros((E, D), jnp.float32), 'sw1': jax.random.normal(ks[5], (S, D, H), jnp.float32) * s, 'sb1': jnp.zeros((S, H), jnp.float32), 'sw2': jax.random.normal(ks[6], (S, D, H), jnp.float32) * s, 'sb2': jnp.zeros((S, H), jnp.float32), 'sw3': jax.random.normal(ks[7], (S, H, D), jnp.float32) * s, 'sb3': jnp.zeros((S, D), jnp.float32)}
    _L1_ffn_all = _L1_ffn_setup()
    _L1_ffn_in = {k: v for k, v in _L1_ffn_all.items() if k in ('gate_w', 'gate_b', 'rw1', 'rb1', 'rw2', 'rb2', 'rw3', 'rb3', 'sw1', 'sb1', 'sw2', 'sb2', 'sw3', 'sb3')}
    del _L1_ffn_all

    def _L2_attn_setup():
        import jax, jax.numpy as jnp
        import numpy as np
        _DENSE_LOCAL_W = 32
        _DYADIC = [48, 64, 96, 128, 192, 32, 48, 64, 96, 128, 192]
        OFFSETS = sorted(set(range(_DENSE_LOCAL_W + 1)) | set(_DYADIC))
        B, N, D, H = (2, 512, 128, 16)
        HD = D // H
        NEG = -1e+30

        def _shift(t, o):
            if o == 0:
                return t
            n = t.shape[2]
            return jnp.pad(t, ((0, 0), (0, 0), (o, 0), (0, 0)))[:, :, :n]
        key = jax.random.key(seed)
        ks = jax.random.split(key, 9)
        alphas = jnp.linspace(0.2, 2.0, H)
        delta = jnp.log1p(jnp.asarray(OFFSETS, dtype=jnp.float32))
        pos_bias = -delta[:, None] * alphas[None, :]
        return {'x': jax.random.normal(ks[0], (B, N, D), jnp.float32), 'qkv_w': jax.random.normal(ks[1], (3 * D, D), jnp.float32) * 0.02, 'qkv_b': jax.random.normal(ks[2], (3 * D,), jnp.float32) * 0.01, 'out_w': jax.random.normal(ks[3], (D, D), jnp.float32) * 0.02, 'out_b': jnp.zeros((D,), jnp.float32), 'gate_w': jax.random.normal(ks[4], (D, D), jnp.float32) * 0.02, 'gate_b': jnp.zeros((D,), jnp.float32), 'pos_bias': pos_bias, 'scale_embed': jax.random.normal(ks[5], (len(OFFSETS), HD), jnp.float32) * 0.02, 'if_gain': 1.0 + jax.random.normal(ks[6], (H,), jnp.float32) * 0.05}
    _L2_attn_all = _L2_attn_setup()
    _L2_attn_in = {k: v for k, v in _L2_attn_all.items() if k in ('qkv_w', 'qkv_b', 'out_w', 'out_b', 'gate_w', 'gate_b', 'pos_bias', 'scale_embed', 'if_gain')}
    del _L2_attn_all

    def _L2_xattn_setup():
        import jax, jax.numpy as jnp
        import numpy as np
        N_HEADS = 16
        D_MODEL = 128
        HEAD_DIM = D_MODEL // N_HEADS
        MASK_FILL = -100000000.0

        def _split_heads(x):
            B, S, _ = x.shape
            return x.reshape(B, S, N_HEADS, HEAD_DIM).transpose(0, 2, 1, 3)
        key = jax.random.key(seed)
        ks = jax.random.split(key, 12)
        B, L, P = (2, 256, 256)
        s = 1.0 / np.sqrt(D_MODEL).astype(np.float32)
        inp = {'q': jax.random.normal(ks[0], (B, L, D_MODEL), dtype=jnp.float32), 'k': jax.random.normal(ks[1], (B, P, D_MODEL), dtype=jnp.float32), 'v': jax.random.normal(ks[2], (B, P, D_MODEL), dtype=jnp.float32), 'attention_mask': jnp.ones((B, P), dtype=bool), 'Wq': jax.random.normal(ks[3], (D_MODEL, D_MODEL), dtype=jnp.float32) * s, 'bq': jnp.zeros((D_MODEL,), dtype=jnp.float32), 'Wk': jax.random.normal(ks[4], (D_MODEL, D_MODEL), dtype=jnp.float32) * s, 'bk': jnp.zeros((D_MODEL,), dtype=jnp.float32), 'Wv': jax.random.normal(ks[5], (D_MODEL, D_MODEL), dtype=jnp.float32) * s, 'bv': jnp.zeros((D_MODEL,), dtype=jnp.float32), 'Wo': jax.random.normal(ks[6], (D_MODEL, D_MODEL), dtype=jnp.float32) * s, 'bo': jnp.zeros((D_MODEL,), dtype=jnp.float32)}
        return inp
    _L2_xattn_all = _L2_xattn_setup()
    _L2_xattn_in = {k: v for k, v in _L2_xattn_all.items() if k in ('Wq', 'bq', 'Wk', 'bk', 'Wv', 'bv', 'Wo', 'bo')}
    del _L2_xattn_all

    def _L2_ffn_setup():
        import jax, jax.numpy as jnp
        import numpy as np
        B, S, D = (2, 256, 128)
        E, H, K = (8, 704, 2)
        N_RESERVED = 4
        key = jax.random.key(seed)
        ks = jax.random.split(key, 5)
        scale = 0.02
        x = jax.random.normal(ks[0], (B, S, D), dtype=jnp.float32)
        gate_w = jax.random.normal(ks[1], (E, D), dtype=jnp.float32) * scale
        w1 = jax.random.normal(ks[2], (E, D, H), dtype=jnp.float32) * scale
        w3 = jax.random.normal(ks[3], (E, D, H), dtype=jnp.float32) * scale
        w2 = jax.random.normal(ks[4], (E, H, D), dtype=jnp.float32) * scale
        return {'x': x, 'gate_w': gate_w, 'w1': w1, 'w2': w2, 'w3': w3}
    _L2_ffn_all = _L2_ffn_setup()
    _L2_ffn_in = {k: v for k, v in _L2_ffn_all.items() if k in ('gate_w', 'w1', 'w2', 'w3')}
    del _L2_ffn_all

    def _L3_attn_setup():
        import jax, jax.numpy as jnp
        import numpy as np
        D = 128
        H = 16
        HD = D // H
        B = 2
        T = 256

        def _apply_rotary(x, rope):
            x1, x2 = (x[..., ::2], x[..., 1::2])
            sin, cos = (rope[..., ::2], rope[..., 1::2])
            return jnp.concatenate([x1 * cos - x2 * sin, x1 * sin + x2 * cos], axis=-1)
        key = jax.random.key(seed)
        k0, k1, k2 = jax.random.split(key, 3)
        s = 1.0 / np.sqrt(D)
        return {'x': jax.random.normal(k0, (B, T, D), dtype=jnp.float32), 'qkv_w': jax.random.normal(k1, (D, 3 * D), dtype=jnp.float32) * s, 'qkv_b': jnp.zeros((3 * D,), dtype=jnp.float32), 'out_w': jax.random.normal(k2, (D, D), dtype=jnp.float32) * s, 'out_b': jnp.zeros((D,), dtype=jnp.float32)}
    _L3_attn_all = _L3_attn_setup()
    _L3_attn_in = {k: v for k, v in _L3_attn_all.items() if k in ('qkv_w', 'qkv_b', 'out_w', 'out_b')}
    del _L3_attn_all

    def _L3_xattn_setup():
        import jax, jax.numpy as jnp
        import numpy as np
        EMBED = 128
        HEADS = 16
        HEAD_DIM = EMBED // HEADS
        key = jax.random.key(seed)
        ks = jax.random.split(key, 7)
        B, Sd, Se = (4, 256, 256)
        dec = jax.random.normal(ks[0], (B, Sd, EMBED), dtype=jnp.float32)
        enc = jax.random.normal(ks[1], (B, Se, EMBED), dtype=jnp.float32)
        scale = 1.0 / np.sqrt(EMBED)
        W_q = jax.random.normal(ks[2], (EMBED, EMBED), dtype=jnp.float32) * scale
        W_k = jax.random.normal(ks[3], (EMBED, EMBED), dtype=jnp.float32) * scale
        W_v = jax.random.normal(ks[4], (EMBED, EMBED), dtype=jnp.float32) * scale
        W_o = jax.random.normal(ks[5], (EMBED, EMBED), dtype=jnp.float32) * scale
        b_o = jax.random.normal(ks[6], (EMBED,), dtype=jnp.float32) * 0.01
        return {'decoder_input': dec, 'encoder_output': enc, 'W_q': W_q, 'W_k': W_k, 'W_v': W_v, 'W_o': W_o, 'b_o': b_o}
    _L3_xattn_all = _L3_xattn_setup()
    _L3_xattn_in = {k: v for k, v in _L3_xattn_all.items() if k in ('W_q', 'W_k', 'W_v', 'W_o', 'b_o')}
    del _L3_xattn_all

    def _L3_ffn_setup():
        import jax, jax.numpy as jnp
        import numpy as np
        CAPACITY = 0.5
        key = jax.random.key(seed)
        ks = jax.random.split(key, 7)
        b, s, d, h = (4, 1024, 128, 512)
        sc_r = 1.0 / np.sqrt(d)
        sc_1 = 1.0 / np.sqrt(d)
        sc_2 = 1.0 / np.sqrt(h)
        return {'x': jax.random.normal(ks[0], (b, s, d), dtype=jnp.float32), 'w_r': jax.random.uniform(ks[1], (d, 1), jnp.float32, -sc_r, sc_r), 'b_r': jax.random.uniform(ks[2], (1,), jnp.float32, -sc_r, sc_r), 'W1': jax.random.uniform(ks[3], (d, h), jnp.float32, -sc_1, sc_1), 'b1': jax.random.uniform(ks[4], (h,), jnp.float32, -sc_1, sc_1), 'W2': jax.random.uniform(ks[5], (h, d), jnp.float32, -sc_2, sc_2), 'b2': jax.random.uniform(ks[6], (d,), jnp.float32, -sc_2, sc_2)}
    _L3_ffn_all = _L3_ffn_setup()
    _L3_ffn_in = {k: v for k, v in _L3_ffn_all.items() if k in ('w_r', 'b_r', 'W1', 'b1', 'W2', 'b2')}
    del _L3_ffn_all
    return {'x': x, 'ctx_1024': ctx_1024, 'mask_BxS2_bf1': mask_BxS2_bf1, 'L0_attn_W_qkv': _L0_attn_in['W_qkv'], 'L0_attn_b_qkv': _L0_attn_in['b_qkv'], 'L0_attn_A_qkv': _L0_attn_in['A_qkv'], 'L0_attn_B_qkv': _L0_attn_in['B_qkv'], 'L0_attn_W_proj': _L0_attn_in['W_proj'], 'L0_attn_b_proj': _L0_attn_in['b_proj'], 'L0_attn_A_proj': _L0_attn_in['A_proj'], 'L0_attn_B_proj': _L0_attn_in['B_proj'], 'L0_xattn_Wq': _L0_xattn_in['Wq'], 'L0_xattn_bq': _L0_xattn_in['bq'], 'L0_xattn_Wk': _L0_xattn_in['Wk'], 'L0_xattn_bk': _L0_xattn_in['bk'], 'L0_xattn_Wv': _L0_xattn_in['Wv'], 'L0_xattn_bv': _L0_xattn_in['bv'], 'L0_xattn_Wr': _L0_xattn_in['Wr'], 'L0_xattn_br': _L0_xattn_in['br'], 'L0_ffn_norm_scale': _L0_ffn_in['norm_scale'], 'L0_ffn_wg': _L0_ffn_in['wg'], 'L0_ffn_bg': _L0_ffn_in['bg'], 'L0_ffn_w1': _L0_ffn_in['w1'], 'L0_ffn_b1': _L0_ffn_in['b1'], 'L0_ffn_w2': _L0_ffn_in['w2'], 'L0_ffn_b2': _L0_ffn_in['b2'], 'L1_attn_W_kqv': _L1_attn_in['W_kqv'], 'L1_xattn_w_sim': _L1_xattn_in['w_sim'], 'L1_xattn_b_sim': _L1_xattn_in['b_sim'], 'L1_xattn_W_qv': _L1_xattn_in['W_qv'], 'L1_xattn_b_qv': _L1_xattn_in['b_qv'], 'L1_ffn_gate_w': _L1_ffn_in['gate_w'], 'L1_ffn_gate_b': _L1_ffn_in['gate_b'], 'L1_ffn_rw1': _L1_ffn_in['rw1'], 'L1_ffn_rb1': _L1_ffn_in['rb1'], 'L1_ffn_rw2': _L1_ffn_in['rw2'], 'L1_ffn_rb2': _L1_ffn_in['rb2'], 'L1_ffn_rw3': _L1_ffn_in['rw3'], 'L1_ffn_rb3': _L1_ffn_in['rb3'], 'L1_ffn_sw1': _L1_ffn_in['sw1'], 'L1_ffn_sb1': _L1_ffn_in['sb1'], 'L1_ffn_sw2': _L1_ffn_in['sw2'], 'L1_ffn_sb2': _L1_ffn_in['sb2'], 'L1_ffn_sw3': _L1_ffn_in['sw3'], 'L1_ffn_sb3': _L1_ffn_in['sb3'], 'L2_attn_qkv_w': _L2_attn_in['qkv_w'], 'L2_attn_qkv_b': _L2_attn_in['qkv_b'], 'L2_attn_out_w': _L2_attn_in['out_w'], 'L2_attn_out_b': _L2_attn_in['out_b'], 'L2_attn_gate_w': _L2_attn_in['gate_w'], 'L2_attn_gate_b': _L2_attn_in['gate_b'], 'L2_attn_pos_bias': _L2_attn_in['pos_bias'], 'L2_attn_scale_embed': _L2_attn_in['scale_embed'], 'L2_attn_if_gain': _L2_attn_in['if_gain'], 'L2_xattn_Wq': _L2_xattn_in['Wq'], 'L2_xattn_bq': _L2_xattn_in['bq'], 'L2_xattn_Wk': _L2_xattn_in['Wk'], 'L2_xattn_bk': _L2_xattn_in['bk'], 'L2_xattn_Wv': _L2_xattn_in['Wv'], 'L2_xattn_bv': _L2_xattn_in['bv'], 'L2_xattn_Wo': _L2_xattn_in['Wo'], 'L2_xattn_bo': _L2_xattn_in['bo'], 'L2_ffn_gate_w': _L2_ffn_in['gate_w'], 'L2_ffn_w1': _L2_ffn_in['w1'], 'L2_ffn_w2': _L2_ffn_in['w2'], 'L2_ffn_w3': _L2_ffn_in['w3'], 'L3_attn_qkv_w': _L3_attn_in['qkv_w'], 'L3_attn_qkv_b': _L3_attn_in['qkv_b'], 'L3_attn_out_w': _L3_attn_in['out_w'], 'L3_attn_out_b': _L3_attn_in['out_b'], 'L3_xattn_W_q': _L3_xattn_in['W_q'], 'L3_xattn_W_k': _L3_xattn_in['W_k'], 'L3_xattn_W_v': _L3_xattn_in['W_v'], 'L3_xattn_W_o': _L3_xattn_in['W_o'], 'L3_xattn_b_o': _L3_xattn_in['b_o'], 'L3_ffn_w_r': _L3_ffn_in['w_r'], 'L3_ffn_b_r': _L3_ffn_in['b_r'], 'L3_ffn_W1': _L3_ffn_in['W1'], 'L3_ffn_b1': _L3_ffn_in['b1'], 'L3_ffn_W2': _L3_ffn_in['W2'], 'L3_ffn_b2': _L3_ffn_in['b2']}

def reference(x, ctx_1024, mask_BxS2_bf1, L0_attn_W_qkv, L0_attn_b_qkv, L0_attn_A_qkv, L0_attn_B_qkv, L0_attn_W_proj, L0_attn_b_proj, L0_attn_A_proj, L0_attn_B_proj, L0_xattn_Wq, L0_xattn_bq, L0_xattn_Wk, L0_xattn_bk, L0_xattn_Wv, L0_xattn_bv, L0_xattn_Wr, L0_xattn_br, L0_ffn_norm_scale, L0_ffn_wg, L0_ffn_bg, L0_ffn_w1, L0_ffn_b1, L0_ffn_w2, L0_ffn_b2, L1_attn_W_kqv, L1_xattn_w_sim, L1_xattn_b_sim, L1_xattn_W_qv, L1_xattn_b_qv, L1_ffn_gate_w, L1_ffn_gate_b, L1_ffn_rw1, L1_ffn_rb1, L1_ffn_rw2, L1_ffn_rb2, L1_ffn_rw3, L1_ffn_rb3, L1_ffn_sw1, L1_ffn_sb1, L1_ffn_sw2, L1_ffn_sb2, L1_ffn_sw3, L1_ffn_sb3, L2_attn_qkv_w, L2_attn_qkv_b, L2_attn_out_w, L2_attn_out_b, L2_attn_gate_w, L2_attn_gate_b, L2_attn_pos_bias, L2_attn_scale_embed, L2_attn_if_gain, L2_xattn_Wq, L2_xattn_bq, L2_xattn_Wk, L2_xattn_bk, L2_xattn_Wv, L2_xattn_bv, L2_xattn_Wo, L2_xattn_bo, L2_ffn_gate_w, L2_ffn_w1, L2_ffn_w2, L2_ffn_w3, L3_attn_qkv_w, L3_attn_qkv_b, L3_attn_out_w, L3_attn_out_b, L3_xattn_W_q, L3_xattn_W_k, L3_xattn_W_v, L3_xattn_W_o, L3_xattn_b_o, L3_ffn_w_r, L3_ffn_b_r, L3_ffn_W1, L3_ffn_b1, L3_ffn_W2, L3_ffn_b2):
    import jax
    import jax.numpy as jnp

    def _L0_attn_ref(x, W_qkv, b_qkv, A_qkv, B_qkv, W_proj, b_proj, A_proj, B_proj):
        import jax, jax.numpy as jnp
        import numpy as np
        EMBED = 128
        HEADS = 16
        HEAD_DIM = EMBED // HEADS
        RANK = 8
        ALPHA = 16
        SCALING = ALPHA / RANK

        def _lora_linear(x, W, b, A, Bm):
            return x @ W + b + x @ A @ Bm * SCALING
        B, N, C = x.shape
        qkv = _lora_linear(x, W_qkv, b_qkv, A_qkv, B_qkv)
        qkv = qkv.reshape(B, N, 3, HEADS, HEAD_DIM).transpose(2, 0, 3, 1, 4)
        q, k, v = (qkv[0], qkv[1], qkv[2])
        attn = jnp.einsum('bhnd,bhmd->bhnm', q, k) * HEAD_DIM ** (-0.5)
        attn = jax.nn.softmax(attn, axis=-1)
        out = jnp.einsum('bhnm,bhmd->bhnd', attn, v)
        out = out.transpose(0, 2, 1, 3).reshape(B, N, C)
        return _lora_linear(out, W_proj, b_proj, A_proj, B_proj)

    def _L0_xattn_ref(x, y, Wq, bq, Wk, bk, Wv, bv, Wr, br):
        import jax, jax.numpy as jnp
        import numpy as np
        B, S, D = (4, 256, 128)
        Q = jnp.einsum('bsd,de->bse', x, Wq) + bq
        K = jnp.einsum('bsd,de->bse', y, Wk) + bk
        V = jnp.einsum('bsd,de->bse', y, Wv) + bv
        K_hat = jnp.cos(jnp.einsum('bsd,dr->bsr', K, Wr) + br)
        scores = jnp.einsum('bqr,bkr->bqk', Q, K_hat)
        probs = jax.nn.softmax(scores, axis=-1)
        return jnp.einsum('bqk,bkd->bqd', probs, V)

    def _L0_ffn_ref(x, norm_scale, wg, bg, w1, b1, w2, b2):
        import jax, jax.numpy as jnp
        import numpy as np
        H = 128
        I = 128
        E = 16
        K = 4
        LIMIT = 7.0
        ALPHA = 1.702
        EPS = 1e-05
        shape = x.shape
        xf = x.reshape(-1, shape[-1])
        xn = xf * jax.lax.rsqrt(jnp.mean(xf * xf, axis=-1, keepdims=True) + EPS) * norm_scale
        logits = xn @ wg + bg
        vals, idx = jax.lax.top_k(logits, K)
        gates = jax.nn.softmax(vals, axis=-1)
        gate_full = jnp.einsum('tke,tk->te', jax.nn.one_hot(idx, E, dtype=gates.dtype), gates)
        h = jnp.einsum('th,ehd->etd', xn, w1) + b1[:, None, :]
        a = jnp.minimum(h[..., ::2], LIMIT)
        b = jnp.clip(h[..., 1::2], -LIMIT, LIMIT)
        s = a * jax.nn.sigmoid(ALPHA * a) * (b + 1.0)
        y = jnp.einsum('eti,eih->eth', s, w2) + b2[:, None, :]
        t = jnp.einsum('eth,te->th', y, gate_full)
        return x + t.reshape(shape)

    def _L1_attn_ref(x, W_kqv):
        import jax, jax.numpy as jnp
        import numpy as np
        import math
        N_EMBD = 128
        NUM_HEADS = 16
        HEAD_DIM = N_EMBD // NUM_HEADS

        def alibi_slopes(num_heads):
            x = (2 ** 8) ** (1.0 / num_heads)
            return jnp.array([1.0 / x ** (i + 1) for i in range(num_heads)], dtype=jnp.float32)
        B, S, E = x.shape
        H, D = (NUM_HEADS, HEAD_DIM)
        kqv = jnp.einsum('bse,fe->bsf', x, W_kqv)
        k, q, v = jnp.split(kqv, 3, axis=-1)
        q = q.reshape(B, S, H, D).transpose(0, 2, 1, 3)
        k = k.reshape(B, S, H, D).transpose(0, 2, 1, 3)
        v = v.reshape(B, S, H, D).transpose(0, 2, 1, 3)
        rel = jnp.arange(S)[None, :] - jnp.arange(S)[:, None]
        bias = alibi_slopes(H)[:, None, None] * rel.astype(jnp.float32)
        scale = math.sqrt(E)
        score = jnp.einsum('bhqd,bhkd->bhqk', q, k) / scale + bias[None]
        causal = jnp.tril(jnp.ones((S, S), dtype=bool))
        score = jnp.where(causal[None, None], score, -jnp.inf)
        attn = jax.nn.softmax(score, axis=-1)
        out = jnp.einsum('bhqk,bhkd->bhqd', attn, v)
        return out.transpose(0, 2, 1, 3).reshape(B, S, E)

    def _L1_xattn_ref(encoder_hc, decoder_hq, w_sim, b_sim, W_qv, b_qv):
        import jax, jax.numpy as jnp
        import numpy as np
        B, L_ENC, L_DEC, D = (16, 64, 128, 128)
        d = encoder_hc.shape[-1]
        w1, w2, w3 = (w_sim[:d], w_sim[d:2 * d], w_sim[2 * d:])
        Sim = (encoder_hc @ w1)[:, :, None] + (decoder_hq @ w2)[:, None, :] + jnp.einsum('bid,bjd->bij', encoder_hc * w3, decoder_hq) + b_sim[0]
        A = jax.nn.softmax(Sim, axis=2)
        hq_hat = jnp.einsum('bij,bjd->bid', A, decoder_hq)
        Batt = jax.nn.softmax(jnp.max(Sim, axis=2), axis=1)
        hc_bar = jnp.einsum('bi,bid->bd', Batt, encoder_hc)[:, None, :]
        hc_hat = jnp.broadcast_to(hc_bar, encoder_hc.shape)
        feats = jnp.concatenate([encoder_hc, hq_hat, encoder_hc * hq_hat, encoder_hc * hc_hat], axis=-1)
        hcq = feats @ W_qv + b_qv
        return hcq

    def _L1_ffn_ref(x, gate_w, gate_b, rw1, rb1, rw2, rb2, rw3, rb3, sw1, sb1, sw2, sb2, sw3, sb3):
        import jax, jax.numpy as jnp
        import numpy as np
        B, T, D, H = (4, 256, 128, 256)
        E, S, K = (8, 2, 2)

        def _swiglu_stacked(x, w1, b1, w2, b2, w3, b3):
            p1 = jnp.einsum('btd,ndh->nbth', x, w1) + b1[:, None, None, :]
            p2 = jnp.einsum('btd,ndh->nbth', x, w2) + b2[:, None, None, :]
            glu = jax.nn.silu(p1) * p2
            return jnp.einsum('nbth,nhd->nbtd', glu, w3) + b3[:, None, None, :]
        scores = jax.nn.softmax(x @ gate_w + gate_b, axis=-1)
        weights, indices = jax.lax.top_k(scores, K)
        routed_all = _swiglu_stacked(x, rw1, rb1, rw2, rb2, rw3, rb3)
        out_bted = jnp.transpose(routed_all, (1, 2, 0, 3))
        gathered = jnp.take_along_axis(out_bted, indices[..., None], axis=2)
        routed = jnp.sum(weights[..., None] * gathered, axis=2)
        shared = _swiglu_stacked(x, sw1, sb1, sw2, sb2, sw3, sb3).mean(axis=0)
        return shared + routed

    def _L2_attn_ref(x, qkv_w, qkv_b, out_w, out_b, gate_w, gate_b, pos_bias, scale_embed, if_gain):
        import jax, jax.numpy as jnp
        import numpy as np
        _DENSE_LOCAL_W = 32
        _DYADIC = [48, 64, 96, 128, 192, 32, 48, 64, 96, 128, 192]
        OFFSETS = sorted(set(range(_DENSE_LOCAL_W + 1)) | set(_DYADIC))
        B, N, D, H = (2, 512, 128, 16)
        HD = D // H
        NEG = -1e+30

        def _shift(t, o):
            if o == 0:
                return t
            n = t.shape[2]
            return jnp.pad(t, ((0, 0), (0, 0), (o, 0), (0, 0)))[:, :, :n]
        b, n, d = x.shape
        qkv = x @ qkv_w.T + qkv_b
        q, k, v = jnp.split(qkv, 3, axis=-1)
        heads = lambda t: t.reshape(b, n, H, HD).transpose(0, 2, 1, 3)
        q, k, v = (heads(q), heads(k), heads(v))
        inv = 1.0 / jnp.sqrt(jnp.asarray(HD, x.dtype))
        qs = jnp.einsum('bhnd,od->bhno', q, scale_embed)
        pos = jnp.arange(n)
        logits = []
        for i, o in enumerate(OFFSETS):
            qk = jnp.einsum('bhnd,bhnd->bhn', q, _shift(k, o))
            lg = qk * inv * (1.0 + qs[..., i]) + pos_bias[i][None, :, None]
            lg = jnp.where(pos[None, None, :] >= o, lg, NEG)
            logits.append(lg)
        logits = jnp.stack(logits, axis=-1)
        p = jax.nn.softmax(logits, axis=-1)
        out = jnp.zeros_like(q)
        for i, o in enumerate(OFFSETS):
            out = out + p[..., i][..., None] * _shift(v, o)
        out = out * if_gain[None, :, None, None]
        out_flat = out.transpose(0, 2, 1, 3).reshape(b, n, d)
        gate = jax.nn.sigmoid(x @ gate_w.T + gate_b)
        return out_flat * gate @ out_w.T + out_b

    def _L2_xattn_ref(q, k, v, attention_mask, Wq, bq, Wk, bk, Wv, bv, Wo, bo):
        import jax, jax.numpy as jnp
        import numpy as np
        N_HEADS = 16
        D_MODEL = 128
        HEAD_DIM = D_MODEL // N_HEADS
        MASK_FILL = -100000000.0

        def _split_heads(x):
            B, S, _ = x.shape
            return x.reshape(B, S, N_HEADS, HEAD_DIM).transpose(0, 2, 1, 3)
        qm = _split_heads(q @ Wq.T + bq)
        km = _split_heads(k @ Wk.T + bk)
        vm = _split_heads(v @ Wv.T + bv)
        scores = jnp.einsum('bnlh,bnph->bnlp', qm, km) / np.sqrt(HEAD_DIM).astype(np.float32)
        mask = attention_mask[:, None, None, :]
        scores = jnp.where(mask, scores, MASK_FILL)
        attn = jax.nn.softmax(scores, axis=-1)
        out = jnp.einsum('bnlp,bnph->bnlh', attn, vm)
        B, _, L, _ = out.shape
        out = out.transpose(0, 2, 1, 3).reshape(B, L, D_MODEL)
        return out @ Wo.T + bo

    def _L2_ffn_ref(x, gate_w, w1, w2, w3):
        import jax, jax.numpy as jnp
        import numpy as np
        B, S, D = (2, 256, 128)
        E, H, K = (8, 704, 2)
        N_RESERVED = 4
        b, s, d = x.shape
        T = b * s
        xf = x.reshape(T, d)
        logits = xf @ gate_w.T
        expert_ids = jnp.arange(E)
        logits = jnp.where(expert_ids[None, :] >= E - N_RESERVED, -jnp.inf, logits)
        weights = jax.nn.softmax(logits, axis=-1)
        top_w, top_idx = jax.lax.top_k(weights, K)
        top_w = top_w / jnp.sum(top_w, axis=-1, keepdims=True)
        cw = jnp.zeros((T, E), dtype=x.dtype).at[jnp.arange(T)[:, None], top_idx].add(top_w)
        h = jax.nn.silu(jnp.einsum('td,edh->teh', xf, w1)) * jnp.einsum('td,edh->teh', xf, w3)
        y = jnp.einsum('teh,ehd->ted', h, w2)
        out = jnp.einsum('te,ted->td', cw, y)
        return out.reshape(b, s, d)

    def _L3_attn_ref(x, qkv_w, qkv_b, out_w, out_b):
        import jax, jax.numpy as jnp
        import numpy as np
        D = 128
        H = 16
        HD = D // H
        B = 2
        T = 256

        def _apply_rotary(x, rope):
            x1, x2 = (x[..., ::2], x[..., 1::2])
            sin, cos = (rope[..., ::2], rope[..., 1::2])
            return jnp.concatenate([x1 * cos - x2 * sin, x1 * sin + x2 * cos], axis=-1)
        Bx, Tx, Dm = x.shape
        qkv = (x @ qkv_w + qkv_b).reshape(Bx, Tx, 3, H, HD).transpose(2, 0, 3, 1, 4)
        q, k, v = (qkv[0], qkv[1], qkv[2])
        inv_freq = 1.0 / 10000.0 ** (jnp.arange(0, HD, 2, dtype=jnp.float32) / HD)
        t = jnp.arange(Tx, dtype=jnp.float32)
        freqs = t[:, None] * inv_freq[None, :]
        rope = jnp.concatenate([jnp.sin(freqs), jnp.cos(freqs)], axis=-1)
        q = _apply_rotary(q, rope)
        k = _apply_rotary(k, rope)
        scale = HD ** (-0.5)
        scores = jnp.einsum('bhqd,bhkd->bhqk', q, k) * scale
        causal_mask = jnp.triu(jnp.ones((Tx, Tx), dtype=bool), 1)
        scores = jnp.where(causal_mask, -jnp.inf, scores)
        attn = jax.nn.softmax(scores, axis=-1)
        out = jnp.einsum('bhqk,bhkd->bhqd', attn, v)
        out = out.transpose(0, 2, 1, 3).reshape(Bx, Tx, Dm)
        return out @ out_w + out_b

    def _L3_xattn_ref(decoder_input, encoder_output, W_q, W_k, W_v, W_o, b_o):
        import jax, jax.numpy as jnp
        import numpy as np
        EMBED = 128
        HEADS = 16
        HEAD_DIM = EMBED // HEADS
        B, Sd, E = decoder_input.shape
        Se = encoder_output.shape[1]
        Q = (decoder_input @ W_q).reshape(B, Sd, HEADS, HEAD_DIM)
        K = (encoder_output @ W_k).reshape(B, Se, HEADS, HEAD_DIM)
        V = (encoder_output @ W_v).reshape(B, Se, HEADS, HEAD_DIM)
        scores = jnp.einsum('bqhd,bkhd->bhqk', Q, K) / jnp.sqrt(jnp.float32(HEAD_DIM))
        attn = jax.nn.softmax(scores, axis=-1)
        out = jnp.einsum('bhqk,bkhd->bqhd', attn, V).reshape(B, Sd, E)
        return out @ W_o + b_o

    def _L3_ffn_ref(x, w_r, b_r, W1, b1, W2, b2):
        import jax, jax.numpy as jnp
        import numpy as np
        CAPACITY = 0.5
        b, s, d = x.shape
        k = int(CAPACITY * s)
        weights = (jnp.einsum('bsd,do->bso', x, w_r) + b_r).squeeze(-1)
        top_vals, _ = jax.lax.top_k(weights, k)
        threshold = top_vals[:, -1]
        selected = weights > threshold[:, None]
        hidden = jax.nn.gelu(jnp.einsum('bsd,dh->bsh', x, W1) + b1, approximate=False)
        blk = jnp.einsum('bsh,hd->bsd', hidden, W2) + b2
        m = selected[..., None]
        return jnp.where(m, blk, x)
    x = x + _L0_attn_ref(_layernorm(x, axis=-1), L0_attn_W_qkv, L0_attn_b_qkv, L0_attn_A_qkv, L0_attn_B_qkv, L0_attn_W_proj, L0_attn_b_proj, L0_attn_A_proj, L0_attn_B_proj)
    x = x + _L0_xattn_ref(_layernorm(x, axis=-1), ctx_1024, L0_xattn_Wq, L0_xattn_bq, L0_xattn_Wk, L0_xattn_bk, L0_xattn_Wv, L0_xattn_bv, L0_xattn_Wr, L0_xattn_br)
    x = x + _L0_ffn_ref(_layernorm(x, axis=-1), L0_ffn_norm_scale, L0_ffn_wg, L0_ffn_bg, L0_ffn_w1, L0_ffn_b1, L0_ffn_w2, L0_ffn_b2)
    x = x + _L1_attn_ref(_layernorm(x, axis=-1), L1_attn_W_kqv)
    x = x + _L1_xattn_ref(_layernorm(x, axis=-1), ctx_1024, L1_xattn_w_sim, L1_xattn_b_sim, L1_xattn_W_qv, L1_xattn_b_qv)
    x = x + _L1_ffn_ref(_layernorm(x, axis=-1), L1_ffn_gate_w, L1_ffn_gate_b, L1_ffn_rw1, L1_ffn_rb1, L1_ffn_rw2, L1_ffn_rb2, L1_ffn_rw3, L1_ffn_rb3, L1_ffn_sw1, L1_ffn_sb1, L1_ffn_sw2, L1_ffn_sb2, L1_ffn_sw3, L1_ffn_sb3)
    x = x + _L2_attn_ref(_layernorm(x, axis=-1), L2_attn_qkv_w, L2_attn_qkv_b, L2_attn_out_w, L2_attn_out_b, L2_attn_gate_w, L2_attn_gate_b, L2_attn_pos_bias, L2_attn_scale_embed, L2_attn_if_gain)
    x = x + _L2_xattn_ref(_layernorm(x, axis=-1), ctx_1024, ctx_1024, mask_BxS2_bf1, L2_xattn_Wq, L2_xattn_bq, L2_xattn_Wk, L2_xattn_bk, L2_xattn_Wv, L2_xattn_bv, L2_xattn_Wo, L2_xattn_bo)
    x = x + _L2_ffn_ref(_layernorm(x, axis=-1), L2_ffn_gate_w, L2_ffn_w1, L2_ffn_w2, L2_ffn_w3)
    x = x + _L3_attn_ref(_layernorm(x, axis=-1), L3_attn_qkv_w, L3_attn_qkv_b, L3_attn_out_w, L3_attn_out_b)
    x = x + _L3_xattn_ref(_layernorm(x, axis=-1), ctx_1024, L3_xattn_W_q, L3_xattn_W_k, L3_xattn_W_v, L3_xattn_W_o, L3_xattn_b_o)
    x = x + _L3_ffn_ref(_layernorm(x, axis=-1), L3_ffn_w_r, L3_ffn_b_r, L3_ffn_W1, L3_ffn_b1, L3_ffn_W2, L3_ffn_b2)
    return x

_drawn_inputs = setup_inputs


def setup_inputs(seed=0):
    import zlib

    import numpy as np

    out = dict(_drawn_inputs(seed))
    spreads = {'L0_xattn_bq': (0.0, 0.1),
     'L0_xattn_bk': (0.0, 0.1),
     'L0_xattn_bv': (0.0, 0.1),
     'L0_xattn_br': (0.0, 0.1),
     'L0_ffn_norm_scale': (1.0, 0.6),
     'L1_ffn_gate_b': (0.0, 0.73),
     'L1_ffn_rb1': (0.0, 0.8),
     'L1_ffn_rb2': (0.0, 0.8),
     'L1_ffn_rb3': (0.0, 0.441),
     'L1_ffn_sb1': (0.0, 0.8),
     'L1_ffn_sb2': (0.0, 0.8),
     'L1_ffn_sb3': (0.0, 0.437),
     'L2_attn_out_b': (0.0, 0.352),
     'L2_attn_gate_b': (0.0, 0.8),
     'L2_xattn_bq': (0.0, 1.698),
     'L2_xattn_bk': (0.0, 2.0),
     'L2_xattn_bv': (0.0, 0.396),
     'L2_xattn_bo': (0.0, 0.37),
     'L3_attn_qkv_b': (0.0, 0.578),
     'L3_attn_out_b': (0.0, 0.607)}
    factors = {'L0_attn_W_qkv': 8.0,
     'L0_attn_b_qkv': 4.12,
     'L0_attn_A_qkv': 8.0,
     'L0_attn_B_qkv': 8.0,
     'L0_attn_W_proj': 3.914,
     'L0_attn_A_proj': 8.0,
     'L0_attn_B_proj': 8.0,
     'L0_ffn_wg': 4.169,
     'L0_ffn_bg': 7.835,
     'L0_ffn_w1': 3.957,
     'L0_ffn_b1': 8.0,
     'L0_ffn_w2': 3.731,
     'L0_ffn_b2': 8.0,
     'L1_xattn_w_sim': 3.145,
     'L1_xattn_b_qv': 5.382,
     'L1_ffn_gate_w': 3.532,
     'L1_ffn_rw1': 8.0,
     'L1_ffn_rw2': 8.0,
     'L1_ffn_rw3': 8.0,
     'L1_ffn_sw1': 6.239,
     'L1_ffn_sw2': 6.227,
     'L1_ffn_sw3': 6.181,
     'L2_attn_qkv_w': 4.783,
     'L2_attn_qkv_b': 8.0,
     'L2_attn_out_w': 4.127,
     'L2_attn_gate_w': 8.0,
     'L2_attn_pos_bias': 8.0,
     'L2_attn_scale_embed': 8.0,
     'L2_attn_if_gain': 8.0,
     'L2_ffn_gate_w': 7.432,
     'L2_ffn_w1': 4.423,
     'L2_ffn_w2': 4.417,
     'L2_ffn_w3': 7.031,
     'L3_xattn_b_o': 40.873,
     'L3_ffn_b1': 35.917,
     'L3_ffn_b2': 25.438,
     'L3_ffn_W1': 3.401,
     'L3_ffn_W2': 2.711}
    for name, (base, spread) in spreads.items():
        noise = np.random.default_rng([zlib.crc32(name.encode()), seed]).standard_normal(out[name].shape)
        drawn = base * np.exp(spread * noise) if base else spread * noise
        out[name] = jnp.asarray(drawn.astype(out[name].dtype))
    for name, factor in factors.items():
        out[name] = (out[name] * factor).astype(out[name].dtype)
    return out
```

```python
from contextlib import ExitStack

import numpy as np

import concourse.bass as bass
from concourse import mybir

P = 128
B = 16
SEQ = 256
CTX = 64
H = 16
HD = P // H
TT = SEQ // P
PAIR = 2
NT = PAIR * TT
W2 = PAIR * SEQ

F32 = mybir.dt.float32
BF16 = mybir.dt.bfloat16
U32 = mybir.dt.uint32
I32 = mybir.dt.int32
ALU = mybir.AluOpType
ACT = mybir.ActivationFunctionType
AX = mybir.AxisListType

NEG = -1e30
LN_EPS = 1e-5
ROOT_GUESS = float(0x5F3759DF)
MAGIC = 12582912.0
TWO_PI = (6.28125, 0.0019353071795864769)

OFFSETS = [8 * r + 7 - i for r in range(4) for i in range(8)] + [192, 128, 96, 64, 48, 32]
SORTED = sorted(OFFSETS)
NOFF = len(OFFSETS)
NSLOT = 10
PAD = max(OFFSETS)

E0, K0 = 16, 4
E1, K1, S1 = 8, 2, 2
E2, K2, HID2 = 4, 2, 704
EXPERTS = {"f0": (E0, K0), "f1": (E1, K1), "f2": (E2, K2)}
BIAS_AT = 5
CH0, CH1, CH2, CH3 = E0, 2 * (E1 + S1), E2 * HID2 // P, 4

LAYOUT = [
    [("ident", P), ("blk", 32), ("headmask", 32), ("sixteen", 16),
     ("a0_Wq", P), ("a0_Wk", P), ("a0_Wv", P), ("a0_Wo", P), ("a0_AT", P), ("a0_B", 3 * P),
     ("a0_AoT", P), ("a0_Bo", P), ("a0_bq", 1), ("a0_bk", 1), ("a0_bv", P), ("a0_bo", P),
     ("x0_Wq", P), ("x0_Wk", P), ("x0_Wv", P), ("x0_Wr", P), ("x0_bq", 1), ("x0_bk", 1), ("x0_br", 1), ("x0_bv", P)],
    [("f0_ns", 1), ("f0_wg", E0), ("f0_bg", E0), ("f0_w1", CH0 * P), ("f0_w3", CH0 * P), ("f0_w2", CH0 * P),
     ("f0_b1", CH0), ("f0_b3", CH0), ("f0_bt", P)],
    [("a1_Wq", P), ("a1_Wk", P), ("a1_Wv", P), ("x1_w1", 1), ("x1_w3", 1), ("x1_w2", 1), ("x1_bs", 1),
     ("x1_Wqv", 4 * P), ("x1_b", P),
     ("f1_wg", E1), ("f1_bg", E1), ("f1_w1", CH1 * P), ("f1_w3", CH1 * P), ("f1_w2", CH1 * P),
     ("f1_b1", CH1), ("f1_b3", CH1), ("f1_bt", P)],
    [("o_Wq", P), ("o_Wk", P), ("o_Wv", P), ("o_Wg", P), ("o_Wo", P), ("o_bq", 1), ("o_bk", 1), ("o_bv", 1),
     ("o_bg", 1), ("o_bo", P), ("o_gain", H), ("o_emb", 4 * NSLOT),
     ("a2_Wq", P), ("a2_Wk", P), ("a2_Wv", P), ("a2_Wo", P), ("a2_bq", 1), ("a2_bk", 1), ("a2_bv", P), ("a2_bo", P),
     ("f2_wg", E2), ("f2_w1", CH2 * P), ("f2_w3", CH2 * P), ("f2_w2", CH2 * P)],
    [("a3_Wq", P), ("a3_Wqs", P), ("a3_Wk", P), ("a3_Wks", P), ("a3_Wv", P), ("a3_Wo", P),
     ("a3_bq", 1), ("a3_bqs", 1), ("a3_bk", 1), ("a3_bks", 1), ("a3_bv", P), ("a3_bo", P), ("rope", 2 * SEQ),
     ("a4_Wq", P), ("a4_Wk", P), ("a4_Wv", P), ("a4_Wo", P), ("a4_bo", P),
     ("f3_wr", 1), ("f3_br", 1), ("f3_w1", CH3 * P), ("f3_w2", CH3 * P), ("f3_b1", CH3), ("f3_b2", P)],
]
COLS = {}
GROUP = []
_at = 0
for _g in LAYOUT:
    _from = _at
    for _name, _n in _g:
        COLS[_name] = (_at, _n)
        _at += _n
    GROUP.append((_from, _at))
NW = _at
BCOLS = {"sel": (0, H), "identb": (H, P), "mask_qk": (H + P, 3 * P), "mask_kq": (H + 4 * P, 3 * P)}
NBC = H + 7 * P

Q_PARTS = (0, 0, 0, 1, 1, 2)
K_PARTS = (0, 1, 2, 0, 1, 0)
ROWS = 8 * len(Q_PARTS)

GROUP_OF = {"a0": 0, "x0": 0, "f0": 1, "a1": 2, "x1": 2, "f1": 2, "o": 3, "a2": 3, "f2": 3, "a3": 4, "a4": 4, "f3": 4}
STAGES = ["a0", "x0", "f0", "a1", "x1", "f1", "o", "a2", "f2", "a3", "a4", "f3"]
ATT = {"a0": (SEQ, False, HD ** -0.5), "a1": (SEQ, True, P ** -0.5), "a2": (CTX, False, HD ** -0.5),
       "a3": (SEQ, True, 1.0), "a4": (CTX, False, HD ** -0.5)}


class Signal:

    def __init__(self, sem, keys, by=1):
        self.s = sem
        self.value = {k: by * (i + 1) for i, k in enumerate(keys)}

    def at(self, *key):
        return self.value[key]


class Ring:

    def __init__(self, tile, full):
        self.tile, self.full = tile, full
        self.n, self.fills, self.drains = 0, {}, [None] * len(full)

    def take(self, key, drained):
        slot = self.n % len(self.full)
        before, self.drains[slot] = self.drains[slot], drained
        assert key not in self.fills, key
        self.fills[key] = (slot, self.n // len(self.full) + 1)
        self.n += 1
        return slot, before

    def at(self, *key):
        return self.fills[key]


def build_decoder(nc, x_in, ctx_in, mask_in, packed, packed_bf, rows_alibi, rows_const, rows_pb, scratch_q, scratch_k, scratch_kc, out,
                  stages=STAGES, iters=B // PAIR):
    ctx = ExitStack()
    with ctx:
        def sb(name, shape, dt=F32):
            return ctx.enter_context(nc.sbuf_tensor(name, shape, dt))

        def sem(name):
            return ctx.enter_context(nc.semaphore(name))

        two = range(PAIR)

        wt = sb("weights", [P, NW])
        cb = sb("constants_bf", [P, NBC], BF16)
        x = sb("x", [P, PAIR, TT, P])
        xn = sb("xn", [P, PAIR, TT, P])
        xnT = sb("xnT", [P, PAIR, SEQ])
        ctok = sb("ctok", [CTX, PAIR, P])
        ctxT = sb("ctxT", [P, PAIR, CTX])
        mask8 = sb("mask8", [P, PAIR, CTX], mask_in.dtype)
        maskf = sb("maskf", [P, PAIR, CTX])
        maskneg = sb("maskneg", [P, PAIR, CTX], BF16)
        zrow = sb("zrow", [P, 2])
        bn = sb("bn_stats", [P, PAIR, TT, 6])
        mv = sb("mv", [P, NT, 2])
        var = sb("var", [P, NT])
        rstd = sb("rstd", [P, NT])
        nt = sb("newton", [P, NT])
        sumsq = sb("sumsq", [P, NT])
        halfpi = sb("halfpi", [P, 1])
        ones = sb("ones", [P, P])
        emb = sb("emb", [P, NSLOT, P])
        pbias = sb("pbias", [P, TT, 4 * NSLOT, H])
        qs = sb("q_stack", [P, PAIR, H // 2, SEQ], BF16)
        ks = sb("k_stack", [P, PAIR, 2, H // 2, SEQ], BF16)
        vaug = sb("vaug", [P, PAIR, TT, H, HD + 1])
        negm = sb("negm", [P, PAIR, TT, H])
        mres = sb("mres", [P, PAIR, TT, H])
        mparts = sb("mparts", [P, PAIR, TT, P], BF16)
        negmT = sb("negmT", [P, PAIR, SEQ], BF16)
        rinv = sb("rinv", [P, PAIR, TT, H])
        small = sb("small", [P, PAIR, 16])
        lg = sb("lg", [P, NT, 16])
        ex = sb("ex", [P, NT, 16])
        em = sb("em", [P, NT, 16])
        top = sb("top", [P, NT, 8])
        topi = sb("topi", [P, NT, 8], U32)
        topf = sb("topf", [P, NT, 8])
        hot = sb("hot", [P, NT, 4, 16])
        rsum = sb("rsum", [P, NT, 2])
        gates = sb("gates", [P, NT, 16])
        gatesT = sb("gatesT", [16, W2])
        work = sb("work", [P, 8064])

        def w(name):
            a, n = COLS[name]
            return wt[:, a:a + n]

        def wb(name):
            a, n = BCOLS[name]
            return cb[:, a:a + n]

        def cut(at, *dims):
            n = int(np.prod(dims))
            v = work[:, at:at + n]
            if len(dims) == 1:
                return v
            names = "abcd"[:len(dims)]
            return v.rearrange(f"p ({' '.join(names)}) -> p {' '.join(names)}", **dict(zip(names[1:], dims[1:])))

        qk = cut(0, PAIR, 2 * SEQ)
        res = cut(1024, PAIR, 2 * SEQ)
        parts = work[:, 2048:3584].bitcast(BF16).rearrange("p (b c t) -> p b c t", b=PAIR, c=3)
        probs = cut(3584, 2, 1024)
        osp = cut(5632, PAIR, 4, SEQ)
        otok = cut(0, PAIR, TT, P)
        oT = cut(512, PAIR, SEQ)
        rt = cut(5632, 2, SEQ)
        zc = cut(1024, PAIR, CTX)
        zn = cut(1152, PAIR, CTX)
        khat = cut(1280, PAIR, CTX)
        pr = cut(1408, PAIR, TT, CTX)
        sim = cut(1664, PAIR, TT, CTX)
        dk = cut(1920, PAIR, CTX)
        prT = cut(2048, PAIR, SEQ)
        vx = cut(2560, PAIR, P)
        hqT = cut(2816, PAIR, SEQ)
        feat3 = cut(3328, PAIR, SEQ)
        feat4 = cut(3840, PAIR, SEQ)
        junk = cut(7168, 2, SEQ)
        hid = cut(0, 3, W2)
        sg = cut(1536, 2, W2)
        ab = cut(2560, 2, W2)
        ub = cut(3584, 2, W2)
        vb = cut(4608, 2, W2)
        sel3 = cut(5632, NT, 4)
        blend = cut(5664, 2, NT, P)
        cmpj = cut(6688, SEQ)
        oq = cut(0, SEQ)
        kpad = cut(256, PAD + SEQ)
        vpad = cut(704, PAD + SEQ)
        prod = cut(1152, 2, 4, SEQ)
        qks = cut(3200, 2, 2 * SEQ)
        L = cut(4224, NSLOT, SEQ)
        pexp = cut(4224, 2, 8, P)
        ltok = cut(6784, TT, 4 * NSLOT, H)
        part = cut(3200, 5, P)
        oacc = oq

        wide_t = ctx.enter_context(nc.psum_tensor("wide", [P, 2, 1024], F32))
        narrow_t = ctx.enter_context(nc.psum_tensor("narrow", [P, 2, 512], F32))
        accum_t = ctx.enter_context(nc.psum_tensor("accum", [P, 1, 1024], F32))

        group_loaded = [sem(f"group_loaded{g}") for g in range(len(GROUP))]
        const_set = sem("const_set")
        pbias_in = sem("pbias_in")
        pre_step = sem("pre_step")
        pre_mm = sem("pre_mm")
        pre_fold = sem("pre_fold")
        all_ended = sem("all_ended")
        go_on = sem("go_on")
        went_on = sem("went_on")

        first_counted = []

        def signal(name, keys, by=1):
            s = sem(name)
            first_counted.append(s)
            return Signal(s, keys, by)

        def ring(name, tile, n):
            full = [sem(f"{name}_full{i}") for i in range(n)]
            first_counted.extend(full)
            return Ring(tile, full)

        def per_batch(names):
            return [(s, b) for s in names for b in two]

        att = [s for s in stages if s in ATT]
        cross = [s for s in stages if s[0] == "x"]
        ffn = [s for s in stages if s[0] == "f"]
        routed = [s for s in ffn if s != "f3"]
        chunks = {"f0": CH0, "f1": CH1, "f2": CH2, "f3": CH3}

        wide, narrow, accum = ring("wide", wide_t, 2), ring("narrow", narrow_t, 2), ring("accum", accum_t, 1)
        inputs_in = signal("inputs_in", [("all",)], 16 * (2 + 2 * PAIR))
        mask_ready = signal("mask_ready", [("all",)])
        ctxT_ready = signal("ctxT_ready", [("all",)])
        out_stored = signal("out_stored", [("all",)], 16 * PAIR)
        dve_done = signal("dve_done", [])
        out_taken = signal("out_taken", [(s, b) for s in stages for b in two if s[0] != "f"])
        x_final = signal("x_final", [("all",)])
        squares = signal("squares", per_batch(["f0"]))
        xn_mid = signal("xn_mid", per_batch(["f0"]))
        xn_ready = signal("xn_ready", per_batch(stages))
        xnT_ready = signal("xnT_ready", per_batch(stages))
        q_taken = signal("q_taken", per_batch([s for s in att if s == "a3"]))
        qk_ready = signal("qk_ready", per_batch(att))
        part0 = signal("part0", per_batch(att))
        res_ready = signal("res_ready", per_batch(att))
        part1 = signal("part1", per_batch(att))
        parts_ready = signal("parts_ready", per_batch(att))
        v_ready = signal("v_ready", per_batch(att))
        scratch_in = signal("scratch_in", per_batch(att), 32)

        def stack_dmas(s):
            return 12 + {"a1": 4, "a2": 6, "a3": 2}.get(s, 0)

        stack_ready = [signal(f"stack_ready{b}", []) for b in two]
        for b in two:
            total = 0
            for s in att:
                total += 16 * stack_dmas(s)
                stack_ready[b].value[(s,)] = total
        mparts_ready = signal("mparts_ready", per_batch(att))
        negmT_ready = signal("negmT_ready", per_batch(att))
        score_chunks = {s: (8 if ATT[s][0] == SEQ else 4) for s in att}
        max_chunks = {s: (8 if ATT[s][0] == SEQ else 2) for s in att}
        pv_keys = [(s, b, c) for s in att for b in two for c in range(score_chunks[s])]
        max_taken = signal("max_taken", [(s, b, c) for s in att for b in two for c in range(max_chunks[s])])
        probs_ready = signal("probs_ready", pv_keys)
        probs_used = signal("probs_used", pv_keys)
        osp_ready = signal("osp_ready", per_batch(att))
        otok_ready = signal("otok_ready", per_batch(att))
        oT_ready = signal("oT_ready", per_batch([s for s in att if s != "a1"]))
        proj_ready = signal("proj_ready", per_batch(cross))
        vx_ready = signal("vx_ready", per_batch(["x0"]))
        khat_taken = signal("khat_taken", per_batch(["x0"]))
        khat_arg = signal("khat_arg", per_batch(["x0"]))
        khat_ready = signal("khat_ready", per_batch(["x0"]))
        sim_ready = signal("sim_ready", per_batch(["x1"]))
        bsum_taken = signal("bsum_taken", per_batch(["x1"]))
        xmax_ready = signal("xmax_ready", per_batch(cross))
        xexp_ready = signal("xexp_ready", per_batch(cross))
        xprob_ready = signal("xprob_ready", per_batch(cross))
        prT_ready = signal("prT_ready", per_batch(cross))
        hqT_ready = signal("hqT_ready", per_batch(["x1"]))
        bmax_ready = signal("bmax_ready", per_batch(["x1"]))
        bexp_ready = signal("bexp_ready", per_batch(["x1"]))
        feats_ready = signal("feats_ready", per_batch(["x1"]))
        logits_taken = signal("logits_taken", [(f,) for f in ffn])
        counts_ready = signal("counts_ready", [("f3",)])
        logit_arg = signal("logit_arg", [(f,) for f in routed])
        logit_exp = signal("logit_exp", [(f,) for f in routed])
        gates_ready = signal("gates_ready", [(f,) for f in routed])
        gatesT_ready = signal("gatesT_ready", [(f,) for f in routed if f != "f2"])

        def pieces(f, c):
            if f in ("f0", "f1"):
                n = 1 if f == "f0" else 2
                return [(c // n, 0, P, c % n == 0, c % n == n - 1)]
            if f == "f3":
                return [(0, 0, P, c == 0, c == CH3 - 1)]
            found = []
            for e in range(E2):
                a, z = max(e * HID2, c * P), min((e + 1) * HID2, (c + 1) * P)
                if a < z:
                    found.append((e, a - c * P, z - c * P, a == e * HID2, z == (e + 1) * HID2))
            return found

        ends = {(f, e): c for f in routed for c in range(chunks[f]) for e, _, _, _, last in pieces(f, c) if last}
        ch = [(f, c) for f in ffn for c in range(chunks[f])]
        a_ready = signal("a_ready", [(f, c) for f, c in ch if f == "f0"])
        u_ready = signal("u_ready", [(f, c) for f, c in ch if f != "f3"])
        sg_ready = signal("sg_ready", [(f, c) for f, c in ch if f != "f3"])
        t_ready = signal("t_ready", [(f, c) for f, c in ch if f == "f0"])
        hid_ready = signal("hid_ready", ch)
        hid_used = signal("hid_used", ch)
        y_added = signal("y_added", list(ends))
        y_biased = signal("y_biased", [(f,) for f in routed if f != "f2"])
        w_tok = signal("w_tok", [("f3",)])
        oqk_ready = signal("oqk_ready", [(b,) for b in two])
        ov_ready = signal("ov_ready", [(b,) for b in two])
        gth_ready = signal("gth_ready", [(b,) for b in two])
        ltok_ready = signal("ltok_ready", [(b, t, half) for b in two for t in range(TT) for half in range(2)])
        slots = [(b, s) for b in two for s in range(NSLOT)]
        prod_ready = signal("prod_ready", slots)
        prod_used = signal("prod_used", slots)
        qks_ready = signal("qks_ready", [(b, s) for b in two for s in range(NSLOT // 2)])
        L_ready = signal("L_ready", [(b, s) for b in two for s in range(NSLOT // 2)])
        lmax_ready = signal("lmax_ready", [(b,) for b in two])
        lexp_ready = signal("lexp_ready", [(b,) for b in two])
        lprob_ready = signal("lprob_ready", [(b,) for b in two])
        groups = [(b, t, g) for b in two for t in range(TT) for g in range(5)]
        pexp_ready = signal("pexp_ready", groups)
        pv_ready = signal("pv_ready", groups)
        og_ready = signal("og_ready", [(b,) for b in two])
        counted = range(min(s.num for s in first_counted), max(s.num for s in first_counted) + 1)
        assert len(counted) == len(first_counted)

        def g_ring(b, t, g):
            return groups.index((b, t, g)) % 2

        class Steps:

            def __init__(self, eng, sig):
                self.eng, self.s, self.n = eng, sig.s, 0

            def link(self, ins):
                self.mark(ins)
                self.eng.wait_ge(self.s, self.n)

            def mark(self, ins):
                self.n += 1
                ins.then_inc(self.s, 1)
                return self.n

        def end_of_iteration(eng):
            eng.drain().then_inc(all_ended, 1)
            eng.wait_ge(go_on, 1)
            eng.sem_inc(went_on, 1)

        def window(buf, start, step, n, length):
            v = buf[:, start:start + length]
            return bass.AP(v.tensor, v.offset, [list(v.ap[0]), [step, n], [1, length]])

        def offset_runs(i0, n):
            if i0 < 32:
                return [(i0, n, 1)]
            return [(i, 2, OFFSETS[i] - OFFSETS[i + 1]) for i in range(i0, min(i0 + n, NOFF), 2)]

        block = ctx.enter_context(nc.Block())

        @block.tensor
        def _(pe):
            ident = w("ident")

            def take(r, key, drained, *event):
                slot, before = r.take(key, (drained, event))
                if before:
                    pe.wait_ge(before[0].s, before[0].at(*before[1]))
                return slot, r.tile[:, slot, :], r.full[slot]

            pe.wait_ge(group_loaded[0], 32)
            pe.matmul(narrow_t[:, 0, 0:3 * P], w("a0_AT")[0:8, :], w("a0_B")[0:8, :], start=True, stop=True)
            pe.matmul(narrow_t[:, 1, 0:P], w("a0_AoT")[0:8, :], w("a0_Bo")[0:8, :], start=True,
                      stop=True).then_inc(pre_mm, 1)
            pe.wait_ge(pre_fold, 1)

            def norm(s, b):
                _, ps, full = take(narrow, ("norm", s, b), xnT_ready, s, b)
                pe.wait_ge(xn_ready.s, xn_ready.at(s, b))
                for t in range(TT):
                    mm = pe.transpose(ps[:, t * P:(t + 1) * P], xn[:, b, t, :], ident)
                mm.then_inc(full, 1)

            def context():
                _, ps, full = take(narrow, ("ctx",), ctxT_ready, "all")
                pe.wait_ge(inputs_in.s, inputs_in.at("all"))
                for b in two:
                    mm = pe.transpose(ps[:, b * CTX:(b + 1) * CTX], ctok[:, b, :], ident[0:CTX, 0:CTX])
                mm.then_inc(full, 1)

            def att_project(s, b):
                nk = ATT[s][0]
                pe.wait_ge(xnT_ready.s, xnT_ready.at(s, b))
                pe.wait_ge(ctxT_ready.s, ctxT_ready.at("all"))
                src = xnT[:, b, :] if nk == SEQ else ctxT[:, b, :]
                if s == "a3":
                    for n in ("q", "k"):
                        _, ps, full = take(narrow, (n, s, b), q_taken if n == "q" else qk_ready, s, b)
                        pe.matmul(ps[:, 0:SEQ], w(f"a3_W{n}"), xnT[:, b, :], start=True, stop=True)
                        pe.matmul(ps[:, SEQ:2 * SEQ], w(f"a3_W{n}s"), xnT[:, b, :], start=True,
                                  stop=True).then_inc(full, 1)
                else:
                    _, ps, full = take(narrow, ("qk", s, b), qk_ready, s, b)
                    pe.matmul(ps[:, 0:SEQ], w(f"{s}_Wq"), xnT[:, b, :], start=True, stop=True)
                    pe.matmul(ps[:, SEQ:SEQ + nk], w(f"{s}_Wk"), src, start=True, stop=True).then_inc(full, 1)
                _, ps, full = take(narrow, ("v", s, b), v_ready, s, b)
                n = min(nk, P)
                for t in range(nk // n):
                    mm = pe.matmul(ps[0:n, t * P:(t + 1) * P], src[:, t * n:(t + 1) * n], w(f"{s}_Wv"),
                                   start=True, stop=True)
                mm.then_inc(full, 1)

            def att_max(s, b):
                nk, causal, _ = ATT[s]
                pe.wait_ge(stack_ready[b].s, stack_ready[b].at(s))
                per = H // max_chunks[s]
                for c in range(max_chunks[s]):
                    _, ps, full = take(wide, ("max", s, b, c), max_taken, s, b, c)
                    for i in range(per):
                        h = c * per + i
                        q = qs[:, b, h // 2, :]
                        if causal:
                            o = ps[:, 512 * i:512 * i + 384]
                            pe.matmul(o, wb("identb"), wb("mask_qk"), start=True, stop=False)
                            pe.matmul(o[:, 0:P], q[:, 0:P], ks[:, b, h % 2, h // 2, 0:P], start=False, stop=False)
                            mm = pe.matmul(o[:, P:3 * P], q[:, P:2 * P], ks[:, b, h % 2, h // 2, :], start=False, stop=True)
                        else:
                            for t in range(TT):
                                at = (i * TT + t) * nk
                                mm = pe.matmul(ps[:, at:at + nk], q[:, t * P:(t + 1) * P], ks[:, b, h % 2, h // 2, 0:nk],
                                               start=True, stop=True)
                    mm.then_inc(full, 1)

            def att_maxT(s, b):
                _, ps, full = take(narrow, ("maxT", s, b), negmT_ready, s, b)
                pe.wait_ge(mparts_ready.s, mparts_ready.at(s, b))
                psb = ps[:, 0:P].bitcast(BF16)
                for t in range(TT):
                    mm = pe.transpose(psb[:, t * P:(t + 1) * P], mparts[:, b, t, :], wb("identb"))
                mm.then_inc(full, 1)

            def att_scores(s, b, c):
                nk, causal, _ = ATT[s]
                per = H // score_chunks[s]
                _, ps, full = take(wide, ("scores", s, b, c), probs_ready, s, b, c)
                for i in range(per):
                    h = c * per + i
                    q, k, sel = qs[:, b, h // 2, :], ks[:, b, h % 2, h // 2, :], wb("sel")[:, h:h + 1].to_broadcast([P, P])
                    if causal:
                        o = ps[:, 512 * i:512 * i + 384]
                        pe.matmul(o, wb("identb"), wb("mask_kq"), start=True, stop=False)
                        pe.matmul(o[:, 0:SEQ], k[:, 0:P], q, start=False, stop=False)
                        pe.matmul(o[:, SEQ:], k[:, P:], q[:, P:], start=False, stop=False)
                        pe.matmul(o[:, 0:SEQ], sel, negmT[:, b, :], start=False, stop=False)
                        mm = pe.matmul(o[:, SEQ:], sel, negmT[:, b, P:], start=False, stop=True)
                    elif nk == SEQ:
                        for t in range(TT):
                            o = ps[:, (i * TT + t) * SEQ:(i * TT + t + 1) * SEQ]
                            pe.matmul(o, k[:, t * P:(t + 1) * P], q, start=True, stop=False)
                            mm = pe.matmul(o, sel, negmT[:, b, :], start=False, stop=True)
                    else:
                        o = ps[0:CTX, i * SEQ:(i + 1) * SEQ]
                        pe.matmul(o, k[:, 0:CTX], q, start=True, stop=False)
                        mm = pe.matmul(o, sel[:, 0:CTX], negmT[:, b, :], start=False, stop=True)
                mm.then_inc(full, 1)

            def att_values(s, b, c, acc):
                nk, causal, _ = ATT[s]
                per = H // score_chunks[s]
                pe.wait_ge(probs_ready.s, probs_ready.at(s, b, c))
                pr_ = probs[:, pv_keys.index((s, b, c)) % 2, :]
                for i in range(per):
                    h = c * per + i
                    o = acc[32 * (h % 4):32 * (h % 4) + HD + 1, (h // 4) * SEQ:(h // 4 + 1) * SEQ]
                    if causal:
                        p_ = pr_[:, 384 * i:384 * i + 384]
                        pe.matmul(o, vaug[:, b, 0, h, :], p_[:, 0:SEQ], start=True, stop=False)
                        mm = pe.matmul(o[:, P:], vaug[:, b, 1, h, :], p_[:, SEQ:], start=False, stop=True)
                    elif nk == SEQ:
                        for t in range(TT):
                            mm = pe.matmul(o, vaug[:, b, t, h, :], pr_[:, (i * TT + t) * SEQ:(i * TT + t + 1) * SEQ],
                                           start=(t == 0), stop=(t == TT - 1))
                    else:
                        mm = pe.matmul(o, vaug[0:CTX, b, 0, h, :], pr_[0:CTX, i * SEQ:(i + 1) * SEQ],
                                       start=True, stop=True)
                mm.then_inc(probs_used.s, 1)

            def att_core(s, b):
                pe.wait_ge(negmT_ready.s, negmT_ready.at(s, b))
                pe.wait_ge(v_ready.s, v_ready.at(s, b))
                for c in range(score_chunks[s]):
                    att_scores(s, b, c)
                    if c == 1:
                        _, acc, _ = take(accum, ("att", s, b), osp_ready, s, b)
                    if c:
                        att_values(s, b, c - 1, acc)
                att_values(s, b, score_chunks[s] - 1, acc)

            def att_back(s, b):
                _, ps, full = take(wide, ("back", s, b), otok_ready, s, b)
                pe.wait_ge(osp_ready.s, osp_ready.at(s, b))
                for t in range(TT):
                    for g in range(4):
                        at = (t * 4 + g) * P
                        mm = pe.transpose(ps[:, at:at + P], osp[:, b, g, t * P:(t + 1) * P], ident)
                mm.then_inc(full, 1)

            def att_turn(s, b):
                if s == "a1":
                    return
                _, ps, full = take(narrow, ("turn", s, b), oT_ready, s, b)
                pe.wait_ge(otok_ready.s, otok_ready.at(s, b))
                for t in range(TT):
                    mm = pe.transpose(ps[:, t * P:(t + 1) * P], otok[:, b, t, :], ident)
                mm.then_inc(full, 1)

            def project_out(s, b, src, ready, key, weights):
                _, ps, full = take(narrow, ("out", s, b), out_taken, s, b)
                pe.wait_ge(ready.s, ready.at(*key))
                for t in range(TT):
                    for i, (lhs, rhs) in enumerate(zip(src, weights)):
                        mm = pe.matmul(ps[:, t * P:(t + 1) * P], lhs[:, t * P:(t + 1) * P], rhs,
                                       start=(i == 0), stop=(i == len(src) - 1))
                mm.then_inc(full, 1)

            def cross_project(s, b):
                pe.wait_ge(xnT_ready.s, xnT_ready.at(s, b))
                pe.wait_ge(ctxT_ready.s, ctxT_ready.at("all"))
                if s == "x1":
                    return
                _, ps, full = take(narrow, ("qk", s, b), proj_ready, s, b)
                pe.matmul(ps[:, 0:SEQ], w("x0_Wq"), xnT[:, b, :], start=True, stop=True)
                pe.matmul(ps[:, SEQ:SEQ + CTX], w("x0_Wk"), ctxT[:, b, :], start=True, stop=True).then_inc(full, 1)
                _, ps, full = take(narrow, ("v", s, b), vx_ready, s, b)
                pe.matmul(ps[0:CTX, 0:P], ctxT[:, b, :], w("x0_Wv"), start=True, stop=True).then_inc(full, 1)

            def cross_khat(s, b):
                if s == "x1":
                    return
                _, ps, full = take(narrow, ("khat", s, b), khat_taken, s, b)
                pe.wait_ge(proj_ready.s, proj_ready.at(s, b))
                pe.matmul(ps[:, 0:CTX], w("x0_Wr"), qk[:, b, SEQ:SEQ + CTX], start=True, stop=True).then_inc(full, 1)

            def cross_scores(s, b):
                _, ps, full = take(narrow, ("scores", s, b), xexp_ready if s == "x0" else sim_ready, s, b)
                if s == "x0":
                    pe.wait_ge(khat_ready.s, khat_ready.at(s, b))
                    for t in range(TT):
                        mm = pe.matmul(ps[:, t * CTX:(t + 1) * CTX], qk[:, b, t * P:(t + 1) * P], khat[:, b, :],
                                       start=True, stop=True)
                else:
                    pe.wait_ge(proj_ready.s, proj_ready.at(s, b))
                    for t in range(TT):
                        o = ps[:, t * CTX:(t + 1) * CTX]
                        pe.matmul(o, xnT[:, b, t * P:(t + 1) * P], dk[:, b, :], start=True, stop=False)
                        mm = pe.matmul(o, w("x1_w2").to_broadcast([P, P]), ctxT[:, b, :], start=False, stop=True)
                mm.then_inc(full, 1)

            def cross_turn(s, b):
                if s == "x1":
                    _, ps, full = take(narrow, ("bmax", s, b), bmax_ready, s, b)
                    pe.wait_ge(xmax_ready.s, xmax_ready.at(s, b))
                    for t in range(TT):
                        mm = pe.transpose(ps[:, t * P:(t + 1) * P], small[:, b, t:t + 1].to_broadcast([P, P]), ident)
                    mm.then_inc(full, 1)
                _, ps, full = take(narrow, ("turn", s, b), prT_ready, s, b)
                pe.wait_ge(xprob_ready.s, xprob_ready.at(s, b))
                for t in range(TT):
                    mm = pe.transpose(ps[0:CTX, t * P:(t + 1) * P], pr[:, b, t, :], ident)
                mm.then_inc(full, 1)

            def cross_out(s, b):
                if s == "x0":
                    _, ps, full = take(narrow, ("out", s, b), out_taken, s, b)
                    pe.wait_ge(prT_ready.s, prT_ready.at(s, b))
                    for t in range(TT):
                        mm = pe.matmul(ps[:, t * P:(t + 1) * P], prT[0:CTX, b, t * P:(t + 1) * P], vx[0:CTX, b, :],
                                       start=True, stop=True)
                    mm.then_inc(full, 1)
                    return
                _, ps, full = take(narrow, ("hq", s, b), hqT_ready, s, b)
                pe.wait_ge(prT_ready.s, prT_ready.at(s, b))
                pe.matmul(ps[:, 0:SEQ], ctok[:, b, :], prT[0:CTX, b, :], start=True, stop=True).then_inc(full, 1)
                _, ps, full = take(narrow, ("bsum", s, b), bsum_taken, s, b)
                pe.wait_ge(bexp_ready.s, bexp_ready.at(s, b))
                for lhs, at in ((None, 0), (ones, 1)):
                    for t in range(TT):
                        mm = pe.matmul(ps[:, at:at + 1], xn[:, b, t, :] if lhs is None else ones[:, :],
                                       small[:, b, 6 + t:7 + t], start=(t == 0), stop=(t == TT - 1))
                mm.then_inc(full, 1)
                wqv = w("x1_Wqv")
                project_out(s, b, [xnT[:, b, :], hqT[:, b, :], feat3[:, b, :], feat4[:, b, :]], feats_ready,
                            (s, b), [wqv[:, i * P:(i + 1) * P] for i in range(4)])

            def ffn_layer(f):
                tokens = xnT[:, :, :].rearrange("p b t -> p (b t)")
                for b in two:
                    pe.wait_ge(xnT_ready.s, xnT_ready.at(f, b))
                wg = w("f3_wr") if f == "f3" else w(f"{f}_wg")
                e = wg.shape[1]
                _, ps, full = take(narrow, ("logits", f), logits_taken, f)
                for t in range(NT):
                    mm = pe.matmul(ps[:, t * 16:t * 16 + e], tokens[:, t * P:(t + 1) * P], wg, start=True, stop=True)
                mm.then_inc(full, 1)

                def hidden(c):
                    _, ps, full = take(wide, ("hid", f, c), u_ready if f == "f0" else hid_ready, f, c)
                    mm = pe.matmul(ps[:, 0:W2], w(f"{f}_w1")[:, c * P:(c + 1) * P], tokens, start=True, stop=True)
                    if f != "f3":
                        mm = pe.matmul(ps[:, W2:2 * W2], w(f"{f}_w3")[:, c * P:(c + 1) * P], tokens,
                                       start=True, stop=True)
                    mm.then_inc(full, 1)

                def down(c):
                    pe.wait_ge(hid_ready.s, hid_ready.at(f, c))
                    for e, p0, p1, first, last in pieces(f, c):
                        if first and e >= 2:
                            pe.wait_ge(y_added.s, y_added.at(f, e - 2))
                        for t in range(NT):
                            at = (e % 2) * W2 + t * P
                            mm = pe.matmul(accum_t[:, 0, at:at + P], hid[p0:p1, c % 3, t * P:(t + 1) * P],
                                           w(f"{f}_w2")[p0:p1, c * P:(c + 1) * P],
                                           start=first and t == 0, stop=last and t == NT - 1)
                    mm.then_inc(hid_used.s, 1)

                def output_biases():
                    e = E0 if f == "f0" else E1 + S1
                    _, ps, full = take(narrow, ("gatesT", f), gatesT_ready, f)
                    pe.wait_ge(gates_ready.s, gates_ready.at(f))
                    for t in range(NT):
                        mm = pe.transpose(ps[0:16, t * P:(t + 1) * P], gates[:, t, :], ident)
                    mm.then_inc(full, 1)
                    _, ps, full = take(narrow, ("bias", f), y_biased, f)
                    pe.wait_ge(gatesT_ready.s, gatesT_ready.at(f))
                    for t in range(NT):
                        mm = pe.matmul(ps[:, t * P:(t + 1) * P], gatesT[0:e, t * P:(t + 1) * P], w(f"{f}_bt")[0:e, :],
                                       start=True, stop=True)
                    mm.then_inc(full, 1)

                for c in range(chunks[f]):
                    hidden(c)
                    if f == "f3" and c == 1:
                        _, ps, full = take(narrow, ("wrow", f), counts_ready, f)
                        pe.wait_ge(w_tok.s, w_tok.at(f))
                        for t in range(NT):
                            mm = pe.transpose(ps[:, t * P:(t + 1) * P],
                                              lg[:, t, 0:1].to_broadcast([P, P]), ident)
                        mm.then_inc(full, 1)
                    if c >= 2:
                        down(c - 2)
                    if c == BIAS_AT and f in ("f0", "f1"):
                        output_biases()
                down(chunks[f] - 2)
                down(chunks[f] - 1)

            def offset_layer(b):
                pe.wait_ge(xnT_ready.s, xnT_ready.at("o", b))
                for key, names, read in (("oqk", "qk", oqk_ready), ("ov", "v", ov_ready), ("og", "g", gth_ready)):
                    _, ps, full = take(narrow, (key, b), read, b)
                    for i, n in enumerate(names):
                        mm = pe.matmul(ps[:, i * SEQ:(i + 1) * SEQ], w(f"o_W{n}"), xnT[:, b, :], start=True, stop=True)
                    mm.then_inc(full, 1)
                pe.wait_ge(oqk_ready.s, oqk_ready.at(b))
                for s in range(NSLOT):
                    if s % 2 == 0:
                        _, ps, full = take(wide, ("oqk", b, s // 2), L_ready, b, s // 2)
                    pe.wait_ge(prod_ready.s, prod_ready.at(b, s))
                    for j in range(4):
                        src = j if 4 * s + j < NOFF else j - 2
                        mm = pe.matmul(ps[32 * j:32 * j + 32, (s % 2) * SEQ:(s % 2 + 1) * SEQ], w("blk"),
                                       prod[:, s % 2, src, :], start=True, stop=True)
                    mm.then_inc(prod_used.s, 1)
                    mm = pe.matmul(ps[:, W2 + (s % 2) * SEQ:W2 + (s % 2 + 1) * SEQ], emb[:, s, :], oq,
                                   start=True, stop=True)
                    if s % 2:
                        mm.then_inc(full, 1)
                for t in range(TT):
                    for half in range(2):
                        _, ps, full = take(wide, ("oturn", b, t, half), ltok_ready, b, t, half)
                        if t == 0:
                            pe.wait_ge(L_ready.s, L_ready.at(b, 2 if half == 0 else 4))
                        for i in range(5):
                            mm = pe.transpose(ps[:, i * P:(i + 1) * P], L[:, 5 * half + i, t * P:(t + 1) * P], ident)
                        mm.then_inc(full, 1)
                for t in range(TT):
                    for g in range(5):
                        _, ps, full = take(wide, ("oprob", b, t, g), pv_ready, b, t, g)
                        pe.wait_ge(pexp_ready.s, pexp_ready.at(b, t, g))
                        for i in range(8 if g < 4 else 6):
                            mm = pe.transpose(ps[:, i * P:(i + 1) * P], pexp[:, g_ring(b, t, g), i, :], ident)
                        mm.then_inc(full, 1)
                project_out("o", b, [oacc], og_ready, (b,), [w("o_Wo")])

            with pe.Fori(0, iters):
                context()
                for s in stages:
                    pe.wait_ge(group_loaded[GROUP_OF[s]], 16 + 16 * (GROUP_OF[s] == 0))
                    for b in two:
                        norm(s, b)
                    if s in ATT:
                        for b in two:
                            att_project(s, b)
                        for b in two:
                            att_max(s, b)
                        for b in two:
                            att_maxT(s, b)
                        for b in two:
                            att_core(s, b)
                        for b in two:
                            att_back(s, b)
                        for b in two:
                            att_turn(s, b)
                        if s != "a1":
                            for b in two:
                                project_out(s, b, [oT[:, b, :]], oT_ready, (s, b), [w(f"{s}_Wo")])
                    elif s[0] == "x":
                        for step in (cross_project, cross_khat, cross_scores, cross_turn, cross_out):
                            for b in two:
                                step(s, b)
                    elif s == "o":
                        for b in two:
                            offset_layer(b)
                    else:
                        ffn_layer(s)
                end_of_iteration(pe)


        @block.scalar
        def _(act):
            def see(r, *key):
                slot, n = r.at(*key)
                act.wait_ge(r.full[slot], n)
                return r.tile[:, slot, :]

            def copy(dst, src, done, **kw):
                act.activation(dst, src, ACT.Copy, **kw).then_inc(done.s, 1)

            def norm(s, b):
                if s == "f0" and b == 0:
                    for c in two:
                        act.wait_ge(xn_mid.s, xn_mid.at(s, c))
                        for t in range(TT):
                            ins = act.activation(junk[:, c, t * P:(t + 1) * P], xn[:, c, t, :], ACT.Square,
                                                 accum_out=sumsq[:, c * TT + t:c * TT + t + 1])
                        ins.then_inc(squares.s, 1)
                ps = see(narrow, "norm", s, b)
                if s == "f0":
                    act.activation(xnT[:, b, :], ps[:, 0:SEQ], ACT.Copy, scale=w("f0_ns")).then_inc(xnT_ready.s, 1)
                else:
                    copy(xnT[:, b, :], ps[:, 0:SEQ], xnT_ready)

            def att_split(s, b):
                n = SEQ + ATT[s][0]
                act.wait_ge(qk_ready.s, qk_ready.at(s, b))
                copy(parts[:, b, 0, 0:n], qk[:, b, 0:n], part0)
                act.wait_ge(res_ready.s, res_ready.at(s, b))
                copy(parts[:, b, 1, 0:n], res[:, b, 0:n], part1)

            def att_maxT(s, b):
                copy(negmT[:, b, :], see(narrow, "maxT", s, b)[:, 0:P].bitcast(BF16), negmT_ready)

            def att_core(s, b):
                nk, causal, _ = ATT[s]
                for c in range(score_chunks[s]):
                    ps = see(wide, "scores", s, b, c)
                    i = pv_keys.index((s, b, c))
                    if i >= 2:
                        act.wait_ge(probs_used.s, i - 1)
                    if causal:
                        act.activation(probs[:, i % 2, 0:768].rearrange("p (h t) -> p h t", h=2),
                                       ps.rearrange("p (h t) -> p h t", h=2)[:, :, 0:384],
                                       ACT.Exp).then_inc(probs_ready.s, 1)
                    else:
                        n = min(nk, P)
                        act.activation(probs[0:n, i % 2, :], ps[0:n, :], ACT.Exp).then_inc(probs_ready.s, 1)
                act.wait_ge(probs_used.s, probs_used.at(s, b, score_chunks[s] - 1))
                copy(osp[:, b, :, :].rearrange("p g t -> p (g t)"), accum_t[:, 0, :], osp_ready)

            def att_turn(s, b):
                if s != "a1":
                    copy(oT[:, b, :], see(narrow, "turn", s, b)[:, 0:SEQ], oT_ready)

            def cross_khat(s, b):
                if s == "x0":
                    act.wait_ge(khat_arg.s, khat_arg.at(s, b))
                    act.activation(khat[:, b, :], zc[:, b, :], ACT.Sin, bias=halfpi[:, :]).then_inc(khat_ready.s, 1)

            def cross_exp(s, b):
                act.wait_ge(xmax_ready.s, xmax_ready.at(s, b))
                src = see(narrow, "scores", s, b) if s == "x0" else sim[:, b, :, :].rearrange("p t k -> p (t k)")
                for t in range(TT):
                    ins = act.activation(pr[:, b, t, :], src[:, t * CTX:(t + 1) * CTX], ACT.Exp,
                                         bias=small[:, b, 2 + t:3 + t], accum_out=small[:, b, 4 + t:5 + t])
                ins.then_inc(xexp_ready.s, 1)

            def cross_turn(s, b):
                if s == "x1":
                    act.wait_ge(bmax_ready.s, bmax_ready.at(s, b))
                    act.activation(small[:, b, 6:8], small[:, b, 0:2], ACT.Exp,
                                   bias=small[:, b, 8:9]).then_inc(bexp_ready.s, 1)
                copy(prT[0:CTX, b, :], see(narrow, "turn", s, b)[0:CTX, 0:SEQ], prT_ready)

            def cross_hq(s, b):
                if s == "x1":
                    copy(hqT[:, b, :], see(narrow, "hq", s, b)[:, 0:SEQ], hqT_ready)

            def ffn_layer(f):
                if f in ("f1", "f2"):
                    act.wait_ge(logit_arg.s, logit_arg.at(f))
                    e = E1 if f == "f1" else E2
                    act.activation(ex[:, :, 0:e], lg[:, :, 0:e], ACT.Exp).then_inc(logit_exp.s, 1)
                elif f == "f0":
                    act.wait_ge(logit_arg.s, logit_arg.at(f))
                    act.activation(ex[:, :, :], em[:, :, :], ACT.Exp).then_inc(logit_exp.s, 1)

                for c in range(chunks[f]):
                    if f == "f3":
                        ps = see(wide, "hid", f, c)
                        if c >= 3:
                            act.wait_ge(hid_used.s, hid_used.at(f, c - 3))
                        act.activation(hid[:, c % 3, :], ps[:, 0:W2], ACT.Gelu,
                                       bias=w("f3_b1")[:, c:c + 1]).then_inc(hid_ready.s, 1)
                        continue
                    if f == "f0":
                        act.wait_ge(a_ready.s, a_ready.at(f, c))
                        if c >= 2:
                            act.wait_ge(t_ready.s, t_ready.at(f, c - 2))
                        act.activation(sg[:, c % 2, :], ab[:, c % 2, :], ACT.Sigmoid, scale=1.702).then_inc(sg_ready.s, 1)
                    else:
                        ps = see(wide, "hid", f, c)
                        if c >= 2:
                            act.wait_ge(u_ready.s, u_ready.at(f, c - 2))
                        bias = w("f1_b1")[:, c:c + 1] if f == "f1" else 0.0
                        act.activation(sg[:, c % 2, :], ps[:, 0:W2], ACT.Sigmoid, bias=bias).then_inc(sg_ready.s, 1)
                    if c == BIAS_AT and f in ("f0", "f1"):
                        copy(gatesT[:, :], see(narrow, "gatesT", f)[0:16, :], gatesT_ready)

            def offset_layer(b):
                ps = see(narrow, "og", b)
                act.activation(xn[:, b, :, :].rearrange("p t d -> p (t d)"), ps[:, 0:SEQ], ACT.Tanh, scale=0.5, bias=w("o_bg")).then_inc(gth_ready.s, 1)
                for i in range(NSLOT // 2):
                    ps = see(wide, "oqk", b, i)
                    if b or i >= 2:
                        k = b * (NSLOT // 2) + i - 2
                        act.wait_ge(L_ready.s, k + 1)
                    copy(qks[:, i % 2, :], ps[:, 0:W2], qks_ready)
                act.wait_ge(lmax_ready.s, lmax_ready.at(b))
                act.activation(ltok[:, :, :, :], ltok[:, :, :, :], ACT.Exp).then_inc(lexp_ready.s, 1)
                act.wait_ge(lprob_ready.s, lprob_ready.at(b))
                for t in range(TT):
                    for g in range(5):
                        n = 8 if g < 4 else 6
                        i = groups.index((b, t, g))
                        if i % 10 >= 2:
                            prev = groups[i - 2]
                            slot, k = wide.at("oprob", *prev)
                            act.wait_ge(wide.full[slot], k)
                        src = ltok[:, t, 8 * g:8 * g + n, :].unsqueeze(3).to_broadcast([P, n, H, HD])
                        dst = pexp[:, g_ring(b, t, g), 0:n, :].rearrange("p n (h d) -> p n h d", h=H)
                        copy(dst, src, pexp_ready)

            with act.Fori(0, iters):
                copy(ctxT[:, :, :].rearrange("p b k -> p (b k)"), see(narrow, "ctx")[:, 0:PAIR * CTX], ctxT_ready)
                for s in stages:
                    act.wait_ge(group_loaded[GROUP_OF[s]], 16 + 16 * (GROUP_OF[s] == 0))
                    for b in two:
                        norm(s, b)
                    if s in ATT:
                        for b in two:
                            att_split(s, b)
                        for b in two:
                            att_maxT(s, b)
                        for b in two:
                            att_core(s, b)
                        for b in two:
                            att_turn(s, b)
                    elif s[0] == "x":
                        for step in (cross_khat, cross_exp, cross_turn, cross_hq):
                            for b in two:
                                step(s, b)
                    elif s == "o":
                        for b in two:
                            offset_layer(b)
                    else:
                        ffn_layer(s)
                end_of_iteration(act)

        @block.vector
        def _(dve):
            steps = Steps(dve, dve_done)
            link = steps.link

            def see(r, *key):
                slot, n = r.at(*key)
                dve.wait_ge(r.full[slot], n)
                return r.tile[:, slot, :]

            def after(sig, *key):
                dve.wait_ge(sig.s, sig.at(*key))

            def pre(ins, n=[0]):
                n[0] += 1
                ins.then_inc(pre_step, 1)
                dve.wait_ge(pre_step, n[0])

            for tile, value in ((halfpi, float(np.pi / 2)), (ones, 1.0), (vaug, 1.0), (gates, 0.0),
                                (mparts, 0.0), (qs, 0.0), (ks, 0.0), (ex, 0.0)):
                dve.memset(tile[:], value).then_inc(const_set, 1)
            dve.wait_ge(group_loaded[0], 32)
            dve.wait_ge(pre_mm, 1)
            a = COLS["a0_Wq"][0]
            pre(dve.scalar_tensor_tensor(out=wt[:, a:a + 3 * P], in0=narrow_t[:, 0, 0:3 * P], scalar=2.0,
                                         in1=wt[:, a:a + 3 * P], op0=ALU.mult, op1=ALU.add))
            pre(dve.scalar_tensor_tensor(out=w("a0_Wo"), in0=narrow_t[:, 1, 0:P], scalar=2.0, in1=w("a0_Wo"),
                                         op0=ALU.mult, op1=ALU.add))
            dve.memset(accum_t[:], 0.0).then_inc(const_set, 1)
            dve.wait_ge(const_set, 9)
            dve.memset(wide_t[:], 0.0).then_inc(pre_fold, 1)

            def group_setup(g):
                dve.wait_ge(group_loaded[g], 16)
                if g == 1:
                    pre(dve.tensor_scalar(w("f0_b3"), w("f0_b3"), 1.0, None, ALU.add))
                if g == 4:
                    for n in ("a3_Wq", "a3_Wqs", "a3_bq", "a3_bqs"):
                        pre(dve.tensor_scalar(w(n), w(n), HD ** -0.5, None, ALU.mult))
                if g == 3:
                    for j in range(4):
                        src = w("o_emb").rearrange("p (s j) -> p s j", j=4)[:, :, j:j + 1].to_broadcast([P, NSLOT, 32])
                        hm = w("headmask").unsqueeze(1).to_broadcast([P, NSLOT, 32])
                        pre(dve.tensor_tensor(emb[:, :, 32 * j:32 * j + 32], src, hm, ALU.mult))
                    pre(dve.tensor_scalar(w("o_gain"), w("o_gain"), 0.5, None, ALU.mult))
                    pre(dve.tensor_scalar(w("o_bg"), w("o_bg"), 0.5, None, ALU.mult))

            def inverse_root(y, v):
                link(dve.tensor_scalar(y.bitcast(I32), v.bitcast(I32), -0.5, ROOT_GUESS, ALU.mult, ALU.add))
                for _ in range(3):
                    link(dve.scalar_tensor_tensor(out=nt[:, :], in0=y, scalar=-0.5, in1=y, op0=ALU.mult, op1=ALU.mult))
                    link(dve.tensor_tensor(nt[:, :], nt[:, :], v, ALU.mult))
                    link(dve.scalar_tensor_tensor(out=y, in0=nt[:, :], scalar=1.5, in1=y, op0=ALU.add, op1=ALU.mult))

            def norm(s):
                if s == stages[0]:
                    after(inputs_in, "all")
                for b in two:
                    for t in range(TT):
                        ins = dve.bn_stats(bn[:, b, t, :], x[:, b, t, :])
                link(ins)
                for b in two:
                    for t in range(TT):
                        ins = dve.bn_aggr(mv[:, b * TT + t, :], bn[:, b, t, :])
                link(ins)
                link(dve.tensor_scalar(var[:, :], mv[:, :, 1], LN_EPS, None, ALU.add))
                inverse_root(rstd[:, :], var[:, :])
                done = xn_mid if s == "f0" else xn_ready
                for b in two:
                    for t in range(TT):
                        i = b * TT + t
                        ins = dve.tensor_scalar(xn[:, b, t, :], x[:, b, t, :], mv[:, i, 0:1], rstd[:, i:i + 1],
                                                ALU.subtract, ALU.mult)
                    ins.then_inc(done.s, 1)
                if s == "f0":
                    for b in two:
                        after(xn_mid, s, b)
                        ins = dve.tensor_tensor(x[:, b, :, :], x[:, b, :, :], xn[:, b, :, :], ALU.add)
                    link(ins)
                    after(squares, s, 1)
                    link(dve.tensor_scalar(var[:, :], sumsq[:, :], 1.0 / P, LN_EPS, ALU.mult, ALU.add))
                    inverse_root(rstd[:, :], var[:, :])
                    for b in two:
                        for t in range(TT):
                            i = b * TT + t
                            ins = dve.tensor_scalar(xn[:, b, t, :], xn[:, b, t, :], rstd[:, i:i + 1], None, ALU.mult)
                        ins.then_inc(xn_ready.s, 1)

            def add_to_x(s, b, src, bias=None):
                dve.tensor_tensor(x[:, b, :, :], x[:, b, :, :], src, ALU.add).then_inc(out_taken.s, 1)
                after(out_taken, s, b)
                if bias is not None:
                    link(dve.tensor_tensor(x[:, b, :, :], x[:, b, :, :],
                                           w(bias).unsqueeze(1).to_broadcast([P, TT, P]), ALU.add))

            def att_scale(s, b):
                nk, _, scale = ATT[s]
                if s == "a3":
                    tables = w("rope").rearrange("p (n t) -> p n t", n=2)
                    for i, n in enumerate("qk"):
                        ps = see(narrow, n, s, b)
                        o = qk[:, b, i * SEQ:(i + 1) * SEQ]
                        dve.scalar_tensor_tensor(out=o, in0=ps[:, 0:SEQ], scalar=w(f"a3_b{n}"), in1=tables[:, 0, :],
                                                 op0=ALU.add, op1=ALU.mult)
                        ins = dve.scalar_tensor_tensor(out=rt[:, i, :], in0=ps[:, SEQ:], scalar=w(f"a3_b{n}s"),
                                                       in1=tables[:, 1, :], op0=ALU.add, op1=ALU.mult)
                        link(ins)
                        ins = dve.tensor_tensor(o, o, rt[:, i, :], ALU.add)
                        if n == "q":
                            ins.then_inc(q_taken.s, 1)
                        else:
                            ins.then_inc(qk_ready.s, 1)
                else:
                    ps = see(narrow, "qk", s, b)
                    q, k = qk[:, b, 0:SEQ], qk[:, b, SEQ:SEQ + nk]
                    if s in ("a0", "a2"):
                        dve.tensor_scalar(q, ps[:, 0:SEQ], w(f"{s}_bq"), scale, ALU.add, ALU.mult)
                    else:
                        dve.tensor_scalar(q, ps[:, 0:SEQ], scale, None, ALU.mult)
                    if s == "a2":
                        after(mask_ready, "all")
                        dve.scalar_tensor_tensor(out=k, in0=ps[:, SEQ:SEQ + nk], scalar=w("a2_bk"),
                                                 in1=maskf[:, b, :], op0=ALU.add,
                                                 op1=ALU.mult).then_inc(qk_ready.s, 1)
                    elif s == "a0":
                        dve.tensor_scalar(k, ps[:, SEQ:SEQ + nk], w("a0_bk"), None, ALU.add).then_inc(qk_ready.s, 1)
                    else:
                        dve.tensor_copy(k, ps[:, SEQ:SEQ + nk]).then_inc(qk_ready.s, 1)
                ps = see(narrow, "v", s, b)
                n, tiles = min(nk, P), max(nk // P, 1)
                o = vaug[0:n, b, 0:tiles, :, 0:HD]
                src = ps[0:n, 0:tiles * P].rearrange("p (t h d) -> p t h d", t=tiles, h=H)
                if s in ("a0", "a2", "a3"):
                    bias = w(f"{s}_bv")[0:n, :].rearrange("p (h d) -> p h d", h=H)
                    for t in range(tiles):
                        ins = dve.tensor_tensor(o[:, t], src[:, t], bias, ALU.add)
                else:
                    for t in range(tiles):
                        ins = dve.tensor_copy(o[:, t], src[:, t])
                ins.then_inc(v_ready.s, 1)

            def att_split(s, b):
                n = SEQ + ATT[s][0]
                after(qk_ready, s, b)
                after(part0, s, b)
                dve.tensor_tensor(res[:, b, 0:n], qk[:, b, 0:n], parts[:, b, 0, 0:n],
                                  ALU.subtract).then_inc(res_ready.s, 1)

            def att_split2(s, b):
                n = SEQ + ATT[s][0]
                after(res_ready, s, b)
                after(part1, s, b)
                dve.tensor_tensor(parts[:, b, 2, 0:n], res[:, b, 0:n], parts[:, b, 1, 0:n],
                                  ALU.subtract).then_inc(parts_ready.s, 1)

            def att_max(s, b):
                nk, causal, _ = ATT[s]
                per = H // max_chunks[s]
                for c in range(max_chunks[s]):
                    ps = see(wide, "max", s, b, c)
                    heads = slice(c * per, (c + 1) * per)
                    if causal:
                        v = ps.rearrange("p (h t) -> p h t", h=2)
                        dve.tensor_reduce(negm[:, b, 0, heads], v[:, :, 0:P], AX.X, ALU.max, negate=True)
                        ins = dve.tensor_reduce(negm[:, b, 1, heads], v[:, :, P:3 * P], AX.X, ALU.max, negate=True)
                    else:
                        v = ps.rearrange("p (h t k) -> p t h k", t=TT, k=nk)
                        ins = dve.tensor_reduce(negm[:, b, :, heads], v, AX.X, ALU.max, negate=True)
                    ins.then_inc(max_taken.s, 1)
                after(max_taken, s, b, max_chunks[s] - 1)
                link(dve.tensor_copy(mparts[:, b, :, 0:H], negm[:, b, :, :]))
                link(dve.tensor_tensor(mres[:, b, :, :], negm[:, b, :, :], mparts[:, b, :, 0:H], ALU.subtract))
                link(dve.tensor_copy(mparts[:, b, :, 32:32 + H], mres[:, b, :, :]))
                dve.tensor_tensor(mparts[:, b, :, 64:64 + H], mres[:, b, :, :], mparts[:, b, :, 32:32 + H],
                                  ALU.subtract).then_inc(mparts_ready.s, 1)

            def att_back(s, b):
                ps = see(wide, "back", s, b)
                v = ps.rearrange("p (t h r) -> p t h r", t=TT, r=32)
                link(dve.reciprocal(rinv[:, b, :, :], v[:, :, :, HD]))
                o = otok[:, b, :, :].rearrange("p t (h d) -> p t h d", h=H)
                dve.tensor_tensor(o, v[:, :, :, 0:HD], rinv[:, b, :, :].unsqueeze(3).to_broadcast([P, TT, H, HD]),
                                  ALU.mult).then_inc(otok_ready.s, 1)
                if s == "a1":
                    after(otok_ready, s, b)
                    add_to_x(s, b, otok[:, b, :, :])

            def tokens_out(s, b, bias):
                add_to_x(s, b, see(narrow, "out", s, b)[:, 0:SEQ].rearrange("p (t d) -> p t d", t=TT), bias)

            def cross_project(s, b):
                if s == "x1":
                    if b == 0:
                        after(ctxT_ready, "all")
                    dve.tensor_scalar(dk[:, b, :], ctxT[:, b, :], w("x1_w3"), w("x1_w1"), ALU.mult,
                                      ALU.add).then_inc(proj_ready.s, 1)
                    return
                ps = see(narrow, "qk", s, b)
                dve.tensor_scalar(qk[:, b, 0:SEQ], ps[:, 0:SEQ], w("x0_bq"), None, ALU.add)
                dve.tensor_scalar(qk[:, b, SEQ:SEQ + CTX], ps[:, SEQ:SEQ + CTX], w("x0_bk"), None,
                                  ALU.add).then_inc(proj_ready.s, 1)
                ps = see(narrow, "v", s, b)
                dve.tensor_tensor(vx[0:CTX, b, :], ps[0:CTX, 0:P], w("x0_bv")[0:CTX, :], ALU.add).then_inc(vx_ready.s, 1)

            def cross_khat(s, b):
                if s == "x1":
                    return
                ps = see(narrow, "khat", s, b)
                dve.tensor_scalar(zc[:, b, :], ps[:, 0:CTX], w("x0_br"), None, ALU.add).then_inc(khat_taken.s, 1)
                after(khat_taken, s, b)
                link(dve.tensor_scalar(zn[:, b, :], zc[:, b, :], float(1 / (2 * np.pi)), MAGIC, ALU.mult, ALU.add))
                link(dve.tensor_scalar(zn[:, b, :], zn[:, b, :], MAGIC, None, ALU.subtract))
                for part_ in TWO_PI:
                    link(dve.scalar_tensor_tensor(out=zc[:, b, :], in0=zn[:, b, :], scalar=-part_, in1=zc[:, b, :],
                                                  op0=ALU.mult, op1=ALU.add))
                dve.scalar_tensor_tensor(out=zc[:, b, :], in0=zc[:, b, :], scalar=-1.0, in1=zc[:, b, :], op0=ALU.mult,
                                         op1=ALU.min).then_inc(khat_arg.s, 1)

            def cross_max(s, b):
                if s == "x0":
                    ps = see(narrow, "scores", s, b)[:, 0:TT * CTX].rearrange("p (t k) -> p t k", t=TT)
                    dve.tensor_reduce(small[:, b, 2:4], ps, AX.X, ALU.max, negate=True).then_inc(xmax_ready.s, 1)
                    return
                ps = see(narrow, "scores", s, b)
                dve.tensor_scalar(sim[:, b, :, :].rearrange("p t k -> p (t k)"), ps[:, 0:TT * CTX], w("x1_bs"), None,
                                  ALU.add).then_inc(sim_ready.s, 1)
                after(sim_ready, s, b)
                link(dve.tensor_reduce(small[:, b, 0:2], sim[:, b, :, :], AX.X, ALU.max))
                dve.tensor_scalar(small[:, b, 2:4], small[:, b, 0:2], -1.0, None, ALU.mult).then_inc(xmax_ready.s, 1)

            def cross_normalise(s, b):
                if s == "x1":
                    ps = see(narrow, "bmax", s, b)
                    dve.tensor_reduce(small[:, b, 8:9], ps[:, 0:SEQ], AX.X, ALU.max, negate=True).then_inc(bmax_ready.s, 1)
                after(xexp_ready, s, b)
                link(dve.reciprocal(small[:, b, 10:12], small[:, b, 4:6]))
                dve.tensor_tensor(pr[:, b, :, :], pr[:, b, :, :],
                                  small[:, b, 10:12].unsqueeze(2).to_broadcast([P, TT, CTX]),
                                  ALU.mult).then_inc(xprob_ready.s, 1)

            def cross_out(s, b):
                if s == "x0":
                    tokens_out(s, b, None)
                    return
                after(hqT_ready, s, b)
                dve.tensor_tensor(feat3[:, b, :], xnT[:, b, :], hqT[:, b, :], ALU.mult)
                ps = see(narrow, "bsum", s, b)
                link(dve.reciprocal(small[:, b, 12:13], ps[:, 1:2]))
                dve.tensor_tensor(small[:, b, 13:14], ps[:, 0:1], small[:, b, 12:13], ALU.mult).then_inc(bsum_taken.s, 1)
                after(bsum_taken, s, b)
                dve.tensor_scalar(feat4[:, b, :], xnT[:, b, :], small[:, b, 13:14], None,
                                  ALU.mult).then_inc(feats_ready.s, 1)
                tokens_out(s, b, "x1_b")

            def route_logits(f):
                e = EXPERTS[f][0]
                ps = see(narrow, "logits", f)[:, 0:16 * NT].rearrange("p (t e) -> p t e", t=NT)[:, :, 0:e]
                if f == "f2":
                    dve.tensor_copy(lg[:, :, 0:e], ps).then_inc(logits_taken.s, 1)
                else:
                    dve.tensor_tensor(lg[:, :, 0:e], ps, w(f"{f}_bg").unsqueeze(1).to_broadcast([P, NT, e]),
                                      ALU.add).then_inc(logits_taken.s, 1)
                after(logits_taken, f)
                if f == "f0":
                    for t in range(NT):
                        ins = dve.max(top[:, t, :], lg[:, t, :])
                    link(ins)
                    dve.tensor_tensor(em[:, :, :], lg[:, :, :], top[:, :, 0:1].to_broadcast([P, NT, 16]),
                                      ALU.subtract).then_inc(logit_arg.s, 1)
                else:
                    link(dve.tensor_reduce(rsum[:, :, 0:1], lg[:, :, 0:e], AX.X, ALU.max))
                    dve.tensor_tensor(lg[:, :, 0:e], lg[:, :, 0:e], rsum[:, :, 0:1].to_broadcast([P, NT, e]),
                                      ALU.subtract).then_inc(logit_arg.s, 1)
                    if f == "f2":
                        link(dve.memset(ex[:, :, e:8], 0.0))

            def route_choice(f):
                seen = 16 if f == "f0" else 8
                chosen_from = lg if f == "f0" else ex
                if f != "f0":
                    after(logit_exp, f)
                    for t in range(NT):
                        ins = dve.max(top[:, t, :], ex[:, t, 0:8])
                    link(ins)
                for t in range(NT):
                    ins = dve.max_index(topi[:, t, :], top[:, t, :], chosen_from[:, t, 0:seen])
                link(ins)
                link(dve.tensor_copy(topf[:, :, :], topi[:, :, :]))

            def route_weights(f):
                k, seen = EXPERTS[f][1], 16 if f == "f0" else 8
                o = hot[:, :, 0:k, 0:seen]
                link(dve.tensor_tensor(o, topf[:, :, 0:k].unsqueeze(3).to_broadcast([P, NT, k, seen]),
                                       w("sixteen")[:, 0:seen].unsqueeze(1).unsqueeze(1).to_broadcast([P, NT, k, seen]),
                                       ALU.is_equal))
                after(logit_exp, f)
                link(dve.tensor_reduce(em[:, :, 0:seen], o.rearrange("p t k e -> p t e k"), AX.X, ALU.add))
                link(dve.tensor_tensor(em[:, :, 0:seen], em[:, :, 0:seen], ex[:, :, 0:seen], ALU.mult))

            def route_gates(f):
                seen = 16 if f == "f0" else 8
                over = ex if f == "f1" else em
                link(dve.tensor_reduce(rsum[:, :, 0:1], over[:, :, 0:seen], AX.X, ALU.add))
                link(dve.reciprocal(rsum[:, :, 1:2], rsum[:, :, 0:1]))
                ins = dve.tensor_tensor(gates[:, :, 0:seen], em[:, :, 0:seen],
                                        rsum[:, :, 1:2].to_broadcast([P, NT, seen]), ALU.mult)
                if f == "f1":
                    link(ins)
                    ins = dve.memset(gates[:, :, E1:E1 + S1], 1.0 / S1)
                ins.then_inc(gates_ready.s, 1)
                after(gates_ready, f)

            def ffn_layer(f):
                def first_half(c):
                    ps = see(wide, "hid", f, c)
                    if c >= 2:
                        after(t_ready, f, c - 2)
                    dve.tensor_scalar(ab[:, c % 2, :], ps[:, 0:W2], w("f0_b1")[:, c:c + 1], 7.0, ALU.add,
                                      ALU.min).then_inc(a_ready.s, 1)
                    if c >= 2:
                        after(hid_ready, f, c - 2)
                    dve.tensor_scalar(ub[:, c % 2, :], ps[:, W2:], w("f0_b3")[:, c:c + 1], 8.0, ALU.add,
                                      ALU.min).then_inc(u_ready.s, 1)

                def clipped(c):
                    after(t_ready, f, c)
                    after(u_ready, f, c)
                    if c >= 3:
                        after(hid_used, f, c - 3)
                    dve.scalar_tensor_tensor(out=hid[:, c % 3, :], in0=ub[:, c % 2, :], scalar=-6.0,
                                             in1=vb[:, c % 2, :], op0=ALU.max, op1=ALU.mult).then_inc(hid_ready.s, 1)

                def add_output(e):
                    after(hid_used, f, ends[f, e])
                    if e:
                        after(y_added, f, e - 1)
                    for t in range(NT):
                        xt = x[:, t // TT, t % TT, :]
                        at = (e % 2) * W2 + t * P
                        ins = dve.scalar_tensor_tensor(out=xt, in0=accum_t[:, 0, at:at + P], scalar=gates[:, t, e:e + 1],
                                                       in1=xt, op0=ALU.mult, op1=ALU.add)
                    ins.then_inc(y_added.s, 1)

                if f != "f3":
                    route_logits(f)
                    parts_of_route = {0: route_choice, 1: route_weights, 2: route_gates}
                    added = 0
                    for c in range(chunks[f] + 3):
                        if c < chunks[f] and f == "f0":
                            first_half(c)
                        elif c < chunks[f]:
                            ps = see(wide, "hid", f, c)
                            after(sg_ready, f, c)
                            if c >= 2:
                                after(hid_ready, f, c - 2)
                            bias = w("f1_b1")[:, c:c + 1] if f == "f1" else 0.0
                            dve.scalar_tensor_tensor(out=vb[:, c % 2, :], in0=ps[:, 0:W2], scalar=bias,
                                                     in1=sg[:, c % 2, :], op0=ALU.add, op1=ALU.mult).then_inc(u_ready.s, 1)
                        if c in parts_of_route:
                            parts_of_route[c](f)
                        while (f, added) in ends and ends[f, added] <= c - 3:
                            if c > 2:
                                add_output(added)
                            added += 1
                        if f == "f0" and 1 <= c <= chunks[f]:
                            clipped(c - 1)
                        elif f != "f0" and c < chunks[f]:
                            after(u_ready, f, c)
                            if c >= 3:
                                after(hid_used, f, c - 3)
                            bias = w("f1_b3")[:, c:c + 1] if f == "f1" else 0.0
                            dve.scalar_tensor_tensor(out=hid[:, c % 3, :], in0=ps[:, W2:], scalar=bias,
                                                     in1=vb[:, c % 2, :], op0=ALU.add,
                                                     op1=ALU.mult).then_inc(hid_ready.s, 1)
                        if c == BIAS_AT + 1 and f in ("f0", "f1"):
                            ps = see(narrow, "bias", f)
                            after(y_added, f, added - 1)
                            xv = x[:, :, :, :].rearrange("p b t d -> p (b t d)")
                            dve.tensor_tensor(xv, xv, ps, ALU.add).then_inc(y_biased.s, 1)
                            after(y_biased, f)
                    after(y_added, f, max(e for g, e in ends if g == f))
                    return
                ps = see(narrow, "logits", f)[:, 0:16 * NT].rearrange("p (t e) -> p t e", t=NT)
                dve.tensor_tensor(lg[:, :, 0:1], ps[:, :, 0:1], w("f3_br").unsqueeze(1).to_broadcast([P, NT, 1]),
                                  ALU.add).then_inc(logits_taken.s, 1)
                after(logits_taken, f)
                dve.tensor_copy(topf[:, :, 0:1], lg[:, :, 0:1]).then_inc(w_tok.s, 1)
                rows = see(narrow, "wrow", f)
                for t in range(NT):
                    b = t // TT
                    ins = dve.tensor_scalar(cmpj, rows[:, b * SEQ:(b + 1) * SEQ], lg[:, t, 0:1], 0.0, ALU.is_ge, ALU.add,
                                            accum_out=sel3[:, t, 0:1])
                    if t < NT - 1:
                        link(ins)
                ins.then_inc(counts_ready.s, 1)
                after(counts_ready, f)
                dve.tensor_scalar(sel3[:, :, 1:2], sel3[:, :, 0:1], SEQ / 2 - 0.5, None, ALU.is_lt)
                link(dve.tensor_scalar(sel3[:, :, 2:3], sel3[:, :, 0:1], SEQ / 2 - 0.5, None, ALU.is_gt))
                xv = x[:, :, :, :].rearrange("p b t d -> p (b t) d")
                xnv = xn[:, :, :, :].rearrange("p b t d -> p (b t) d")
                link(dve.tensor_tensor(blend[:, 1, :, :], xnv, sel3[:, :, 2:3].to_broadcast([P, NT, P]), ALU.mult))
                link(dve.tensor_tensor(xv, xv, blend[:, 1, :, :], ALU.add))
                after(hid_used, f, CH3 - 1)
                link(dve.tensor_tensor(blend[:, 0, :, :], accum_t[:, 0, 0:W2].rearrange("p (t d) -> p t d", t=NT),
                                       w("f3_b2").unsqueeze(1).to_broadcast([P, NT, P]), ALU.add))
                link(dve.tensor_tensor(blend[:, 0, :, :], blend[:, 0, :, :],
                                       sel3[:, :, 1:2].to_broadcast([P, NT, P]), ALU.mult))
                link(dve.tensor_tensor(xv, xv, blend[:, 0, :, :], ALU.add))

            def offset_layer(b):
                ps = see(narrow, "oqk", b)
                dve.memset(kpad[:, 0:PAD], 0.0)
                dve.memset(vpad[:, 0:PAD], 0.0)
                dve.tensor_scalar(oq, ps[:, 0:SEQ], w("o_bq"), None, ALU.add)
                dve.tensor_scalar(kpad[:, PAD:], ps[:, SEQ:], w("o_bk"), None, ALU.add).then_inc(oqk_ready.s, 1)
                ps = see(narrow, "ov", b)
                dve.tensor_scalar(vpad[:, PAD:], ps[:, 0:SEQ], w("o_bv"), None, ALU.add).then_inc(ov_ready.s, 1)
                after(oqk_ready, b)

                def logits(i):
                    after(qks_ready, b, i)
                    ps = see(wide, "oqk", b, i)
                    o = L[:, 2 * i:2 * i + 2, :].rearrange("p s t -> p (s t)")
                    dve.scalar_tensor_tensor(out=o, in0=ps[:, W2:], scalar=1.0, in1=qks[:, i % 2, :], op0=ALU.add,
                                             op1=ALU.mult).then_inc(L_ready.s, 1)

                for s in range(NSLOT):
                    if s >= 2:
                        after(prod_used, b, s - 2)
                    runs = offset_runs(4 * s, 4)
                    for i0, n, step in runs:
                        j = i0 - 4 * s
                        ins = dve.tensor_tensor(prod[:, s % 2, j:j + n, :], oq.unsqueeze(1).to_broadcast([P, n, SEQ]),
                                                window(kpad, PAD - OFFSETS[i0], step, n, SEQ), ALU.mult)
                    ins.then_inc(prod_ready.s, 1)
                    if s >= 3 and s % 2:
                        logits(s // 2 - 1)
                logits(NSLOT // 2 - 1)
                for t in range(TT):
                    for half in range(2):
                        ps = see(wide, "oturn", b, t, half)
                        dve.tensor_tensor(ltok[:, t, 20 * half:20 * half + 20, :],
                                          ps[:, 0:5 * P].rearrange("p (s r) -> p s r", r=32)[:, :, 0:H],
                                          pbias[:, t, 20 * half:20 * half + 20, :], ALU.add).then_inc(ltok_ready.s, 1)
                after(ltok_ready, b, 1, 1)
                by_head = ltok[:, :, :, :].rearrange("p t o h -> p t h o")
                link(dve.tensor_reduce(rinv[:, b, :, :], by_head, AX.X, ALU.max))
                dve.tensor_tensor(ltok[:, :, :, :], ltok[:, :, :, :],
                                  rinv[:, b, :, :].unsqueeze(2).to_broadcast([P, TT, 4 * NSLOT, H]),
                                  ALU.subtract).then_inc(lmax_ready.s, 1)
                after(lexp_ready, b)
                link(dve.tensor_reduce(rinv[:, b, :, :], by_head, AX.X, ALU.add))
                link(dve.reciprocal(negm[:, b, :, :], rinv[:, b, :, :]))
                link(dve.tensor_tensor(negm[:, b, :, :], negm[:, b, :, :],
                                       w("o_gain").unsqueeze(1).to_broadcast([P, TT, H]), ALU.mult))
                dve.tensor_tensor(ltok[:, :, :, :], ltok[:, :, :, :],
                                  negm[:, b, :, :].unsqueeze(2).to_broadcast([P, TT, 4 * NSLOT, H]),
                                  ALU.mult).then_inc(lprob_ready.s, 1)
                pv = prod[:, :, :, :].rearrange("p r s t -> p r (s t)")
                for t in range(TT):
                    for g in range(5):
                        ps = see(wide, "oprob", b, t, g)
                        n = 8 if g < 4 else 6
                        o = pv[:, g_ring(b, t, g), :].rearrange("p (i t) -> p i t", t=P)
                        runs = offset_runs(8 * g, n)
                        for i0, m, step in runs:
                            j = i0 - 8 * g
                            ins = dve.tensor_tensor(o[:, j:j + m, :],
                                                    ps[:, j * P:(j + m) * P].rearrange("p (i t) -> p i t", t=P),
                                                    window(vpad, PAD + t * P - OFFSETS[i0], step, m, P), ALU.mult)
                        ins.then_inc(pv_ready.s, 1)
                        after(pv_ready, b, t, g)
                        link(dve.tensor_reduce(part[:, g, :], o[:, 0:n, :].rearrange("p i t -> p t i"), AX.X, ALU.add))
                    link(dve.tensor_reduce(oacc[:, t * P:(t + 1) * P], part[:, :, :].rearrange("p g t -> p t g"),
                                           AX.X, ALU.add))
                after(gth_ready, b)
                dve.scalar_tensor_tensor(out=oacc, in0=xn[:, b, :, :].rearrange("p t d -> p (t d)"), scalar=1.0, in1=oacc, op0=ALU.add,
                                         op1=ALU.mult).then_inc(og_ready.s, 1)
                tokens_out("o", b, "o_bo")

            for g in range(1, len(GROUP)):
                group_setup(g)
            dve.wait_ge(const_set, 10)

            with dve.Fori(0, iters):
                after(inputs_in, "all")
                link(dve.tensor_copy(maskf[:, :, :], mask8[:, :, :]))
                dve.tensor_scalar(maskneg[:, :, :], maskf[:, :, :], -1.0, 1e8, ALU.add,
                                  ALU.mult).then_inc(mask_ready.s, 1)
                for s in stages:
                    norm(s)
                    if s in ATT:
                        for step in (att_scale, att_split, att_split2, att_max, att_back):
                            for b in two:
                                step(s, b)
                        if s != "a1":
                            for b in two:
                                tokens_out(s, b, f"{s}_bo")
                    elif s[0] == "x":
                        for step in (cross_project, cross_khat, cross_max, cross_normalise, cross_out):
                            for b in two:
                                step(s, b)
                    elif s == "o":
                        for b in two:
                            offset_layer(b)
                    else:
                        ffn_layer(s)
                dve.drain().then_inc(x_final.s, 1)
                end_of_iteration(dve)

        @block.gpsimd
        def _(pool):
            def after(sig, *key):
                pool.wait_ge(sig.s, sig.at(*key))

            def swish(c):
                after(sg_ready, "f0", c)
                if c >= 2:
                    after(hid_ready, "f0", c - 2)
                pool.tensor_tensor(vb[:, c % 2, :], ab[:, c % 2, :], sg[:, c % 2, :], ALU.mult).then_inc(t_ready.s, 1)

            pool.wait_ge(pbias_in, 16 * TT)
            pool.wait_ge(const_set, 9)
            for i in range(4 * NSLOT):
                for t in range(TT):
                    o = pbias[:, t, i, :]
                    if i >= NOFF:
                        ins = pool.memset(o, NEG)
                    else:
                        ins = pool.affine_select(out=o, in_=o, compare_op=ALU.is_ge, fill=NEG,
                                                 base=t * P - OFFSETS[i], pattern=[[0, H]], channel_multiplier=1)
            pool.drain().then_inc(const_set, 1)

            with pool.Fori(0, iters):
                after(inputs_in, "all")
                for s in stages:
                    if s == "f0":
                        for c in range(CH0):
                            swish(c)
                end_of_iteration(pool)

        @block.sync
        def _(sp):
            def after(sig, *key):
                sp.wait_ge(sig.s, sig.at(*key))

            sp.dma_start(cb[:, :], packed_bf).then_inc(group_loaded[0], 16)
            for g, (a, z) in enumerate(GROUP):
                sp.dma_start(wt[:, a:z], packed[:, a:z]).then_inc(group_loaded[g], 16)
            for t in range(TT):
                sp.dma_start(pbias[:, t, :, :], rows_pb).then_inc(pbias_in, 16)
            sp.wait_ge(const_set, 9)

            def stack(s, b):
                nk = ATT[s][0]
                kdram = scratch_k if nk == SEQ else scratch_kc
                after(parts_ready, s, b)
                sp.dma_start(scratch_q[b].rearrange("c p t -> p c t"), parts[:, b, :, 0:SEQ]).then_inc(scratch_in.s, 16)
                sp.dma_start(kdram[b].rearrange("c p t -> p c t"),
                             parts[:, b, :, SEQ:SEQ + nk]).then_inc(scratch_in.s, 16)
                after(scratch_in, s, b)
                half = H // 2
                for odd in range(2):
                    base = 64 * odd

                    def rows(dram, n, first, count, step):
                        v = dram[b, first, 64 * odd:64 * odd + 64, :]
                        return bass.AP(v.tensor, v.offset, [[step * P * n, count], [half * n, HD], [1, half * n]])

                    for r0, first, count, step in ((0, 0, 3, 0), (24, 1, 2, 0), (40, 2, 1, 0)):
                        sp.dma_start(qs[base + r0:base + r0 + 8 * count, b, :, :],
                                     rows(scratch_q, SEQ, first, count, step)).then_inc(stack_ready[b].s, 16)
                    for r0, first, count, step in ((0, 0, 3, 1), (24, 0, 2, 1), (40, 0, 1, 1)):
                        sp.dma_start(ks[base + r0:base + r0 + 8 * count, b, odd, :, 0:nk],
                                     rows(kdram, nk, first, count, step)).then_inc(stack_ready[b].s, 16)
                    bias = slice(base + ROWS, base + ROWS + 3)
                    if s == "a1":
                        sp.dma_start(qs[bias, b, :, :], rows_const[1]).then_inc(stack_ready[b].s, 16)
                        sp.dma_start(ks[bias, b, odd, :, :], rows_alibi[odd]).then_inc(stack_ready[b].s, 16)
                    if s == "a2":
                        sp.dma_start(qs[bias, b, :, :], rows_const[1]).then_inc(stack_ready[b].s, 16)
                        sp.dma_start(ks[base + ROWS:base + ROWS + 1, b, odd, :, 0:CTX],
                                     maskneg[0:1, b, :].unsqueeze(1).to_broadcast([1, half, CTX])).then_inc(
                                         stack_ready[b].s, 16)
                        sp.dma_start(ks[base + ROWS + 1:base + ROWS + 3, b, odd, :, 0:CTX],
                                     rows_const[0, 0:2, :, 0:CTX]).then_inc(stack_ready[b].s, 16)
                    if s == "a3":
                        sp.dma_start(qs[bias, b, :, :], rows_const[0]).then_inc(stack_ready[b].s, 16)

            with sp.Fori(0, iters) as i:
                for b in two:
                    sp.dma_start(x[:, b, :, :], x_in[bass.ts(i, 1), b].rearrange("i t p d -> p (i t) d")).then_inc(
                        inputs_in.s, 16)
                    sp.dma_start(ctok[:, b, :], ctx_in[bass.ts(i, 1), b].rearrange("i k d -> k (i d)")).then_inc(
                        inputs_in.s, 16)
                    sp.dma_start(mask8[:, b, :], mask_in[bass.ts(i, 1), b, :].to_broadcast([P, CTX])).then_inc(
                        inputs_in.s, 16)
                for s in att:
                    for b in two:
                        stack(s, b)
                after(x_final, "all")
                for b in two:
                    sp.dma_start(out[bass.ts(i, 1), b].rearrange("i t p d -> p (i t) d"), x[:, b, :, :]).then_inc(
                        out_stored.s, 16)
                after(out_stored, "all")
                sp.wait_ge(all_ended, 4)
                sp.sem_clear(counted)
                sp.sem_inc(go_on, 1)
                sp.wait_ge(went_on, 4)
                for s_ in (all_ended, go_on, went_on):
                    sp.sem_clear(s_)


def layout(inputs):
    f = {k: np.asarray(v) for k, v in inputs.items()}
    f32 = np.float32

    def rows(a, n=P):
        a = np.asarray(a).reshape(np.asarray(a).shape[0], -1)
        return np.concatenate([a, np.zeros((n - a.shape[0], a.shape[1]), a.dtype)]) if a.shape[0] < n else a

    def bc(v):
        return np.broadcast_to(np.asarray(v).reshape(1, -1), (P, np.asarray(v).size))

    def col(v):
        return np.asarray(v).reshape(P, 1)

    order = np.array([(2 * p + two) * HD + d for two in range(2) for d in range(HD) for p in range(H // 2)])
    pairs = np.array([0, 2, 4, 6, 1, 3, 5, 7])
    swapped = np.array([1, 3, 5, 7, 0, 2, 4, 6])

    def rotary(which):
        return np.array([(2 * p + two) * HD + which[d] for two in range(2) for d in range(HD) for p in range(H // 2)])

    def chunked(a, n):
        return np.asarray(a).transpose(1, 0, 2).reshape(a.shape[1], -1)

    m = {}
    m["ident"] = np.eye(P, dtype=f32)
    blk = np.zeros((P, 32), f32)
    blk[np.arange(P), np.arange(P) // HD] = HD ** -0.5
    m["blk"] = blk
    hm = np.zeros((P, 32), f32)
    hm[np.arange(P), np.arange(P) // HD] = 1.0
    m["headmask"] = hm
    m["sixteen"] = bc(np.arange(16, dtype=f32))
    W, b = f["L0_attn_W_qkv"], f["L0_attn_b_qkv"]
    m["a0_Wq"], m["a0_Wk"], m["a0_Wv"] = W[:, :P][:, order], W[:, P:2 * P][:, order], W[:, 2 * P:]
    m["a0_bq"], m["a0_bk"], m["a0_bv"] = col(b[:P][order]), col(b[P:2 * P][order]), bc(b[2 * P:])
    m["a0_Wo"], m["a0_bo"] = f["L0_attn_W_proj"], bc(f["L0_attn_b_proj"])
    m["a0_AT"] = rows(f["L0_attn_A_qkv"].T)
    Bq = f["L0_attn_B_qkv"]
    m["a0_B"] = rows(np.concatenate([Bq[:, :P][:, order], Bq[:, P:2 * P][:, order], Bq[:, 2 * P:]], 1))
    m["a0_AoT"], m["a0_Bo"] = rows(f["L0_attn_A_proj"].T), rows(f["L0_attn_B_proj"])
    for n in "qkvr":
        m[f"x0_W{n}"] = f[f"L0_xattn_W{n}"]
    m["x0_bq"], m["x0_bk"], m["x0_br"] = (col(f[f"L0_xattn_b{n}"]) for n in "qkr")
    m["x0_bv"] = bc(f["L0_xattn_bv"])
    w1, b1 = f["L0_ffn_w1"], f["L0_ffn_b1"]
    m["f0_ns"], m["f0_wg"], m["f0_bg"] = col(f["L0_ffn_norm_scale"]), f["L0_ffn_wg"], bc(f["L0_ffn_bg"])
    m["f0_w1"], m["f0_w3"] = chunked(w1[:, :, 0::2], E0), chunked(w1[:, :, 1::2], E0)
    m["f0_w2"] = chunked(f["L0_ffn_w2"], E0)
    m["f0_b1"], m["f0_b3"], m["f0_bt"] = b1[:, 0::2].T, b1[:, 1::2].T, rows(f["L0_ffn_b2"])
    W = f["L1_attn_W_kqv"].T
    m["a1_Wk"], m["a1_Wq"], m["a1_Wv"] = W[:, :P][:, order], W[:, P:2 * P][:, order], W[:, 2 * P:]
    ws = f["L1_xattn_w_sim"]
    m["x1_w1"], m["x1_w3"], m["x1_w2"] = col(ws[:P]), col(ws[2 * P:]), col(ws[P:2 * P])
    m["x1_bs"], m["x1_Wqv"], m["x1_b"] = bc(f["L1_xattn_b_sim"]), chunked(f["L1_xattn_W_qv"].reshape(4, P, P), 4), bc(f["L1_xattn_b_qv"])
    m["f1_wg"], m["f1_bg"] = f["L1_ffn_gate_w"], bc(f["L1_ffn_gate_b"])
    for to, n in (("w1", "w1"), ("w3", "w2")):
        m[f"f1_{to}"] = chunked(np.concatenate([f[f"L1_ffn_r{n}"], f[f"L1_ffn_s{n}"]]), 0)
    m["f1_w2"] = chunked(np.concatenate([f["L1_ffn_rw3"], f["L1_ffn_sw3"]]).reshape(CH1, P, P), CH1)
    for to, n in (("b1", "b1"), ("b3", "b2")):
        m[f"f1_{to}"] = np.concatenate([f[f"L1_ffn_r{n}"], f[f"L1_ffn_s{n}"]]).reshape(CH1, P).T
    m["f1_bt"] = rows(np.concatenate([f["L1_ffn_rb3"], f["L1_ffn_sb3"]]))
    W, b = f["L2_attn_qkv_w"].T, f["L2_attn_qkv_b"]
    for i, n in enumerate("qkv"):
        m[f"o_W{n}"], m[f"o_b{n}"] = W[:, i * P:(i + 1) * P], col(b[i * P:(i + 1) * P])
    m["o_Wg"], m["o_bg"] = f["L2_attn_gate_w"].T, col(f["L2_attn_gate_b"])
    m["o_Wo"], m["o_bo"], m["o_gain"] = f["L2_attn_out_w"].T, bc(f["L2_attn_out_b"]), bc(f["L2_attn_if_gain"])
    perm = np.array([SORTED.index(o) for o in OFFSETS] + [0] * (4 * NSLOT - NOFF))
    m["o_emb"] = np.tile(f["L2_attn_scale_embed"][perm].T, (H, 1))
    pos_bias = np.ascontiguousarray(bc(f["L2_attn_pos_bias"][perm])).reshape(P, 4 * NSLOT, H)
    for n, t in (("q", "q"), ("k", "k")):
        m[f"a2_W{n}"], m[f"a2_b{n}"] = f[f"L2_xattn_W{n}"].T[:, order], col(f[f"L2_xattn_b{n}"][order])
    m["a2_Wv"], m["a2_bv"] = f["L2_xattn_Wv"].T, bc(f["L2_xattn_bv"])
    m["a2_Wo"], m["a2_bo"] = f["L2_xattn_Wo"].T, bc(f["L2_xattn_bo"])
    m["f2_wg"] = f["L2_ffn_gate_w"][:E2].T
    m["f2_w1"], m["f2_w3"] = chunked(f["L2_ffn_w1"][:E2], 0), chunked(f["L2_ffn_w3"][:E2], 0)
    m["f2_w2"] = chunked(f["L2_ffn_w2"][:E2].reshape(CH2, P, P), CH2)
    W, b = f["L3_attn_qkv_w"], f["L3_attn_qkv_b"]
    for i, n in enumerate("qk"):
        Wn, bn_ = W[:, i * P:(i + 1) * P], b[i * P:(i + 1) * P]
        m[f"a3_W{n}"], m[f"a3_b{n}"] = Wn[:, rotary(pairs)], col(bn_[rotary(pairs)])
        m[f"a3_W{n}s"], m[f"a3_b{n}s"] = Wn[:, rotary(swapped)], col(bn_[rotary(swapped)])
    m["a3_Wv"], m["a3_bv"] = W[:, 2 * P:], bc(b[2 * P:])
    m["a3_Wo"], m["a3_bo"] = f["L3_attn_out_w"], bc(f["L3_attn_out_b"])
    inv_freq = (f32(1.0) / f32(10000.0) ** (np.arange(0, HD, 2, dtype=f32) / f32(HD))).astype(f32)
    freqs = np.arange(SEQ, dtype=f32)[:, None] * inv_freq[None, :]
    table = np.concatenate([np.sin(freqs), np.cos(freqs)], -1).astype(f32)
    sin, cos = table[:, 0::2], table[:, 1::2]
    C = np.concatenate([cos, cos], 1).T
    S = np.concatenate([-sin, sin], 1).T
    at = np.array([d for two in range(2) for d in range(HD) for p in range(H // 2)])
    m["rope"] = np.concatenate([C[at], S[at]], 1).astype(f32)
    for n in "qk":
        m[f"a4_W{n}"] = f[f"L3_xattn_W_{n}"][:, order]
    m["a4_Wv"], m["a4_Wo"], m["a4_bo"] = f["L3_xattn_W_v"], f["L3_xattn_W_o"], bc(f["L3_xattn_b_o"])
    m["f3_wr"], m["f3_br"], m["f3_w1"] = f["L3_ffn_w_r"], bc(f["L3_ffn_b_r"]), f["L3_ffn_W1"]
    m["f3_w2"] = chunked(f["L3_ffn_W2"].reshape(CH3, P, P), CH3)
    m["f3_b1"], m["f3_b2"] = f["L3_ffn_b1"].reshape(CH3, P).T, bc(f["L3_ffn_b2"])
    for name, (_, n) in COLS.items():
        assert m[name].shape == (P, n), (name, m[name].shape, n)
    packed = np.concatenate([np.asarray(m[name], f32) for g in LAYOUT for name, _ in g], 1)

    bf = mybir.dt.np(BF16)
    sel = np.zeros((P, H), f32)
    for h in range(H):
        for part in range(3):
            sel[32 * part + h, h] = 1.0
    i = np.arange(P)
    qk_mask = np.where(i[None, :] <= i[:, None], 0.0, NEG)
    zero = np.zeros((P, P))
    packed_bf = np.concatenate([sel.reshape(P, -1), np.eye(P), qk_mask, zero, qk_mask,
                                qk_mask.T, zero, qk_mask.T], 1).astype(bf)
    base = (2 ** 8) ** (1.0 / H)
    slopes = np.array([1.0 / base ** (h + 1) for h in range(H)], f32)
    bias = (slopes[:, None] * np.arange(SEQ, dtype=f32)[None, :]).astype(f32)
    p0 = bias.astype(bf)
    p1 = (bias - p0.astype(f32)).astype(bf)
    p2 = (bias - p0.astype(f32) - p1.astype(f32)).astype(bf)
    alibi = np.stack([np.stack([q[odd::2] for q in (p0, p1, p2)]) for odd in range(2)])
    const = np.stack([np.zeros((3, H // 2, SEQ)), np.ones((3, H // 2, SEQ))]).astype(bf)
    n = B // PAIR
    return {
        "x": np.ascontiguousarray(f["x"]).reshape(n, PAIR, TT, P, P),
        "ctx": np.ascontiguousarray(f["ctx_1024"]).reshape(n, PAIR, CTX, P),
        "mask": np.ascontiguousarray(f["mask_BxS2_bf1"]).view(np.uint8).reshape(n, PAIR, CTX),
        "packed": packed, "packed_bf": packed_bf, "alibi": alibi, "const": const, "pos_bias": pos_bias,
    }


def build(nc, arrays, **kw):
    aps = [nc.dram_tensor(f"in_{k}", a.shape, mybir.dt.from_np(a.dtype), kind="ExternalInput").ap()
           for k, a in arrays.items()]
    scratch = [nc.dram_tensor(n, [PAIR, 3, P, t], BF16, kind="Internal").ap()
               for n, t in (("scratch_q", SEQ), ("scratch_k", SEQ), ("scratch_kc", CTX))]
    out = nc.dram_tensor("out", [B // PAIR, PAIR, TT, P, P], F32, kind="ExternalOutput").ap()
    build_decoder(nc, *aps, *scratch, out, **kw)


def kernel(**inputs):
    import concourse.bacc as bacc
    from concourse.bass_utils import run_bass_kernel_spmd

    arrays = layout(inputs)
    nc = bacc.Bacc("TRN2", target_bir_lowering=False, num_devices=1)
    build(nc, arrays)
    r = run_bass_kernel_spmd(nc, [{f"in_{k}": a for k, a in arrays.items()}], core_ids=[0])
    return np.asarray(r.results[0]["out"]).reshape(B, SEQ, P)
```

```python
from contextlib import ExitStack

import numpy as np

import concourse.bass as bass
from concourse import mybir

P = 128
B = 16
SEQ = 256
CTX = 64
H = 16
HD = P // H
TT = SEQ // P
PAIR = 2
NT = PAIR * TT
W2 = PAIR * SEQ

F32 = mybir.dt.float32
BF16 = mybir.dt.bfloat16
U32 = mybir.dt.uint32
I32 = mybir.dt.int32
ALU = mybir.AluOpType
ACT = mybir.ActivationFunctionType
AX = mybir.AxisListType

NEG = -1e30
LN_EPS = 1e-5
ROOT_GUESS = float(0x5F3759DF)
MAGIC = 12582912.0
TWO_PI = (6.28125, 0.0019353071795864769)

OFFSETS = [8 * r + 7 - i for r in range(4) for i in range(8)] + [192, 128, 96, 64, 48, 32]
SORTED = sorted(OFFSETS)
NOFF = len(OFFSETS)
NSLOT = 10
PAD = max(OFFSETS)

E0, K0 = 16, 4
E1, K1, S1 = 8, 2, 2
E2, K2, HID2 = 4, 2, 704
EXPERTS = {"f0": (E0, K0), "f1": (E1, K1), "f2": (E2, K2)}
BIAS_AT = 6
CH0, CH1, CH2, CH3 = E0, 2 * (E1 + S1), E2 * HID2 // P, 4

LAYOUT = [
    [("ident", P), ("blk", 32), ("headmask", 32), ("sixteen", 16),
     ("a0_Wq", P), ("a0_Wk", P), ("a0_Wv", P), ("a0_Wo", P), ("a0_AT", P), ("a0_B", 3 * P),
     ("a0_AoT", P), ("a0_Bo", P), ("a0_bq", 1), ("a0_bk", 1), ("a0_bv", P), ("a0_bo", P),
     ("x0_Wq", P), ("x0_Wk", P), ("x0_Wv", P), ("x0_Wr", P), ("x0_bq", 1), ("x0_bk", 1), ("x0_br", 1), ("x0_bv", P)],
    [("f0_ns", 1), ("f0_wg", E0), ("f0_bg", E0), ("f0_w1", CH0 * P), ("f0_w3", CH0 * P), ("f0_w2", CH0 * P),
     ("f0_b1", CH0), ("f0_b3", CH0), ("f0_bt", P)],
    [("a1_Wq", P), ("a1_Wk", P), ("a1_Wv", P), ("x1_w1", 1), ("x1_w3", 1), ("x1_w2", 1), ("x1_bs", 1),
     ("x1_Wqv", 4 * P), ("x1_b", P),
     ("f1_wg", E1), ("f1_bg", E1), ("f1_w1", CH1 * P), ("f1_w3", CH1 * P), ("f1_w2", CH1 * P),
     ("f1_b1", CH1), ("f1_b3", CH1), ("f1_bt", P)],
    [("o_Wq", P), ("o_Wk", P), ("o_Wv", P), ("o_Wg", P), ("o_Wo", P), ("o_bq", 1), ("o_bk", 1), ("o_bv", 1),
     ("o_bg", 1), ("o_bo", P), ("o_gain", H), ("o_emb", 4 * NSLOT),
     ("a2_Wq", P), ("a2_Wk", P), ("a2_Wv", P), ("a2_Wo", P), ("a2_bq", 1), ("a2_bk", 1), ("a2_bv", P), ("a2_bo", P),
     ("f2_wg", E2), ("f2_w1", CH2 * P), ("f2_w3", CH2 * P), ("f2_w2", CH2 * P)],
    [("a3_Wq", P), ("a3_Wqs", P), ("a3_Wk", P), ("a3_Wks", P), ("a3_Wv", P), ("a3_Wo", P),
     ("a3_bq", 1), ("a3_bqs", 1), ("a3_bk", 1), ("a3_bks", 1), ("a3_bv", P), ("a3_bo", P), ("rope", 2 * SEQ),
     ("a4_Wq", P), ("a4_Wk", P), ("a4_Wv", P), ("a4_Wo", P), ("a4_bo", P),
     ("f3_wr", 1), ("f3_br", 1), ("f3_w1", CH3 * P), ("f3_w2", CH3 * P), ("f3_b1", CH3), ("f3_b2", P)],
]
COLS = {}
GROUP = []
_at = 0
for _g in LAYOUT:
    _from = _at
    for _name, _n in _g:
        COLS[_name] = (_at, _n)
        _at += _n
    GROUP.append((_from, _at))
NW = _at
BCOLS = {"sel": (0, H), "identb": (H, P), "mask_qk": (H + P, 3 * P), "mask_kq": (H + 4 * P, 3 * P)}
NBC = H + 7 * P
BANKS = 6
PART = 2816

Q_SLOTS = {0: (2, 1, 3), 1: (1, 4, 2), 2: (0, 1, 1)}
K_SLOTS = {0: (0, 1, 3), 1: (3, 2, 2), 2: (4, 1, 1)}
SLOTS = 7

GROUP_OF = {"a0": 0, "x0": 0, "f0": 1, "a1": 2, "x1": 2, "f1": 2, "o": 3, "a2": 3, "f2": 3, "a3": 4, "a4": 4, "f3": 4}
STAGES = ["a0", "x0", "f0", "a1", "x1", "f1", "o", "a2", "f2", "a3", "a4", "f3"]
ATT = {"a0": (SEQ, False, HD ** -0.5), "a1": (SEQ, True, P ** -0.5), "a2": (CTX, False, HD ** -0.5),
       "a3": (SEQ, True, None), "a4": (CTX, False, HD ** -0.5)}


DOWN_LAG = 3
CHUNKS = {"f0": CH0, "f1": CH1, "f2": CH2, "f3": CH3}
MAX_CHUNKS = {s: (16 if ATT[s][0] == SEQ else 4) for s in ATT}
SCORE_CHUNKS = {s: (16 if ATT[s][0] == SEQ else 8) for s in ATT}


def steps_of(s, b):
    norm = [("stats", s, b), ("norm", s, b)]
    if s == "f0":
        norm += [("rms", s, b), ("rms_norm", s, b)]
    norm += [("turn_norm", s, b)]
    if s in ATT:
        return (norm + [("project", s, b), ("split", s, b)]
                + [("max", s, b, c) for c in range(MAX_CHUNKS[s])] + [("split_max", s, b), ("turn_max", s, b)]
                + [("core", s, b, c) for c in range(SCORE_CHUNKS[s] + 1)]
                + [("back", s, b), ("turn", s, b), ("out", s, b)])
    if s[0] == "x":
        return norm + [("cross_project", s, b), ("cross_khat", s, b), ("cross_scores", s, b),
                ("cross_turn", s, b), ("cross_out", s, b)]
    if s == "o":
        return norm + [("offset_scores", s, b), ("offset_softmax", s, b), ("offset_values", s, b)]
    return (norm + [("logits", s, b)] + [("chunk", s, b, c) for c in range(CHUNKS[s] + DOWN_LAG + 1)]
            + ([("select", s, b)] if s == "f3" else []))


SPAN = {"stats": 5, "norm": 3.5, "rms": 5, "rms_norm": 2.1, "turn_norm": 2.1, "project": 2, "split": 28.8,
        "max": 0.8, "split_max": 3.3, "turn_max": 1.2, "core": 1.4, "back": 3.6, "turn": 1.5, "out": 2.4,
        "cross_project": 4.8, "cross_khat": 1.5, "cross_scores": 3.9, "cross_turn": 2, "cross_out": 7.2,
        "logits": 1.1, "chunk": 1.4, "select": 3.4, "offset_scores": 0, "offset_softmax": 0,
        "offset_values": 0}


LAGS = [12, 3]


def merged(a, b, lag):
    at = []
    for which, steps in enumerate((a, b)):
        start = lag * which
        for v in steps:
            at.append((start, which, len(at), v))
            start += SPAN[v[0]]
    return [v for _, _, _, v in sorted(at)]


def plan_of(stages):
    if "o" not in stages:
        return merged(*([v for s in stages for v in steps_of(s, b)] for b in range(PAIR)), LAGS[0])
    at = stages.index("o")
    norm = len(steps_of("o", 0)) - 3
    before, layer, after = ([[v for s in part for v in steps_of(s, b)] for b in range(PAIR)]
                            for part in (stages[:at], ["o"], stages[at + 1:]))
    steps = merged(*(before[b] + layer[b][:norm] for b in range(PAIR)), LAGS[0]) + layer[0][norm:]
    for i, v in enumerate(layer[1][norm:]):
        steps += after[0][i:min(i + 1, norm - 1)] + [v]
    return steps + merged(after[0][norm - 1:], after[1], LAGS[1])


class Signal:

    def __init__(self, sem, keys, by=1):
        self.s = sem
        self.value = {k: by * (i + 1) for i, k in enumerate(keys)}

    def at(self, *key):
        return self.value[key]


class Ring:

    def __init__(self, tile, full):
        self.tile, self.full = tile, full
        self.n, self.fills, self.drains = 0, {}, [None] * len(full)

    def take(self, key, drained):
        slot = self.n % len(self.full)
        before, self.drains[slot] = self.drains[slot], drained
        assert key not in self.fills, key
        self.fills[key] = (slot, self.n // len(self.full) + 1)
        self.n += 1
        return slot, before

    def at(self, *key):
        return self.fills[key]


def build_decoder(nc, x_in, ctx_in, mask_in, packed, packed_bf, rows_q, rows_k, rows_pb, image_q, image_k, image_kc, out,
                  stages=STAGES, iters=B // PAIR):
    ctx = ExitStack()
    with ctx:
        def sb(name, shape, dt=F32):
            return ctx.enter_context(nc.sbuf_tensor(name, shape, dt))

        def sem(name):
            return ctx.enter_context(nc.semaphore(name))

        two = range(PAIR)

        wt = sb("weights", [P, NW])
        cb = sb("constants_bf", [P, NBC], BF16)
        x = sb("x", [P, PAIR, TT, P])
        xn = sb("xn", [P, PAIR, TT, P])
        xnT = sb("xnT", [P, PAIR, SEQ])
        ctok = sb("ctok", [CTX, PAIR, P])
        ctxT = sb("ctxT", [P, PAIR, CTX])
        mask8 = sb("mask8", [P, PAIR, CTX], mask_in.dtype)
        maskf = sb("maskf", [P, PAIR, CTX])
        maskneg = sb("maskneg", [P, PAIR, CTX], BF16)
        bn = sb("bn_stats", [P, PAIR, TT, 6])
        mv = sb("mv", [P, NT, 2])
        var = sb("var", [P, NT])
        rstd = sb("rstd", [P, NT])
        nt = sb("newton", [P, NT])
        sumsq = sb("sumsq", [P, NT])
        halfpi = sb("halfpi", [P, 1])
        f0_b3p = sb("f0_b3p", [P, CH0])
        f1_b1h = sb("f1_b1h", [P, CH1])
        gain = sb("gain", [P, H])
        o_bgh = sb("o_bgh", [P, 1])
        ones = sb("ones", [P, P])
        emb = sb("emb", [P, NSLOT, P])
        pbias = sb("pbias", [P, TT, 4 * NSLOT, H])
        qs = sb("q_stack", [P, PAIR, H // 2, SEQ], BF16)
        ks = sb("k_stack", [P, PAIR, 2, H // 2, SEQ], BF16)
        vaug = sb("vaug", [P, PAIR, TT, H, HD + 1])
        negm = sb("negm", [P, PAIR, TT, H])
        mres = sb("mres", [P, PAIR, TT, H])
        mparts = sb("mparts", [P, PAIR, TT, P], BF16)
        negmT = sb("negmT", [P, PAIR, SEQ], BF16)
        rinv = sb("rinv", [P, PAIR, TT, H])
        small = sb("small", [P, PAIR, 16])
        lg = sb("lg", [P, NT, 16])
        ex = sb("ex", [P, NT, 16])
        em = sb("em", [P, NT, 16])
        top = sb("top", [P, NT, 8])
        topi = sb("topi", [P, NT, 8], U32)
        topf = sb("topf", [P, NT, 8])
        hot = sb("hot", [P, NT, 4, 16])
        rsum = sb("rsum", [P, NT, 2])
        gates = sb("gates", [P, NT, 16])
        gatesT = sb("gatesT", [16, W2])
        work = sb("work", [P, 8064])

        def w(name):
            a, n = COLS[name]
            return wt[:, a:a + n]

        def wb(name):
            a, n = BCOLS[name]
            return cb[:, a:a + n]

        def cut(at, *dims):
            n = int(np.prod(dims))
            v = work[:, at:at + n]
            if len(dims) == 1:
                return v
            names = "abcd"[:len(dims)]
            return v.rearrange(f"p ({' '.join(names)}) -> p {' '.join(names)}", **dict(zip(names[1:], dims[1:])))

        def both(at, *dims):
            n = int(np.prod(dims))
            v = work[:, 0:PAIR * PART].rearrange("p (b n) -> p b n", b=PAIR)[:, :, at:at + n]
            if len(dims) == 1:
                return v
            names = "xyz"[:len(dims)]
            return v.rearrange(f"p b ({' '.join(names)}) -> p b {' '.join(names)}", **dict(zip(names[1:], dims[1:])))

        qk = both(0, 2 * SEQ)
        res = both(512, 2 * SEQ)
        parts = both(1024, 768).bitcast(BF16).rearrange("p b (c t) -> p b c t", c=3)
        osp = both(1792, 4, SEQ)
        otok = both(0, TT, P)
        oT = both(256, SEQ)
        rt = both(1792, 2, SEQ)
        probs = cut(PAIR * PART, 4, 512)
        zc = both(512, CTX)
        zn = both(576, CTX)
        khat = both(640, CTX)
        pr = both(704, TT, CTX)
        sim = both(832, TT, CTX)
        dk = both(960, CTX)
        prT = both(1024, SEQ)
        vx = both(1280, P)
        hqT = both(1408, SEQ)
        feat3 = both(1664, SEQ)
        feat4 = both(1920, SEQ)
        hid = both(0, 3, SEQ)
        sg = both(768, 2, SEQ)
        ab = both(1280, 2, SEQ)
        ub = both(1792, 2, SEQ)
        vb = both(2304, 2, SEQ)
        junk = both(2304, SEQ)
        sel3 = both(768, TT, 4)
        blend = both(1024, 2, TT, P)
        cmpj = both(1536, SEQ)
        oq = cut(0, SEQ)
        kpad = cut(256, PAD + SEQ)
        vpad = cut(704, PAD + SEQ)
        prod = cut(1152, 2, 4, SEQ)
        qks = cut(3200, 2, 2 * SEQ)
        L = cut(4224, NSLOT, SEQ)
        pexp = cut(4224, 2, 8, P)
        ltok = cut(6784, TT, 4 * NSLOT, H)
        oacc = oq

        banks_t = ctx.enter_context(nc.psum_tensor("banks", [P, BANKS, 512], F32))
        doubles_t = banks_t[:, 0:4, :].rearrange("p (s a) n -> p s (a n)", a=2)
        accum_t = ctx.enter_context(nc.psum_tensor("accum", [P, PAIR, 512], F32))

        group_loaded = [sem(f"group_loaded{g}") for g in range(len(GROUP))]
        const_set = sem("const_set")
        pbias_in = sem("pbias_in")
        images_set = sem("images_set")
        pre_step = sem("pre_step")
        pre_mm = sem("pre_mm")
        pre_fold = sem("pre_fold")
        all_ended = sem("all_ended")
        go_on = sem("go_on")
        went_on = sem("went_on")

        first_counted = []

        def signal(name, keys, by=1):
            s = sem(name)
            first_counted.append(s)
            return Signal(s, keys, by)

        def ring(name, tile, n):
            full = [sem(f"{name}_full{i}") for i in range(n)]
            first_counted.extend(full)
            return Ring(tile, full)

        plan = plan_of(stages)

        def during(*names, only=None):
            return [tuple(key) for step, *key in plan if step in names and (only is None or key[0] in only)]

        def at_chunk(n, only=tuple(EXPERTS)):
            return [(f, b) for f, b, c in during("chunk", only=only) if c == n]

        att = [s for s in stages if s in ATT]
        routed = [s for s in stages if s in EXPERTS]

        banks, doubles = ring("bank", banks_t, BANKS), ring("double", doubles_t, 2)
        inputs_in = signal("inputs_in", [("all",)], 16 * (2 + 2 * PAIR))
        mask_ready = signal("mask_ready", [("all",)])
        ctxT_ready = signal("ctxT_ready", [("all",)])
        out_stored = signal("out_stored", [("all",)], 16 * PAIR)
        dve_done = signal("dve_done", [])
        out_taken = signal("out_taken", [(s, b) for step, s, b, *_ in plan
                                         if step == ("back" if s == "a1" else "out") or step in ("cross_out", "offset_values")])
        x_final = signal("x_final", [("all",)])
        squares = signal("squares", during("rms"))
        xn_mid = signal("xn_mid", during("norm", only=("f0",)))
        v_stats = signal("variance_ready", [(step, s, b) for step, s, b, *_ in plan if step in ("stats", "rms")])
        rstd_ready = signal("rstd_ready", [(step, s, b) for step, s, b, *_ in plan if step in ("stats", "rms")])
        pool_done = signal("pool_done", [])
        xn_ready = signal("xn_ready", [(s, b) for step, s, b, *_ in plan
                                       if step == ("rms_norm" if s == "f0" else "norm")])
        xnT_ready = signal("xnT_ready", during("turn_norm"))
        q_taken = signal("q_taken", during("project", only=("a3",)))
        qk_ready = signal("qk_ready", during("project"))
        part0 = signal("part0", during("split"))
        res_ready = signal("res_ready", during("split"))
        part1 = signal("part1", during("split"))
        parts_ready = signal("parts_ready", during("split"))
        v_ready = signal("v_ready", during("project"))
        scratch_in = signal("scratch_in", during("split"), 16 * 2 * 3)

        stack_ready = [signal(f"stack_ready{b}", [(s,) for s in att], 16 * 4) for b in two]
        mask_stored = signal("mask_stored", [("all",)], 16 * 2 * PAIR)
        mparts_ready = signal("mparts_ready", during("split_max"))
        negmT_ready = signal("negmT_ready", during("turn_max"))
        max_taken = signal("max_taken", during("max"))
        probs_keys = [(s, b, c) for s, b, c in during("core") if c < SCORE_CHUNKS[s]]
        probs_ready = signal("probs_ready", probs_keys)
        probs_used = signal("probs_used", [(s, b, c - 1) for s, b, c in during("core") if c])
        osp_ready = signal("osp_ready", [(s, b, 2 * c // SCORE_CHUNKS[s] - 1) for s, b, c in during("core")
                                         if c and 2 * c % SCORE_CHUNKS[s] == 0])
        otok_ready = signal("otok_ready", [(s, b, t) for s, b in during("back") for t in range(TT)])
        oT_ready = signal("oT_ready", [(s, b) for s, b in during("turn") if s != "a1"])
        proj_ready = signal("proj_ready", during("cross_project"))
        vx_ready = signal("vx_ready", during("cross_project", only=["x0"]))
        khat_taken = signal("khat_taken", during("cross_khat", only=["x0"]))
        khat_arg = signal("khat_arg", during("cross_khat", only=["x0"]))
        khat_ready = signal("khat_ready", during("cross_khat", only=["x0"]))
        sim_ready = signal("sim_ready", during("cross_scores", only=["x1"]))
        bsum_taken = signal("bsum_taken", during("cross_out", only=["x1"]))
        xmax_ready = signal("xmax_ready", during("cross_scores"))
        xexp_ready = signal("xexp_ready", during("cross_scores"))
        xprob_ready = signal("xprob_ready", during("cross_turn"))
        prT_ready = signal("prT_ready", during("cross_turn"))
        hqT_ready = signal("hqT_ready", during("cross_out", only=["x1"]))
        bmax_ready = signal("bmax_ready", during("cross_turn", only=["x1"]))
        bexp_ready = signal("bexp_ready", during("cross_turn", only=["x1"]))
        feats_ready = signal("feats_ready", during("cross_out", only=["x1"]))
        logits_taken = signal("logits_taken", during("logits"))
        counts_ready = signal("counts_ready", during("logits", only=("f3",)))
        w_tok = signal("w_tok", during("logits", only=("f3",)))
        logit_arg = signal("logit_arg", during("logits", only=routed))
        logit_exp = signal("logit_exp", during("logits", only=routed))
        gates_ready = signal("gates_ready", at_chunk(2))
        gatesT_ready = signal("gatesT_ready", at_chunk(BIAS_AT, only=("f0", "f1")))

        def pieces(f):
            found = []
            for c in range(CHUNKS[f]):
                if f == "f2":
                    for e in range(E2):
                        a, z = max(e * HID2, c * P), min((e + 1) * HID2, (c + 1) * P)
                        if a < z:
                            found.append((c, e, a - c * P, z - c * P, a == e * HID2, z == (e + 1) * HID2,
                                          c + (a > c * P)))
                else:
                    n = {"f0": 1, "f1": 2, "f3": CH3}[f]
                    found.append((c, c // n, 0, P, c % n == 0, c % n == n - 1, c))
            return found

        def last_use(f, c):
            return max(p[1] for p in pieces(f) if p[0] == c)

        ends = {(f, e): c for f in routed for c, e, _, _, _, last, _ in pieces(f) if last}
        ch = [(f, b, c) for f, b, c in during("chunk") if c < CHUNKS[f]]
        a_ready = signal("a_ready", [k for k in ch if k[0] == "f0"])
        u_ready = signal("u_ready", [(f, b, c - (f != "f0")) for f, b, c in during("chunk", only=routed)
                                     if 0 <= c - (f != "f0") < CHUNKS[f]])
        sg_ready = signal("sg_ready", [k for k in ch if k[0] != "f3"])
        th_ready = signal("th_ready", [k for k in ch if k[0] != "f3"])
        t_ready = signal("t_ready", [k for k in ch if k[0] == "f0"])
        hid_ready = signal("hid_ready", [(f, b, c - (f != "f3")) for f, b, c in during("chunk")
                                         if 0 <= c - (f != "f3") < CHUNKS[f]])
        hid_used = signal("hid_used", [(f, b, p[0], p[1]) for f, b, c in during("chunk") for p in pieces(f) if p[6] == c - DOWN_LAG])
        y_added = signal("y_added", [(f, b, e) for f, b, c in during("chunk") for g, e in ends
                                     if g == f and ends[g, e] == c - DOWN_LAG - 1])
        y_biased = signal("y_biased", at_chunk(BIAS_AT + 1, only=("f0", "f1")))
        oqk_ready = signal("oqk_ready", [(b,) for b in two])
        ov_ready = signal("ov_ready", [(b,) for b in two])
        gth_ready = signal("gth_ready", [(b,) for b in two])
        ltok_ready = signal("ltok_ready", [(b, t, half) for b in two for t in range(TT) for half in range(2)])
        slots = [(b, s) for b in two for s in range(NSLOT)]
        prod_ready = signal("prod_ready", slots)
        prod_used = signal("prod_used", slots)
        qks_ready = signal("qks_ready", [(b, s) for b in two for s in range(NSLOT // 2)])
        L_ready = signal("L_ready", [(b, s) for b in two for s in range(NSLOT // 2)])
        lmax_ready = signal("lmax_ready", [(b, t) for b in two for t in range(TT)])
        lexp_ready = signal("lexp_ready", [(b, t) for b in two for t in range(TT)])
        lprob_ready = signal("lprob_ready", [(b, t) for b in two for t in range(TT)])
        groups = [(b, t, g) for b in two for t in range(TT) for g in range(5)]
        pexp_ready = signal("pexp_ready", groups)
        pv_ready = signal("pv_ready", groups)
        pv_used = signal("pv_used", groups)
        og_ready = signal("og_ready", [(b,) for b in two])
        counted = range(min(s.num for s in first_counted), max(s.num for s in first_counted) + 1)
        assert len(counted) == len(first_counted)

        def g_ring(b, t, g):
            return groups.index((b, t, g)) % 2

        class Steps:

            def __init__(self, eng, sig):
                self.eng, self.s, self.n = eng, sig.s, 0

            def link(self, ins):
                self.mark(ins)
                self.eng.wait_ge(self.s, self.n)

            def mark(self, ins):
                self.n += 1
                ins.then_inc(self.s, 1)
                return self.n

        def end_of_iteration(eng):
            eng.drain().then_inc(all_ended, 1)
            eng.wait_ge(go_on, 1)
            eng.sem_inc(went_on, 1)

        def window(buf, start, step, n, length):
            v = buf[:, start:start + length]
            return bass.AP(v.tensor, v.offset, [list(v.ap[0]), [step, n], [1, length]])

        def offset_runs(i0, n):
            if i0 < 32:
                return [(i0, n, 1)]
            return [(i, 2, OFFSETS[i] - OFFSETS[i + 1]) for i in range(i0, min(i0 + n, NOFF), 2)]

        block = ctx.enter_context(nc.Block())

        @block.tensor
        def _(pe):
            ident = w("ident")

            def take(r, key, drained, *event):
                slot, before = r.take(key, (drained, event))
                if before:
                    pe.wait_ge(before[0].s, before[0].at(*before[1]))
                return slot, r.tile[:, slot, :], r.full[slot]

            pe.wait_ge(group_loaded[0], 32)
            pe.matmul(banks_t[:, 0, 0:3 * P], w("a0_AT")[0:8, :], w("a0_B")[0:8, :], start=True, stop=True)
            pe.matmul(banks_t[:, 1, 0:P], w("a0_AoT")[0:8, :], w("a0_Bo")[0:8, :], start=True,
                      stop=True).then_inc(pre_mm, 1)
            pe.wait_ge(pre_fold, 1)

            def norm(s, b):
                pe.wait_ge(group_loaded[GROUP_OF[s]], 16 + 16 * (GROUP_OF[s] == 0))
                _, ps, full = take(banks, ("norm", s, b), xnT_ready, s, b)
                pe.wait_ge(xn_ready.s, xn_ready.at(s, b))
                for t in range(TT):
                    mm = pe.transpose(ps[:, t * P:(t + 1) * P], xn[:, b, t, :], ident)
                mm.then_inc(full, 1)

            def context():
                _, ps, full = take(banks, ("ctx",), ctxT_ready, "all")
                pe.wait_ge(inputs_in.s, inputs_in.at("all"))
                for b in two:
                    mm = pe.transpose(ps[:, b * CTX:(b + 1) * CTX], ctok[:, b, :], ident[0:CTX, 0:CTX])
                mm.then_inc(full, 1)

            def att_project(s, b):
                nk = ATT[s][0]
                pe.wait_ge(xnT_ready.s, xnT_ready.at(s, b))
                pe.wait_ge(ctxT_ready.s, ctxT_ready.at("all"))
                src = xnT[:, b, :] if nk == SEQ else ctxT[:, b, :]
                if s == "a3":
                    for n in ("q", "k"):
                        _, ps, full = take(banks, (n, s, b), q_taken if n == "q" else qk_ready, s, b)
                        pe.matmul(ps[:, 0:SEQ], w(f"a3_W{n}"), xnT[:, b, :], start=True, stop=True)
                        pe.matmul(ps[:, SEQ:2 * SEQ], w(f"a3_W{n}s"), xnT[:, b, :], start=True,
                                  stop=True).then_inc(full, 1)
                else:
                    _, ps, full = take(banks, ("qk", s, b), qk_ready, s, b)
                    pe.matmul(ps[:, 0:SEQ], w(f"{s}_Wq"), xnT[:, b, :], start=True, stop=True)
                    pe.matmul(ps[:, SEQ:SEQ + nk], w(f"{s}_Wk"), src, start=True, stop=True).then_inc(full, 1)
                _, ps, full = take(banks, ("v", s, b), v_ready, s, b)
                n = min(nk, P)
                for t in range(nk // n):
                    mm = pe.matmul(ps[0:n, t * P:(t + 1) * P], src[:, t * n:(t + 1) * n], w(f"{s}_Wv"),
                                   start=True, stop=True)
                mm.then_inc(full, 1)

            def att_max(s, b, c):
                nk, causal, _ = ATT[s]
                if c == 0:
                    pe.wait_ge(stack_ready[b].s, stack_ready[b].at(s))
                per = H // MAX_CHUNKS[s]
                _, ps, full = take(banks, ("max", s, b, c), max_taken, s, b, c)
                for i in range(per):
                    h = c * per + i
                    q = qs[:, b, h // 2, :]
                    if causal:
                        o = ps[:, 0:3 * P]
                        pe.matmul(o, wb("identb"), wb("mask_qk"), start=True, stop=False)
                        pe.matmul(o[:, 0:P], q[:, 0:P], ks[:, b, h % 2, h // 2, 0:P], start=False, stop=False)
                        mm = pe.matmul(o[:, P:3 * P], q[:, P:2 * P], ks[:, b, h % 2, h // 2, :], start=False, stop=True)
                    else:
                        for t in range(TT):
                            at = (i * TT + t) * nk
                            mm = pe.matmul(ps[:, at:at + nk], q[:, t * P:(t + 1) * P], ks[:, b, h % 2, h // 2, 0:nk],
                                           start=True, stop=True)
                mm.then_inc(full, 1)

            def att_maxT(s, b):
                _, ps, full = take(banks, ("maxT", s, b), negmT_ready, s, b)
                pe.wait_ge(mparts_ready.s, mparts_ready.at(s, b))
                psb = ps[:, 0:P].bitcast(BF16)
                for t in range(TT):
                    mm = pe.transpose(psb[:, t * P:(t + 1) * P], mparts[:, b, t, :], wb("identb"))
                mm.then_inc(full, 1)

            def att_scores(s, b, c):
                nk, causal, _ = ATT[s]
                per = H // SCORE_CHUNKS[s]
                _, ps, full = take(banks, ("scores", s, b, c), probs_ready, s, b, c)
                for i in range(per):
                    h = c * per + i
                    q, k, sel = qs[:, b, h // 2, :], ks[:, b, h % 2, h // 2, :], wb("sel")[:, h:h + 1].to_broadcast([P, P])
                    if causal:
                        o = ps[:, 0:3 * P]
                        pe.matmul(o, wb("identb"), wb("mask_kq"), start=True, stop=False)
                        pe.matmul(o[:, 0:SEQ], k[:, 0:P], q, start=False, stop=False)
                        pe.matmul(o[:, SEQ:], k[:, P:], q[:, P:], start=False, stop=False)
                        pe.matmul(o[:, 0:SEQ], sel, negmT[:, b, :], start=False, stop=False)
                        mm = pe.matmul(o[:, SEQ:], sel, negmT[:, b, P:], start=False, stop=True)
                    elif nk == SEQ:
                        for t in range(TT):
                            o = ps[:, (i * TT + t) * SEQ:(i * TT + t + 1) * SEQ]
                            pe.matmul(o, k[:, t * P:(t + 1) * P], q, start=True, stop=False)
                            mm = pe.matmul(o, sel, negmT[:, b, :], start=False, stop=True)
                    else:
                        o = ps[0:CTX, i * SEQ:(i + 1) * SEQ]
                        pe.matmul(o, k[:, 0:CTX], q, start=True, stop=False)
                        mm = pe.matmul(o, sel[:, 0:CTX], negmT[:, b, :], start=False, stop=True)
                mm.then_inc(full, 1)

            def att_values(s, b, c):
                nk, causal, _ = ATT[s]
                per = H // SCORE_CHUNKS[s]
                pe.wait_ge(probs_ready.s, probs_ready.at(s, b, c))
                pr_ = probs[:, probs_keys.index((s, b, c)) % 4, :]
                if 2 * c == SCORE_CHUNKS[s]:
                    pe.wait_ge(osp_ready.s, osp_ready.at(s, b, 0))
                for i in range(per):
                    h = c * per + i
                    o = accum_t[32 * (h % 4):32 * (h % 4) + HD + 1, b, (h // 4 % 2) * SEQ:(h // 4 % 2 + 1) * SEQ]
                    if causal:
                        p_ = pr_[:, 0:3 * P]
                        pe.matmul(o, vaug[:, b, 0, h, :], p_[:, 0:SEQ], start=True, stop=False)
                        mm = pe.matmul(o[:, P:], vaug[:, b, 1, h, :], p_[:, SEQ:], start=False, stop=True)
                    elif nk == SEQ:
                        for t in range(TT):
                            mm = pe.matmul(o, vaug[:, b, t, h, :], pr_[:, (i * TT + t) * SEQ:(i * TT + t + 1) * SEQ],
                                           start=(t == 0), stop=(t == TT - 1))
                    else:
                        mm = pe.matmul(o, vaug[0:CTX, b, 0, h, :], pr_[0:CTX, i * SEQ:(i + 1) * SEQ],
                                       start=True, stop=True)
                mm.then_inc(probs_used.s, 1)

            def att_core(s, b, c):
                if c == 0:
                    pe.wait_ge(negmT_ready.s, negmT_ready.at(s, b))
                    pe.wait_ge(v_ready.s, v_ready.at(s, b))
                if c < SCORE_CHUNKS[s]:
                    att_scores(s, b, c)
                if c:
                    att_values(s, b, c - 1)

            def att_back(s, b):
                pe.wait_ge(osp_ready.s, osp_ready.at(s, b, 1))
                for t in range(TT):
                    _, ps, full = take(banks, ("back", s, b, t), otok_ready, s, b, t)
                    for g in range(4):
                        mm = pe.transpose(ps[:, g * P:(g + 1) * P], osp[:, b, g, t * P:(t + 1) * P], ident)
                    mm.then_inc(full, 1)

            def att_turn(s, b):
                if s == "a1":
                    return
                _, ps, full = take(banks, ("turn", s, b), oT_ready, s, b)
                pe.wait_ge(otok_ready.s, otok_ready.at(s, b, 1))
                for t in range(TT):
                    mm = pe.transpose(ps[:, t * P:(t + 1) * P], otok[:, b, t, :], ident)
                mm.then_inc(full, 1)

            def att_out(s, b):
                if s != "a1":
                    project_out(s, b, [oT[:, b, :]], oT_ready, (s, b), [w(f"{s}_Wo")])

            def project_out(s, b, src, ready, key, weights):
                _, ps, full = take(banks, ("out", s, b), out_taken, s, b)
                pe.wait_ge(ready.s, ready.at(*key))
                for t in range(TT):
                    for i, (lhs, rhs) in enumerate(zip(src, weights)):
                        mm = pe.matmul(ps[:, t * P:(t + 1) * P], lhs[:, t * P:(t + 1) * P], rhs,
                                       start=(i == 0), stop=(i == len(src) - 1))
                mm.then_inc(full, 1)

            def cross_project(s, b):
                pe.wait_ge(xnT_ready.s, xnT_ready.at(s, b))
                pe.wait_ge(ctxT_ready.s, ctxT_ready.at("all"))
                if s == "x1":
                    return
                _, ps, full = take(banks, ("qk", s, b), proj_ready, s, b)
                pe.matmul(ps[:, 0:SEQ], w("x0_Wq"), xnT[:, b, :], start=True, stop=True)
                pe.matmul(ps[:, SEQ:SEQ + CTX], w("x0_Wk"), ctxT[:, b, :], start=True, stop=True).then_inc(full, 1)
                _, ps, full = take(banks, ("v", s, b), vx_ready, s, b)
                pe.matmul(ps[0:CTX, 0:P], ctxT[:, b, :], w("x0_Wv"), start=True, stop=True).then_inc(full, 1)

            def cross_khat(s, b):
                if s == "x1":
                    return
                _, ps, full = take(banks, ("khat", s, b), khat_taken, s, b)
                pe.wait_ge(proj_ready.s, proj_ready.at(s, b))
                pe.matmul(ps[:, 0:CTX], w("x0_Wr"), qk[:, b, SEQ:SEQ + CTX], start=True, stop=True).then_inc(full, 1)

            def cross_scores(s, b):
                _, ps, full = take(banks, ("scores", s, b), xexp_ready if s == "x0" else sim_ready, s, b)
                if s == "x0":
                    pe.wait_ge(khat_ready.s, khat_ready.at(s, b))
                    for t in range(TT):
                        mm = pe.matmul(ps[:, t * CTX:(t + 1) * CTX], qk[:, b, t * P:(t + 1) * P], khat[:, b, :],
                                       start=True, stop=True)
                else:
                    pe.wait_ge(proj_ready.s, proj_ready.at(s, b))
                    for t in range(TT):
                        o = ps[:, t * CTX:(t + 1) * CTX]
                        pe.matmul(o, xnT[:, b, t * P:(t + 1) * P], dk[:, b, :], start=True, stop=False)
                        mm = pe.matmul(o, w("x1_w2").to_broadcast([P, P]), ctxT[:, b, :], start=False, stop=True)
                mm.then_inc(full, 1)

            def cross_turn(s, b):
                if s == "x1":
                    _, ps, full = take(banks, ("bmax", s, b), bmax_ready, s, b)
                    pe.wait_ge(xmax_ready.s, xmax_ready.at(s, b))
                    for t in range(TT):
                        mm = pe.transpose(ps[:, t * P:(t + 1) * P], small[:, b, t:t + 1].to_broadcast([P, P]), ident)
                    mm.then_inc(full, 1)
                _, ps, full = take(banks, ("turn", s, b), prT_ready, s, b)
                pe.wait_ge(xprob_ready.s, xprob_ready.at(s, b))
                for t in range(TT):
                    mm = pe.transpose(ps[0:CTX, t * P:(t + 1) * P], pr[:, b, t, :], ident)
                mm.then_inc(full, 1)

            def cross_out(s, b):
                if s == "x0":
                    _, ps, full = take(banks, ("out", s, b), out_taken, s, b)
                    pe.wait_ge(prT_ready.s, prT_ready.at(s, b))
                    for t in range(TT):
                        mm = pe.matmul(ps[:, t * P:(t + 1) * P], prT[0:CTX, b, t * P:(t + 1) * P], vx[0:CTX, b, :],
                                       start=True, stop=True)
                    mm.then_inc(full, 1)
                    return
                _, ps, full = take(banks, ("hq", s, b), hqT_ready, s, b)
                pe.wait_ge(prT_ready.s, prT_ready.at(s, b))
                pe.matmul(ps[:, 0:SEQ], ctok[:, b, :], prT[0:CTX, b, :], start=True, stop=True).then_inc(full, 1)
                _, ps, full = take(banks, ("bsum", s, b), bsum_taken, s, b)
                pe.wait_ge(bexp_ready.s, bexp_ready.at(s, b))
                for lhs, at in ((None, 0), (ones, 1)):
                    for t in range(TT):
                        mm = pe.matmul(ps[:, at:at + 1], xn[:, b, t, :] if lhs is None else ones[:, :],
                                       small[:, b, 6 + t:7 + t], start=(t == 0), stop=(t == TT - 1))
                mm.then_inc(full, 1)
                wqv = w("x1_Wqv")
                project_out(s, b, [xnT[:, b, :], hqT[:, b, :], feat3[:, b, :], feat4[:, b, :]], feats_ready,
                            (s, b), [wqv[:, i * P:(i + 1) * P] for i in range(4)])

            def ffn_logits(f, b):
                pe.wait_ge(xnT_ready.s, xnT_ready.at(f, b))
                wg = w("f3_wr") if f == "f3" else w(f"{f}_wg")
                e = wg.shape[1]
                _, ps, full = take(banks, ("logits", f, b), logits_taken, f, b)
                for t in range(TT):
                    mm = pe.matmul(ps[:, t * 16:t * 16 + e], xnT[:, b, t * P:(t + 1) * P], wg, start=True, stop=True)
                mm.then_inc(full, 1)
                if f == "f3":
                    _, ps, full = take(banks, ("wrow", f, b), counts_ready, f, b)
                    pe.wait_ge(w_tok.s, w_tok.at(f, b))
                    for t in range(TT):
                        mm = pe.transpose(ps[:, t * P:(t + 1) * P], lg[:, b * TT + t, 0:1].to_broadcast([P, P]), ident)
                    mm.then_inc(full, 1)

            def hidden(f, b, c):
                _, ps, full = take(banks, ("hid", f, b, c), u_ready if f == "f0" else hid_ready, f, b, c)
                mm = pe.matmul(ps[:, 0:SEQ], w(f"{f}_w1")[:, c * P:(c + 1) * P], xnT[:, b, :], start=True, stop=True)
                if f != "f3":
                    mm = pe.matmul(ps[:, SEQ:2 * SEQ], w(f"{f}_w3")[:, c * P:(c + 1) * P], xnT[:, b, :],
                                   start=True, stop=True)
                mm.then_inc(full, 1)

            def down(f, b, c):
                for chunk, e, p0, p1, first, last, step in pieces(f):
                    if step != c:
                        continue
                    pe.wait_ge(hid_ready.s, hid_ready.at(f, b, chunk))
                    if first and e:
                        pe.wait_ge(y_added.s, y_added.at(f, b, e - 1))
                    for t in range(TT):
                        mm = pe.matmul(accum_t[:, b, t * P:(t + 1) * P], hid[p0:p1, b, chunk % 3, t * P:(t + 1) * P],
                                       w(f"{f}_w2")[p0:p1, chunk * P:(chunk + 1) * P],
                                       start=first and t == 0, stop=last and t == TT - 1)
                    mm.then_inc(hid_used.s, 1)

            def output_biases(f, b):
                e = E0 if f == "f0" else E1 + S1
                _, ps, full = take(banks, ("gatesT", f, b), gatesT_ready, f, b)
                pe.wait_ge(gates_ready.s, gates_ready.at(f, b))
                for t in range(TT):
                    mm = pe.transpose(ps[0:16, t * P:(t + 1) * P], gates[:, b * TT + t, :], ident)
                mm.then_inc(full, 1)
                _, ps, full = take(banks, ("bias", f, b), y_biased, f, b)
                pe.wait_ge(gatesT_ready.s, gatesT_ready.at(f, b))
                for t in range(TT):
                    mm = pe.matmul(ps[:, t * P:(t + 1) * P], gatesT[0:e, b * SEQ + t * P:b * SEQ + (t + 1) * P],
                                   w(f"{f}_bt")[0:e, :], start=True, stop=True)
                mm.then_inc(full, 1)

            def ffn_chunk(f, b, c):
                if c < CHUNKS[f]:
                    hidden(f, b, c)
                if DOWN_LAG <= c < CHUNKS[f] + DOWN_LAG:
                    down(f, b, c - DOWN_LAG)
                if c == BIAS_AT and f in ("f0", "f1"):
                    output_biases(f, b)

            def offset_scores(_, b):
                pe.wait_ge(xnT_ready.s, xnT_ready.at("o", b))
                for key, names, read in (("oqk", "qk", oqk_ready), ("ov", "v", ov_ready), ("og", "g", gth_ready)):
                    _, ps, full = take(banks, (key, b), read, b)
                    for i, n in enumerate(names):
                        mm = pe.matmul(ps[:, i * SEQ:(i + 1) * SEQ], w(f"o_W{n}"), xnT[:, b, :], start=True, stop=True)
                    mm.then_inc(full, 1)
                for read in (oqk_ready, ov_ready, gth_ready):
                    pe.wait_ge(read.s, read.at(b))
                for s in range(NSLOT):
                    if s % 2 == 0:
                        _, ps, full = take(doubles, ("oqk", b, s // 2), L_ready, b, s // 2)
                    pe.wait_ge(prod_ready.s, prod_ready.at(b, s))
                    for j in range(4):
                        src = j if 4 * s + j < NOFF else j - 2
                        mm = pe.matmul(ps[32 * j:32 * j + 32, (s % 2) * SEQ:(s % 2 + 1) * SEQ], w("blk"),
                                       prod[:, s % 2, src, :], start=True, stop=True)
                    mm.then_inc(prod_used.s, 1)
                    mm = pe.matmul(ps[:, W2 + (s % 2) * SEQ:W2 + (s % 2 + 1) * SEQ], emb[:, s, :], oq,
                                   start=True, stop=True)
                    if s % 2:
                        mm.then_inc(full, 1)

            def offset_softmax(_, b):
                for t in range(TT):
                    for half in range(2):
                        _, ps, full = take(doubles, ("oturn", b, t, half), ltok_ready, b, t, half)
                        if t == 0:
                            pe.wait_ge(L_ready.s, L_ready.at(b, 2 if half == 0 else 4))
                        for i in range(5):
                            mm = pe.transpose(ps[:, i * P:(i + 1) * P], L[:, 5 * half + i, t * P:(t + 1) * P], ident)
                        mm.then_inc(full, 1)

            def offset_values(_, b):
                def sums(t, g):
                    n = 8 if g < 4 else 6
                    pe.wait_ge(pv_ready.s, pv_ready.at(b, t, g))
                    for i in range(n):
                        mm = pe.matmul(accum_t[:, b, t * P:(t + 1) * P], ident,
                                       prod[:, g_ring(b, t, g), i // 2, (i % 2) * P:(i % 2 + 1) * P],
                                       start=(g == 0 and i == 0), stop=(g == 4 and i == n - 1))
                    mm.then_inc(pv_used.s, 1)

                mine = [(t, g) for t in range(TT) for g in range(5)]
                for k, (t, g) in enumerate(mine):
                    _, ps, full = take(doubles, ("oprob", b, t, g), pv_ready, b, t, g)
                    pe.wait_ge(pexp_ready.s, pexp_ready.at(b, t, g))
                    for i in range(8 if g < 4 else 6):
                        mm = pe.transpose(ps[:, i * P:(i + 1) * P], pexp[:, g_ring(b, t, g), i, :], ident)
                    mm.then_inc(full, 1)
                    if k:
                        sums(*mine[k - 1])
                sums(*mine[-1])
                project_out("o", b, [oacc], og_ready, (b,), [w("o_Wo")])

            emit = {"turn_norm": norm, "project": att_project, "max": att_max, "turn_max": att_maxT, "core": att_core,
                    "back": att_back, "turn": att_turn, "out": att_out, "cross_project": cross_project,
                    "cross_khat": cross_khat, "cross_scores": cross_scores, "cross_turn": cross_turn,
                    "cross_out": cross_out, "logits": ffn_logits, "chunk": ffn_chunk, "offset_scores": offset_scores, "offset_softmax": offset_softmax,
                    "offset_values": offset_values}
            with pe.Fori(0, iters):
                context()
                for step, *key in plan:
                    if step in emit:
                        emit[step](*key)
                end_of_iteration(pe)


        @block.scalar
        def _(act):
            def see(r, *key):
                slot, n = r.at(*key)
                act.wait_ge(r.full[slot], n)
                return r.tile[:, slot, :]

            def copy(dst, src, done, **kw):
                act.activation(dst, src, ACT.Copy, **kw).then_inc(done.s, 1)

            def rms(s, b):
                act.wait_ge(xn_mid.s, xn_mid.at(s, b))
                for t in range(TT):
                    ins = act.activation(junk[:, b, t * P:(t + 1) * P], xn[:, b, t, :], ACT.Square,
                                         accum_out=sumsq[:, b * TT + t:b * TT + t + 1])
                ins.then_inc(squares.s, 1)

            def norm(s, b):
                act.wait_ge(group_loaded[GROUP_OF[s]], 16 + 16 * (GROUP_OF[s] == 0))
                ps = see(banks, "norm", s, b)
                if s == "f0":
                    act.activation(xnT[:, b, :], ps[:, 0:SEQ], ACT.Copy, scale=w("f0_ns")).then_inc(xnT_ready.s, 1)
                else:
                    copy(xnT[:, b, :], ps[:, 0:SEQ], xnT_ready)

            def att_split(s, b):
                n = SEQ + ATT[s][0]
                act.wait_ge(qk_ready.s, qk_ready.at(s, b))
                copy(parts[:, b, 0, 0:n], qk[:, b, 0:n], part0)
                act.wait_ge(res_ready.s, res_ready.at(s, b))
                copy(parts[:, b, 1, 0:n], res[:, b, 0:n], part1)

            def att_maxT(s, b):
                copy(negmT[:, b, :], see(banks, "maxT", s, b)[:, 0:P].bitcast(BF16), negmT_ready)

            def att_core(s, b, c):
                nk, causal, _ = ATT[s]
                if c < SCORE_CHUNKS[s]:
                    ps = see(banks, "scores", s, b, c)
                    i = probs_keys.index((s, b, c))
                    if i >= 4:
                        act.wait_ge(probs_used.s, probs_used.at(*probs_keys[i - 4]))
                    n, width = min(nk, P), 3 * P if causal else 512
                    act.activation(probs[0:n, i % 4, 0:width], ps[0:n, 0:width], ACT.Exp,
                                   scale=HD ** -0.5 if s == "a3" else 1.0).then_inc(probs_ready.s, 1)
                if c and 2 * c % SCORE_CHUNKS[s] == 0:
                    act.wait_ge(probs_used.s, probs_used.at(s, b, c - 1))
                    g = 2 * (2 * c // SCORE_CHUNKS[s] - 1)
                    copy(osp[:, b, g:g + 2, :].rearrange("p g t -> p (g t)"), accum_t[:, b, :], osp_ready)

            def att_turn(s, b):
                if s != "a1":
                    copy(oT[:, b, :], see(banks, "turn", s, b)[:, 0:SEQ], oT_ready)

            def cross_khat(s, b):
                if s == "x0":
                    act.wait_ge(khat_arg.s, khat_arg.at(s, b))
                    act.activation(khat[:, b, :], zc[:, b, :], ACT.Sin, bias=halfpi[:, :]).then_inc(khat_ready.s, 1)

            def cross_scores(s, b):
                act.wait_ge(xmax_ready.s, xmax_ready.at(s, b))
                src = see(banks, "scores", s, b) if s == "x0" else sim[:, b, :, :].rearrange("p t k -> p (t k)")
                for t in range(TT):
                    ins = act.activation(pr[:, b, t, :], src[:, t * CTX:(t + 1) * CTX], ACT.Exp,
                                         bias=small[:, b, 2 + t:3 + t], accum_out=small[:, b, 4 + t:5 + t])
                ins.then_inc(xexp_ready.s, 1)

            def cross_turn(s, b):
                if s == "x1":
                    act.wait_ge(bmax_ready.s, bmax_ready.at(s, b))
                    act.activation(small[:, b, 6:8], small[:, b, 0:2], ACT.Exp,
                                   bias=small[:, b, 8:9]).then_inc(bexp_ready.s, 1)
                copy(prT[0:CTX, b, :], see(banks, "turn", s, b)[0:CTX, 0:SEQ], prT_ready)

            def cross_out(s, b):
                if s == "x1":
                    copy(hqT[:, b, :], see(banks, "hq", s, b)[:, 0:SEQ], hqT_ready)

            def ffn_logits(f, b):
                if f in EXPERTS:
                    act.wait_ge(logit_arg.s, logit_arg.at(f, b))
                    mine, e = slice(b * TT, (b + 1) * TT), EXPERTS[f][0]
                    act.activation(ex[:, mine, 0:e], (em if f == "f0" else lg)[:, mine, 0:e],
                                   ACT.Exp).then_inc(logit_exp.s, 1)

            def ffn_chunk(f, b, c):
                if c >= CHUNKS[f]:
                    return
                if f == "f3":
                    ps = see(banks, "hid", f, b, c)
                    if c >= 3:
                        act.wait_ge(hid_used.s, hid_used.at(f, b, c - 3, 0))
                    act.activation(hid[:, b, c % 3, :], ps[:, 0:SEQ], ACT.Gelu,
                                   bias=w("f3_b1")[:, c:c + 1]).then_inc(hid_ready.s, 1)
                elif f == "f0":
                    act.wait_ge(a_ready.s, a_ready.at(f, b, c))
                    if c >= 2:
                        act.wait_ge(t_ready.s, t_ready.at(f, b, c - 2))
                    act.activation(sg[:, b, c % 2, :], ab[:, b, c % 2, :], ACT.Tanh,
                                   scale=0.851).then_inc(th_ready.s, 1)
                else:
                    ps = see(banks, "hid", f, b, c)
                    if c >= 2:
                        act.wait_ge(u_ready.s, u_ready.at(f, b, c - 2))
                    bias = f1_b1h[:, c:c + 1] if f == "f1" else 0.0
                    act.activation(sg[:, b, c % 2, :], ps[:, 0:SEQ], ACT.Tanh, scale=0.5,
                                   bias=bias).then_inc(th_ready.s, 1)
                if f != "f3":
                    act.wait_ge(th_ready.s, th_ready.at(f, b, c))
                    act.activation(sg[:, b, c % 2, :], sg[:, b, c % 2, :], ACT.Copy, bias=1.0).then_inc(sg_ready.s, 1)
                if c == BIAS_AT and f in ("f0", "f1"):
                    copy(gatesT[:, b * SEQ:(b + 1) * SEQ], see(banks, "gatesT", f, b)[0:16, 0:SEQ],
                         gatesT_ready, scale=2.0)

            def offset_scores(_, b):
                ps = see(banks, "og", b)
                act.activation(xn[:, b, :, :].rearrange("p t d -> p (t d)"), ps[:, 0:SEQ], ACT.Tanh, scale=0.5, bias=o_bgh[:, :]).then_inc(gth_ready.s, 1)
                for i in range(NSLOT // 2):
                    ps = see(doubles, "oqk", b, i)
                    if b or i >= 2:
                        k = b * (NSLOT // 2) + i - 2
                        act.wait_ge(L_ready.s, k + 1)
                    copy(qks[:, i % 2, :], ps[:, 0:W2], qks_ready)

            def offset_softmax(_, b):
                for t in range(TT):
                    act.wait_ge(lmax_ready.s, lmax_ready.at(b, t))
                    act.activation(ltok[:, t, :, :], ltok[:, t, :, :], ACT.Exp).then_inc(lexp_ready.s, 1)

            def offset_values(_, b):
                for t in range(TT):
                    act.wait_ge(lprob_ready.s, lprob_ready.at(b, t))
                    for g in range(5):
                        n = 8 if g < 4 else 6
                        i = groups.index((b, t, g))
                        if i % 10 >= 2:
                            prev = groups[i - 2]
                            slot, k = doubles.at("oprob", *prev)
                            act.wait_ge(doubles.full[slot], k)
                        src = ltok[:, t, 8 * g:8 * g + n, :].unsqueeze(3).to_broadcast([P, n, H, HD])
                        dst = pexp[:, g_ring(b, t, g), 0:n, :].rearrange("p n (h d) -> p n h d", h=H)
                        copy(dst, src, pexp_ready)

            emit = {"rms": rms, "turn_norm": norm, "split": att_split, "turn_max": att_maxT, "core": att_core, "turn": att_turn,
                    "cross_khat": cross_khat, "cross_scores": cross_scores, "cross_turn": cross_turn,
                    "cross_out": cross_out, "logits": ffn_logits, "chunk": ffn_chunk, "offset_scores": offset_scores, "offset_softmax": offset_softmax,
                    "offset_values": offset_values}
            act.wait_ge(inputs_in.s, inputs_in.at("all"))
            for g, (a, z) in enumerate(GROUP):
                if g:
                    act.dma_start(wt[:, a:z], packed[:, a:z]).then_inc(group_loaded[g], 16)
            with act.Fori(0, iters):
                copy(ctxT[:, :, :].rearrange("p b k -> p (b k)"), see(banks, "ctx")[:, 0:PAIR * CTX], ctxT_ready)
                for step, *key in plan:
                    if step in emit:
                        emit[step](*key)
                end_of_iteration(act)

        @block.vector
        def _(dve):
            steps = Steps(dve, dve_done)
            link = steps.link

            def see(r, *key):
                slot, n = r.at(*key)
                dve.wait_ge(r.full[slot], n)
                return r.tile[:, slot, :]

            def after(sig, *key):
                dve.wait_ge(sig.s, sig.at(*key))

            def pre(ins, n=[0]):
                n[0] += 1
                ins.then_inc(pre_step, 1)
                dve.wait_ge(pre_step, n[0])

            for tile, value in ((halfpi, float(np.pi / 2)), (ones, 1.0), (vaug, 1.0), (gates, 0.0),
                                (mparts, 0.0), (qs, 0.0), (ks, 0.0), (ex, 0.0)):
                dve.memset(tile[:], value).then_inc(const_set, 1)
            dve.wait_ge(group_loaded[0], 32)
            dve.wait_ge(pre_mm, 1)
            a = COLS["a0_Wq"][0]
            pre(dve.scalar_tensor_tensor(out=wt[:, a:a + 3 * P], in0=banks_t[:, 0, 0:3 * P], scalar=2.0,
                                         in1=wt[:, a:a + 3 * P], op0=ALU.mult, op1=ALU.add))
            pre(dve.scalar_tensor_tensor(out=w("a0_Wo"), in0=banks_t[:, 1, 0:P], scalar=2.0, in1=w("a0_Wo"),
                                         op0=ALU.mult, op1=ALU.add))
            dve.memset(accum_t[:], 0.0).then_inc(const_set, 1)
            dve.wait_ge(const_set, 9)
            dve.memset(banks_t[:], 0.0).then_inc(pre_fold, 1)

            def prepare(s):
                dve.wait_ge(group_loaded[GROUP_OF[s]], 16 + 16 * (GROUP_OF[s] == 0))
                if s == "f0":
                    link(dve.tensor_scalar(f0_b3p[:, :], w("f0_b3"), 1.0, None, ALU.add))
                if s == "f1":
                    link(dve.tensor_scalar(f1_b1h[:, :], w("f1_b1"), 0.5, None, ALU.mult))
                if s == "o":
                    for j in range(4):
                        src = w("o_emb").rearrange("p (s j) -> p s j", j=4)[:, :, j:j + 1].to_broadcast([P, NSLOT, 32])
                        hm = w("headmask").unsqueeze(1).to_broadcast([P, NSLOT, 32])
                        dve.tensor_tensor(emb[:, :, 32 * j:32 * j + 32], src, hm, ALU.mult)
                    dve.tensor_scalar(gain[:, :], w("o_gain"), 0.5, None, ALU.mult)
                    link(dve.tensor_scalar(o_bgh[:, :], w("o_bg"), 0.5, None, ALU.mult))

            def stats(s, b):
                if s == stages[0] and b == 0:
                    after(inputs_in, "all")
                if b == 0:
                    prepare(s)
                mine = slice(b * TT, (b + 1) * TT)
                for t in range(TT):
                    ins = dve.bn_stats(bn[:, b, t, :], x[:, b, t, :])
                link(ins)
                for t in range(TT):
                    ins = dve.bn_aggr(mv[:, b * TT + t, :], bn[:, b, t, :])
                link(ins)
                dve.tensor_scalar(var[:, mine], mv[:, mine, 1], LN_EPS, None, ALU.add).then_inc(v_stats.s, 1)

            def norm(s, b):
                after(rstd_ready, "stats", s, b)
                for t in range(TT):
                    i = b * TT + t
                    ins = dve.tensor_scalar(xn[:, b, t, :], x[:, b, t, :], mv[:, i, 0:1], rstd[:, i:i + 1],
                                            ALU.subtract, ALU.mult)
                ins.then_inc((xn_mid if s == "f0" else xn_ready).s, 1)

            def rms(s, b):
                after(xn_mid, s, b)
                link(dve.tensor_tensor(x[:, b, :, :], x[:, b, :, :], xn[:, b, :, :], ALU.add))
                after(squares, s, b)
                mine = slice(b * TT, (b + 1) * TT)
                dve.tensor_scalar(var[:, mine], sumsq[:, mine], 1.0 / P, LN_EPS, ALU.mult, ALU.add).then_inc(v_stats.s, 1)

            def rms_norm(s, b):
                after(rstd_ready, "rms", s, b)
                for t in range(TT):
                    i = b * TT + t
                    ins = dve.tensor_scalar(xn[:, b, t, :], xn[:, b, t, :], rstd[:, i:i + 1], None, ALU.mult)
                ins.then_inc(xn_ready.s, 1)

            def add_to_x(s, b, src, bias=None):
                dve.tensor_tensor(x[:, b, :, :], x[:, b, :, :], src, ALU.add).then_inc(out_taken.s, 1)
                after(out_taken, s, b)
                if bias is not None:
                    link(dve.tensor_tensor(x[:, b, :, :], x[:, b, :, :],
                                           w(bias).unsqueeze(1).to_broadcast([P, TT, P]), ALU.add))

            def att_scale(s, b):
                nk, _, scale = ATT[s]
                if s == "a3":
                    tables = w("rope").rearrange("p (n t) -> p n t", n=2)
                    for i, n in enumerate("qk"):
                        ps = see(banks, n, s, b)
                        o = qk[:, b, i * SEQ:(i + 1) * SEQ]
                        dve.scalar_tensor_tensor(out=o, in0=ps[:, 0:SEQ], scalar=w(f"a3_b{n}"), in1=tables[:, 0, :],
                                                 op0=ALU.add, op1=ALU.mult)
                        ins = dve.scalar_tensor_tensor(out=rt[:, b, i, :], in0=ps[:, SEQ:], scalar=w(f"a3_b{n}s"),
                                                       in1=tables[:, 1, :], op0=ALU.add, op1=ALU.mult)
                        link(ins)
                        ins = dve.tensor_tensor(o, o, rt[:, b, i, :], ALU.add)
                        if n == "q":
                            ins.then_inc(q_taken.s, 1)
                        else:
                            ins.then_inc(qk_ready.s, 1)
                else:
                    ps = see(banks, "qk", s, b)
                    q, k = qk[:, b, 0:SEQ], qk[:, b, SEQ:SEQ + nk]
                    if s in ("a0", "a2"):
                        dve.tensor_scalar(q, ps[:, 0:SEQ], w(f"{s}_bq"), scale, ALU.add, ALU.mult)
                    else:
                        dve.tensor_scalar(q, ps[:, 0:SEQ], scale, None, ALU.mult)
                    if s == "a2":
                        after(mask_ready, "all")
                        dve.scalar_tensor_tensor(out=k, in0=ps[:, SEQ:SEQ + nk], scalar=w("a2_bk"),
                                                 in1=maskf[:, b, :], op0=ALU.add,
                                                 op1=ALU.mult).then_inc(qk_ready.s, 1)
                    elif s == "a0":
                        dve.tensor_scalar(k, ps[:, SEQ:SEQ + nk], w("a0_bk"), None, ALU.add).then_inc(qk_ready.s, 1)
                    else:
                        dve.tensor_copy(k, ps[:, SEQ:SEQ + nk]).then_inc(qk_ready.s, 1)
                ps = see(banks, "v", s, b)
                n, tiles = min(nk, P), max(nk // P, 1)
                o = vaug[0:n, b, 0:tiles, :, 0:HD]
                src = ps[0:n, 0:tiles * P].rearrange("p (t h d) -> p t h d", t=tiles, h=H)
                if s in ("a0", "a2", "a3"):
                    bias = w(f"{s}_bv")[0:n, :].rearrange("p (h d) -> p h d", h=H)
                    for t in range(tiles):
                        ins = dve.tensor_tensor(o[:, t], src[:, t], bias, ALU.add)
                else:
                    for t in range(tiles):
                        ins = dve.tensor_copy(o[:, t], src[:, t])
                ins.then_inc(v_ready.s, 1)

            def att_split(s, b):
                n = SEQ + ATT[s][0]
                after(qk_ready, s, b)
                after(part0, s, b)
                dve.tensor_tensor(res[:, b, 0:n], qk[:, b, 0:n], parts[:, b, 0, 0:n],
                                  ALU.subtract).then_inc(res_ready.s, 1)

                after(res_ready, s, b)
                after(part1, s, b)
                dve.tensor_tensor(parts[:, b, 2, 0:n], res[:, b, 0:n], parts[:, b, 1, 0:n],
                                  ALU.subtract).then_inc(parts_ready.s, 1)

            def att_max(s, b, c):
                nk, causal, _ = ATT[s]
                per = H // MAX_CHUNKS[s]
                ps = see(banks, "max", s, b, c)
                heads = slice(c * per, (c + 1) * per)
                if causal:
                    dve.tensor_reduce(negm[:, b, 0, heads], ps[:, 0:P], AX.X, ALU.max, negate=True)
                    ins = dve.tensor_reduce(negm[:, b, 1, heads], ps[:, P:3 * P], AX.X, ALU.max, negate=True)
                else:
                    v = ps.rearrange("p (h t k) -> p t h k", t=TT, k=nk)
                    ins = dve.tensor_reduce(negm[:, b, :, heads], v, AX.X, ALU.max, negate=True)
                ins.then_inc(max_taken.s, 1)

            def att_maxT(s, b):
                after(max_taken, s, b, MAX_CHUNKS[s] - 1)
                link(dve.tensor_copy(mparts[:, b, :, 0:H], negm[:, b, :, :]))
                link(dve.tensor_tensor(mres[:, b, :, :], negm[:, b, :, :], mparts[:, b, :, 0:H], ALU.subtract))
                link(dve.tensor_copy(mparts[:, b, :, 32:32 + H], mres[:, b, :, :]))
                dve.tensor_tensor(mparts[:, b, :, 64:64 + H], mres[:, b, :, :], mparts[:, b, :, 32:32 + H],
                                  ALU.subtract).then_inc(mparts_ready.s, 1)

            def att_back(s, b):
                for t in range(TT):
                    v = see(banks, "back", s, b, t).rearrange("p (h r) -> p h r", r=32)
                    link(dve.reciprocal(rinv[:, b, t, :], v[:, :, HD]))
                    o = otok[:, b, t, :].rearrange("p (h d) -> p h d", h=H)
                    dve.tensor_tensor(o, v[:, :, 0:HD], rinv[:, b, t, :].unsqueeze(2).to_broadcast([P, H, HD]),
                                      ALU.mult).then_inc(otok_ready.s, 1)
                if s == "a1":
                    after(otok_ready, s, b, 1)
                    add_to_x(s, b, otok[:, b, :, :])

            def att_out(s, b):
                if s != "a1":
                    tokens_out(s, b, f"{s}_bo")

            def tokens_out(s, b, bias):
                add_to_x(s, b, see(banks, "out", s, b)[:, 0:SEQ].rearrange("p (t d) -> p t d", t=TT), bias)

            def cross_project(s, b):
                if s == "x1":
                    after(ctxT_ready, "all")
                    dve.tensor_scalar(dk[:, b, :], ctxT[:, b, :], w("x1_w3"), w("x1_w1"), ALU.mult,
                                      ALU.add).then_inc(proj_ready.s, 1)
                    return
                ps = see(banks, "qk", s, b)
                dve.tensor_scalar(qk[:, b, 0:SEQ], ps[:, 0:SEQ], w("x0_bq"), None, ALU.add)
                dve.tensor_scalar(qk[:, b, SEQ:SEQ + CTX], ps[:, SEQ:SEQ + CTX], w("x0_bk"), None,
                                  ALU.add).then_inc(proj_ready.s, 1)
                ps = see(banks, "v", s, b)
                dve.tensor_tensor(vx[0:CTX, b, :], ps[0:CTX, 0:P], w("x0_bv")[0:CTX, :], ALU.add).then_inc(vx_ready.s, 1)

            def cross_khat(s, b):
                if s == "x1":
                    return
                ps = see(banks, "khat", s, b)
                dve.tensor_scalar(zc[:, b, :], ps[:, 0:CTX], w("x0_br"), None, ALU.add).then_inc(khat_taken.s, 1)
                after(khat_taken, s, b)
                link(dve.tensor_scalar(zn[:, b, :], zc[:, b, :], float(1 / (2 * np.pi)), MAGIC, ALU.mult, ALU.add))
                link(dve.tensor_scalar(zn[:, b, :], zn[:, b, :], MAGIC, None, ALU.subtract))
                for part_ in TWO_PI:
                    link(dve.scalar_tensor_tensor(out=zc[:, b, :], in0=zn[:, b, :], scalar=-part_, in1=zc[:, b, :],
                                                  op0=ALU.mult, op1=ALU.add))
                dve.scalar_tensor_tensor(out=zc[:, b, :], in0=zc[:, b, :], scalar=-1.0, in1=zc[:, b, :], op0=ALU.mult,
                                         op1=ALU.min).then_inc(khat_arg.s, 1)

            def cross_scores(s, b):
                if s == "x0":
                    ps = see(banks, "scores", s, b)[:, 0:TT * CTX].rearrange("p (t k) -> p t k", t=TT)
                    dve.tensor_reduce(small[:, b, 2:4], ps, AX.X, ALU.max, negate=True).then_inc(xmax_ready.s, 1)
                    return
                ps = see(banks, "scores", s, b)
                dve.tensor_scalar(sim[:, b, :, :].rearrange("p t k -> p (t k)"), ps[:, 0:TT * CTX], w("x1_bs"), None,
                                  ALU.add).then_inc(sim_ready.s, 1)
                after(sim_ready, s, b)
                link(dve.tensor_reduce(small[:, b, 0:2], sim[:, b, :, :], AX.X, ALU.max))
                dve.tensor_scalar(small[:, b, 2:4], small[:, b, 0:2], -1.0, None, ALU.mult).then_inc(xmax_ready.s, 1)

            def cross_turn(s, b):
                if s == "x1":
                    ps = see(banks, "bmax", s, b)
                    dve.tensor_reduce(small[:, b, 8:9], ps[:, 0:SEQ], AX.X, ALU.max, negate=True).then_inc(bmax_ready.s, 1)
                after(xexp_ready, s, b)
                link(dve.reciprocal(small[:, b, 10:12], small[:, b, 4:6]))
                dve.tensor_tensor(pr[:, b, :, :], pr[:, b, :, :],
                                  small[:, b, 10:12].unsqueeze(2).to_broadcast([P, TT, CTX]),
                                  ALU.mult).then_inc(xprob_ready.s, 1)

            def cross_out(s, b):
                if s == "x0":
                    tokens_out(s, b, None)
                    return
                after(hqT_ready, s, b)
                dve.tensor_tensor(feat3[:, b, :], xnT[:, b, :], hqT[:, b, :], ALU.mult)
                ps = see(banks, "bsum", s, b)
                link(dve.reciprocal(small[:, b, 12:13], ps[:, 1:2]))
                dve.tensor_tensor(small[:, b, 13:14], ps[:, 0:1], small[:, b, 12:13], ALU.mult).then_inc(bsum_taken.s, 1)
                after(bsum_taken, s, b)
                dve.tensor_scalar(feat4[:, b, :], xnT[:, b, :], small[:, b, 13:14], None,
                                  ALU.mult).then_inc(feats_ready.s, 1)
                tokens_out(s, b, "x1_b")

            def route_logits(f, b):
                e = EXPERTS[f][0]
                ps = see(banks, "logits", f, b)[:, 0:16 * TT].rearrange("p (t e) -> p t e", t=TT)[:, :, 0:e]
                if f == "f2":
                    dve.tensor_copy(lg[:, b * TT:(b + 1) * TT, 0:e], ps).then_inc(logits_taken.s, 1)
                else:
                    dve.tensor_tensor(lg[:, b * TT:(b + 1) * TT, 0:e], ps, w(f"{f}_bg").unsqueeze(1).to_broadcast([P, TT, e]),
                                      ALU.add).then_inc(logits_taken.s, 1)
                after(logits_taken, f, b)
                if f == "f0":
                    for t in range(TT):
                        ins = dve.max(top[:, b * TT + t, :], lg[:, b * TT + t, :])
                    link(ins)
                    dve.tensor_tensor(em[:, b * TT:(b + 1) * TT, :], lg[:, b * TT:(b + 1) * TT, :], top[:, b * TT:(b + 1) * TT, 0:1].to_broadcast([P, TT, 16]),
                                      ALU.subtract).then_inc(logit_arg.s, 1)
                else:
                    link(dve.tensor_reduce(rsum[:, b * TT:(b + 1) * TT, 0:1], lg[:, b * TT:(b + 1) * TT, 0:e], AX.X, ALU.max))
                    dve.tensor_tensor(lg[:, b * TT:(b + 1) * TT, 0:e], lg[:, b * TT:(b + 1) * TT, 0:e], rsum[:, b * TT:(b + 1) * TT, 0:1].to_broadcast([P, TT, e]),
                                      ALU.subtract).then_inc(logit_arg.s, 1)
                    if f == "f2":
                        link(dve.memset(ex[:, b * TT:(b + 1) * TT, e:8], 0.0))

            def route_choice(f, b):
                seen = 16 if f == "f0" else 8
                chosen_from = lg if f == "f0" else ex
                if f != "f0":
                    after(logit_exp, f, b)
                    for t in range(TT):
                        ins = dve.max(top[:, b * TT + t, :], ex[:, b * TT + t, 0:8])
                    link(ins)
                for t in range(TT):
                    ins = dve.max_index(topi[:, b * TT + t, :], top[:, b * TT + t, :], chosen_from[:, b * TT + t, 0:seen])
                link(ins)
                link(dve.tensor_copy(topf[:, b * TT:(b + 1) * TT, :], topi[:, b * TT:(b + 1) * TT, :]))

            def route_weights(f, b):
                k, seen = EXPERTS[f][1], 16 if f == "f0" else 8
                o = hot[:, b * TT:(b + 1) * TT, 0:k, 0:seen]
                link(dve.tensor_tensor(o, topf[:, b * TT:(b + 1) * TT, 0:k].unsqueeze(3).to_broadcast([P, TT, k, seen]),
                                       w("sixteen")[:, 0:seen].unsqueeze(1).unsqueeze(1).to_broadcast([P, TT, k, seen]),
                                       ALU.is_equal))
                after(logit_exp, f, b)
                link(dve.tensor_reduce(em[:, b * TT:(b + 1) * TT, 0:seen], o.rearrange("p t k e -> p t e k"), AX.X, ALU.add))
                link(dve.tensor_tensor(em[:, b * TT:(b + 1) * TT, 0:seen], em[:, b * TT:(b + 1) * TT, 0:seen], ex[:, b * TT:(b + 1) * TT, 0:seen], ALU.mult))

            def route_gates(f, b):
                seen = 16 if f == "f0" else 8
                over = ex if f == "f1" else em
                link(dve.tensor_reduce(rsum[:, b * TT:(b + 1) * TT, 0:1], over[:, b * TT:(b + 1) * TT, 0:seen], AX.X, ALU.add))
                link(dve.reciprocal(rsum[:, b * TT:(b + 1) * TT, 1:2], rsum[:, b * TT:(b + 1) * TT, 0:1]))
                link(dve.tensor_scalar(rsum[:, b * TT:(b + 1) * TT, 1:2], rsum[:, b * TT:(b + 1) * TT, 1:2], 0.5, None,
                                       ALU.mult))
                ins = dve.tensor_tensor(gates[:, b * TT:(b + 1) * TT, 0:seen], em[:, b * TT:(b + 1) * TT, 0:seen],
                                        rsum[:, b * TT:(b + 1) * TT, 1:2].to_broadcast([P, TT, seen]), ALU.mult)
                if f == "f1":
                    link(ins)
                    ins = dve.memset(gates[:, b * TT:(b + 1) * TT, E1:E1 + S1], 0.5 / S1)
                ins.then_inc(gates_ready.s, 1)
                after(gates_ready, f, b)

            def ffn_logits(f, b):
                if f in EXPERTS:
                    route_logits(f, b)
                    return
                ps = see(banks, "logits", f, b)[:, 0:16 * TT].rearrange("p (t e) -> p t e", t=TT)
                mine = slice(b * TT, (b + 1) * TT)
                dve.tensor_tensor(lg[:, mine, 0:1], ps[:, :, 0:1], w("f3_br").unsqueeze(1).to_broadcast([P, TT, 1]),
                                  ALU.add).then_inc(logits_taken.s, 1)
                after(logits_taken, f, b)
                dve.tensor_copy(topf[:, mine, 0:1], lg[:, mine, 0:1]).then_inc(w_tok.s, 1)
                rows = see(banks, "wrow", f, b)
                for t in range(TT):
                    ins = dve.tensor_scalar(cmpj[:, b, :], rows[:, 0:SEQ], lg[:, b * TT + t, 0:1], 0.0, ALU.is_ge, ALU.add,
                                            accum_out=sel3[:, b, t, 0:1])
                    if t < TT - 1:
                        link(ins)
                ins.then_inc(counts_ready.s, 1)
                after(counts_ready, f, b)
                dve.tensor_scalar(sel3[:, b, :, 1:2], sel3[:, b, :, 0:1], SEQ / 2 - 0.5, None, ALU.is_lt)
                link(dve.tensor_scalar(sel3[:, b, :, 2:3], sel3[:, b, :, 0:1], SEQ / 2 - 0.5, None, ALU.is_gt))
                link(dve.tensor_tensor(blend[:, b, 1, :, :], xn[:, b, :, :], sel3[:, b, :, 2:3].to_broadcast([P, TT, P]),
                                       ALU.mult))
                link(dve.tensor_tensor(x[:, b, :, :], x[:, b, :, :], blend[:, b, 1, :, :], ALU.add))

            def select(f, b):
                after(hid_used, f, b, CH3 - 1, 0)
                link(dve.tensor_tensor(blend[:, b, 0, :, :], accum_t[:, b, 0:SEQ].rearrange("p (t d) -> p t d", t=TT),
                                       w("f3_b2").unsqueeze(1).to_broadcast([P, TT, P]), ALU.add))
                link(dve.tensor_tensor(blend[:, b, 0, :, :], blend[:, b, 0, :, :],
                                       sel3[:, b, :, 1:2].to_broadcast([P, TT, P]), ALU.mult))
                link(dve.tensor_tensor(x[:, b, :, :], x[:, b, :, :], blend[:, b, 0, :, :], ALU.add))

            def first_half(f, b, c):
                ps = see(banks, "hid", f, b, c)
                if c >= 2:
                    after(t_ready, f, b, c - 2)
                dve.tensor_scalar(ab[:, b, c % 2, :], ps[:, 0:SEQ], w("f0_b1")[:, c:c + 1], 7.0, ALU.add,
                                  ALU.min).then_inc(a_ready.s, 1)
                if c >= 2:
                    after(hid_ready, f, b, c - 2)
                dve.tensor_scalar(ub[:, b, c % 2, :], ps[:, SEQ:2 * SEQ], f0_b3p[:, c:c + 1], 8.0, ALU.add,
                                  ALU.min).then_inc(u_ready.s, 1)

            def clipped(f, b, c):
                after(t_ready, f, b, c)
                after(u_ready, f, b, c)
                if c >= 3:
                    after(hid_used, f, b, c - 3, last_use(f, c - 3))
                dve.scalar_tensor_tensor(out=hid[:, b, c % 3, :], in0=ub[:, b, c % 2, :], scalar=-6.0,
                                         in1=vb[:, b, c % 2, :], op0=ALU.max, op1=ALU.mult).then_inc(hid_ready.s, 1)

            def swish(f, b, c):
                ps = see(banks, "hid", f, b, c)
                after(sg_ready, f, b, c)
                if c >= 2:
                    after(hid_ready, f, b, c - 2)
                bias = w("f1_b1")[:, c:c + 1] if f == "f1" else 0.0
                dve.scalar_tensor_tensor(out=vb[:, b, c % 2, :], in0=ps[:, 0:SEQ], scalar=bias, in1=sg[:, b, c % 2, :],
                                         op0=ALU.add, op1=ALU.mult).then_inc(u_ready.s, 1)

            def times_second(f, b, c):
                ps = see(banks, "hid", f, b, c)
                after(u_ready, f, b, c)
                if c >= 3:
                    after(hid_used, f, b, c - 3, last_use(f, c - 3))
                bias = w("f1_b3")[:, c:c + 1] if f == "f1" else 0.0
                dve.scalar_tensor_tensor(out=hid[:, b, c % 3, :], in0=ps[:, SEQ:2 * SEQ], scalar=bias,
                                         in1=vb[:, b, c % 2, :], op0=ALU.add, op1=ALU.mult).then_inc(hid_ready.s, 1)

            def add_output(f, b, e):
                after(hid_used, f, b, ends[f, e], e)
                if e:
                    after(y_added, f, b, e - 1)
                for t in range(TT):
                    xt = x[:, b, t, :]
                    ins = dve.scalar_tensor_tensor(out=xt, in0=accum_t[:, b, t * P:(t + 1) * P],
                                                   scalar=gates[:, b * TT + t, e:e + 1], in1=xt, op0=ALU.mult, op1=ALU.add)
                ins.then_inc(y_added.s, 1)

            route = {0: route_choice, 1: route_weights, 2: route_gates}

            def ffn_chunk(f, b, c):
                if f == "f3":
                    return
                ended = [e for g, e in ends if g == f and ends[g, e] == c - DOWN_LAG - 1]
                for e in ended:
                    add_output(f, b, e)
                if f == "f0" and c < CHUNKS[f]:
                    first_half(f, b, c)
                elif f != "f0" and 1 <= c <= CHUNKS[f]:
                    swish(f, b, c - 1)
                if c in route:
                    route[c](f, b)
                if f == "f0" and 1 <= c <= CHUNKS[f]:
                    clipped(f, b, c - 1)
                elif f != "f0" and 1 <= c <= CHUNKS[f]:
                    times_second(f, b, c - 1)
                if c == BIAS_AT + 1 and f in ("f0", "f1"):
                    ps = see(banks, "bias", f, b)
                    after(y_added, f, b, max(e for g, e in ends if g == f and ends[g, e] < c - DOWN_LAG))
                    xv = x[:, b, :, :].rearrange("p t d -> p (t d)")
                    dve.tensor_tensor(xv, xv, ps[:, 0:SEQ], ALU.add).then_inc(y_biased.s, 1)
                    after(y_biased, f, b)
                if c == CHUNKS[f] + DOWN_LAG:
                    after(y_added, f, b, max(e for g, e in ends if g == f))

            def offset_scores(_, b):
                ps = see(banks, "oqk", b)
                dve.memset(kpad[:, 0:PAD], 0.0)
                dve.memset(vpad[:, 0:PAD], 0.0)
                dve.tensor_scalar(oq, ps[:, 0:SEQ], w("o_bq"), None, ALU.add)
                dve.tensor_scalar(kpad[:, PAD:], ps[:, SEQ:], w("o_bk"), None, ALU.add).then_inc(oqk_ready.s, 1)
                ps = see(banks, "ov", b)
                dve.tensor_scalar(vpad[:, PAD:], ps[:, 0:SEQ], w("o_bv"), None, ALU.add).then_inc(ov_ready.s, 1)
                after(oqk_ready, b)

                def logits(i):
                    after(qks_ready, b, i)
                    ps = see(doubles, "oqk", b, i)
                    o = L[:, 2 * i:2 * i + 2, :].rearrange("p s t -> p (s t)")
                    dve.scalar_tensor_tensor(out=o, in0=ps[:, W2:], scalar=1.0, in1=qks[:, i % 2, :], op0=ALU.add,
                                             op1=ALU.mult).then_inc(L_ready.s, 1)

                for s in range(NSLOT):
                    if s >= 2:
                        after(prod_used, b, s - 2)
                    runs = offset_runs(4 * s, 4)
                    for i0, n, step in runs:
                        j = i0 - 4 * s
                        ins = dve.tensor_tensor(prod[:, s % 2, j:j + n, :], oq.unsqueeze(1).to_broadcast([P, n, SEQ]),
                                                window(kpad, PAD - OFFSETS[i0], step, n, SEQ), ALU.mult)
                    ins.then_inc(prod_ready.s, 1)
                    if s >= 3 and s % 2:
                        logits(s // 2 - 1)
                logits(NSLOT // 2 - 1)
            def offset_softmax(_, b):
                def by_head(t):
                    return ltok[:, t, :, :].rearrange("p o h -> p h o")

                dve.wait_ge(const_set, 10)
                for t in range(TT):
                    for half in range(2):
                        ps = see(doubles, "oturn", b, t, half)
                        dve.tensor_tensor(ltok[:, t, 20 * half:20 * half + 20, :],
                                          ps[:, 0:5 * P].rearrange("p (s r) -> p s r", r=32)[:, :, 0:H],
                                          pbias[:, t, 20 * half:20 * half + 20, :], ALU.add).then_inc(ltok_ready.s, 1)
                    after(ltok_ready, b, t, 1)
                    link(dve.tensor_reduce(rinv[:, b, t, :], by_head(t), AX.X, ALU.max))
                    dve.tensor_tensor(ltok[:, t, :, :], ltok[:, t, :, :],
                                      rinv[:, b, t, :].unsqueeze(1).to_broadcast([P, 4 * NSLOT, H]),
                                      ALU.subtract).then_inc(lmax_ready.s, 1)
                for t in range(TT):
                    after(lexp_ready, b, t)
                    link(dve.tensor_reduce(rinv[:, b, t, :], by_head(t), AX.X, ALU.add))
                    link(dve.reciprocal(negm[:, b, t, :], rinv[:, b, t, :]))
                    link(dve.tensor_tensor(negm[:, b, t, :], negm[:, b, t, :], gain[:, :], ALU.mult))
                    dve.tensor_tensor(ltok[:, t, :, :], ltok[:, t, :, :],
                                      negm[:, b, t, :].unsqueeze(1).to_broadcast([P, 4 * NSLOT, H]),
                                      ALU.mult).then_inc(lprob_ready.s, 1)

            def offset_values(_, b):
                pv = prod[:, :, :, :].rearrange("p r s t -> p r (s t)")
                for t in range(TT):
                    for g in range(5):
                        ps = see(doubles, "oprob", b, t, g)
                        k = groups.index((b, t, g))
                        if k % 10 >= 2:
                            after(pv_used, *groups[k - 2])
                        n = 8 if g < 4 else 6
                        o = pv[:, g_ring(b, t, g), :].rearrange("p (i t) -> p i t", t=P)
                        for i0, m, step in offset_runs(8 * g, n):
                            j = i0 - 8 * g
                            ins = dve.tensor_tensor(o[:, j:j + m, :],
                                                    ps[:, j * P:(j + m) * P].rearrange("p (i t) -> p i t", t=P),
                                                    window(vpad, PAD + t * P - OFFSETS[i0], step, m, P), ALU.mult)
                        ins.then_inc(pv_ready.s, 1)
                after(pv_used, b, 1, 4)
                after(gth_ready, b)
                dve.scalar_tensor_tensor(out=oacc, in0=xn[:, b, :, :].rearrange("p t d -> p (t d)"), scalar=1.0,
                                         in1=accum_t[:, b, 0:SEQ], op0=ALU.add, op1=ALU.mult).then_inc(og_ready.s, 1)
                tokens_out("o", b, "o_bo")

            emit = {"stats": stats, "norm": norm, "rms": rms, "rms_norm": rms_norm, "project": att_scale,
                    "split": att_split, "max": att_max, "split_max": att_maxT,
                    "back": att_back, "out": att_out, "cross_project": cross_project, "cross_khat": cross_khat,
                    "cross_scores": cross_scores, "cross_turn": cross_turn, "cross_out": cross_out,
                    "logits": ffn_logits, "chunk": ffn_chunk, "select": select, "offset_scores": offset_scores, "offset_softmax": offset_softmax,
                    "offset_values": offset_values}
            with dve.Fori(0, iters):
                after(inputs_in, "all")
                link(dve.tensor_copy(maskf[:, :, :], mask8[:, :, :]))
                dve.tensor_scalar(maskneg[:, :, :], maskf[:, :, :], -1.0, 1e8, ALU.add,
                                  ALU.mult).then_inc(mask_ready.s, 1)
                for step, *key in plan:
                    if step in emit:
                        emit[step](*key)
                dve.drain().then_inc(x_final.s, 1)
                end_of_iteration(dve)

        @block.gpsimd
        def _(pool):
            def after(sig, *key):
                pool.wait_ge(sig.s, sig.at(*key))

            steps = Steps(pool, pool_done)
            link = steps.link

            def inverse_root(step, s, b):
                mine = slice(b * TT, (b + 1) * TT)
                y, v, tmp = rstd[:, mine], var[:, mine], nt[:, mine]
                after(v_stats, step, s, b)
                link(pool.tensor_scalar(y.bitcast(I32), v.bitcast(I32), -0.5, ROOT_GUESS, ALU.mult, ALU.add))
                for i in range(3):
                    link(pool.tensor_tensor(tmp, y, y, ALU.mult))
                    link(pool.tensor_tensor(tmp, tmp, v, ALU.mult))
                    link(pool.tensor_scalar(tmp, tmp, -0.5, 1.5, ALU.mult, ALU.add))
                    ins = pool.tensor_tensor(y, y, tmp, ALU.mult)
                    if i < 2:
                        link(ins)
                ins.then_inc(rstd_ready.s, 1)

            def swish(f, b, c):
                if f != "f0" or c >= CHUNKS[f]:
                    return
                after(sg_ready, f, b, c)
                if c >= 2:
                    after(hid_ready, f, b, c - 2)
                pool.tensor_tensor(vb[:, b, c % 2, :], ab[:, b, c % 2, :], sg[:, b, c % 2, :],
                                   ALU.mult).then_inc(t_ready.s, 1)

            pool.wait_ge(pbias_in, 16 * TT)
            pool.wait_ge(const_set, 9)
            for i in range(4 * NSLOT):
                for t in range(TT):
                    o = pbias[:, t, i, :]
                    if i >= NOFF:
                        ins = pool.memset(o, NEG)
                    else:
                        ins = pool.affine_select(out=o, in_=o, compare_op=ALU.is_ge, fill=NEG,
                                                 base=t * P - OFFSETS[i], pattern=[[0, H]], channel_multiplier=1)
            pool.drain().then_inc(const_set, 1)

            with pool.Fori(0, iters):
                after(inputs_in, "all")
                for step, *key in plan:
                    if step == "chunk":
                        swish(*key)
                    elif step in ("stats", "rms"):
                        inverse_root(step, *key)
                end_of_iteration(pool)

        @block.sync
        def _(sp):
            def after(sig, *key):
                sp.wait_ge(sig.s, sig.at(*key))

            sp.dma_start(cb[:, :], packed_bf).then_inc(group_loaded[0], 16)
            a, z = GROUP[0]
            sp.dma_start(wt[:, a:z], packed[:, a:z]).then_inc(group_loaded[0], 16)
            for t in range(TT):
                sp.dma_start(pbias[:, t, :, :], rows_pb).then_inc(pbias_in, 16)

            for b in two:
                for kind in range(2):
                    sp.dma_start(image_q[kind, b, SLOTS - 1], rows_q[kind]).then_inc(images_set, 16)
                    sp.dma_start(image_k[kind, b, SLOTS - 1], rows_k[kind]).then_inc(images_set, 16)
                    sp.dma_start(image_kc[kind, b, SLOTS - 1], rows_q[0, :, 0:CTX]).then_inc(images_set, 16)

            def stack(s, b):
                nk = ATT[s][0]
                image_keys = image_k if nk == SEQ else image_kc
                biased = int(s in ("a1", "a2"))
                for c, ready in ((0, part0), (1, part1), (2, parts_ready)):
                    after(ready, s, b)
                    for image, n, at, slots in ((image_q, SEQ, 0, Q_SLOTS), (image_keys, nk, SEQ, K_SLOTS)):
                        first, step, count = slots[c]
                        v = image[biased, b, first]
                        dst = bass.AP(v.tensor, v.offset, [[n, P], [step * P * n, count], [1, n]])
                        src = parts[:, b, c, at:at + n].unsqueeze(1).to_broadcast([P, count, n])
                        sp.dma_start(dst, src).then_inc(scratch_in.s, 16)
                after(scratch_in, s, b)
                if s == "a2":
                    after(mask_stored, "all")
                half = H // 2
                for odd in range(2):
                    rows = slice(64 * odd, 64 * odd + HD * SLOTS)
                    for image, n, dst in ((image_q, SEQ, qs[rows, b, :, :]), (image_keys, nk, ks[rows, b, odd, :, 0:nk])):
                        v = image[biased, b, 0, 64 * odd:64 * odd + 64, :]
                        src = bass.AP(v.tensor, v.offset, [[P * n, SLOTS], [half * n, HD], [1, half * n]])
                        sp.dma_start(dst, src).then_inc(stack_ready[b].s, 16)

            with sp.Fori(0, iters) as i:
                for b in two:
                    sp.dma_start(x[:, b, :, :], x_in[bass.ts(i, 1), b].rearrange("i t p d -> p (i t) d")).then_inc(
                        inputs_in.s, 16)
                    sp.dma_start(ctok[:, b, :], ctx_in[bass.ts(i, 1), b].rearrange("i k d -> k (i d)")).then_inc(
                        inputs_in.s, 16)
                    sp.dma_start(mask8[:, b, :], mask_in[bass.ts(i, 1), b, :].to_broadcast([P, CTX])).then_inc(
                        inputs_in.s, 16)
                after(mask_ready, "all")
                for b in two:
                    for odd in range(2):
                        sp.dma_start(image_kc[1, b, SLOTS - 1, 64 * odd:64 * odd + H // 2, :],
                                     maskneg[0:H // 2, b, :]).then_inc(mask_stored.s, 16)
                sp.wait_ge(const_set, 9)
                sp.wait_ge(images_set, 16 * 6 * PAIR)
                for s, b in during("split"):
                    stack(s, b)
                after(x_final, "all")
                for b in two:
                    sp.dma_start(out[bass.ts(i, 1), b].rearrange("i t p d -> p (i t) d"), x[:, b, :, :]).then_inc(
                        out_stored.s, 16)
                after(out_stored, "all")
                after(mask_stored, "all")
                sp.wait_ge(all_ended, 4)
                sp.sem_clear(counted)
                sp.sem_inc(go_on, 1)
                sp.wait_ge(went_on, 4)
                for s_ in (all_ended, go_on, went_on):
                    sp.sem_clear(s_)


def layout(inputs):
    f = {k: np.asarray(v) for k, v in inputs.items()}
    f32 = np.float32

    def rows(a, n=P):
        a = np.asarray(a).reshape(np.asarray(a).shape[0], -1)
        return np.concatenate([a, np.zeros((n - a.shape[0], a.shape[1]), a.dtype)]) if a.shape[0] < n else a

    def bc(v):
        return np.broadcast_to(np.asarray(v).reshape(1, -1), (P, np.asarray(v).size))

    def col(v):
        return np.asarray(v).reshape(P, 1)

    order = np.array([(2 * p + two) * HD + d for two in range(2) for d in range(HD) for p in range(H // 2)])
    pairs = np.array([0, 2, 4, 6, 1, 3, 5, 7])
    swapped = np.array([1, 3, 5, 7, 0, 2, 4, 6])

    def rotary(which):
        return np.array([(2 * p + two) * HD + which[d] for two in range(2) for d in range(HD) for p in range(H // 2)])

    def chunked(a):
        return np.asarray(a).transpose(1, 0, 2).reshape(a.shape[1], -1)

    m = {}
    m["ident"] = np.eye(P, dtype=f32)
    blk = np.zeros((P, 32), f32)
    blk[np.arange(P), np.arange(P) // HD] = HD ** -0.5
    m["blk"] = blk
    hm = np.zeros((P, 32), f32)
    hm[np.arange(P), np.arange(P) // HD] = 1.0
    m["headmask"] = hm
    m["sixteen"] = bc(np.arange(16, dtype=f32))
    W, b = f["L0_attn_W_qkv"], f["L0_attn_b_qkv"]
    m["a0_Wq"], m["a0_Wk"], m["a0_Wv"] = W[:, :P][:, order], W[:, P:2 * P][:, order], W[:, 2 * P:]
    m["a0_bq"], m["a0_bk"], m["a0_bv"] = col(b[:P][order]), col(b[P:2 * P][order]), bc(b[2 * P:])
    m["a0_Wo"], m["a0_bo"] = f["L0_attn_W_proj"], bc(f["L0_attn_b_proj"])
    m["a0_AT"] = rows(f["L0_attn_A_qkv"].T)
    Bq = f["L0_attn_B_qkv"]
    m["a0_B"] = rows(np.concatenate([Bq[:, :P][:, order], Bq[:, P:2 * P][:, order], Bq[:, 2 * P:]], 1))
    m["a0_AoT"], m["a0_Bo"] = rows(f["L0_attn_A_proj"].T), rows(f["L0_attn_B_proj"])
    for n in "qkvr":
        m[f"x0_W{n}"] = f[f"L0_xattn_W{n}"]
    m["x0_bq"], m["x0_bk"], m["x0_br"] = (col(f[f"L0_xattn_b{n}"]) for n in "qkr")
    m["x0_bv"] = bc(f["L0_xattn_bv"])
    w1, b1 = f["L0_ffn_w1"], f["L0_ffn_b1"]
    m["f0_ns"], m["f0_wg"], m["f0_bg"] = col(f["L0_ffn_norm_scale"]), f["L0_ffn_wg"], bc(f["L0_ffn_bg"])
    m["f0_w1"], m["f0_w3"] = chunked(w1[:, :, 0::2]), chunked(w1[:, :, 1::2])
    m["f0_w2"] = chunked(f["L0_ffn_w2"])
    m["f0_b1"], m["f0_b3"], m["f0_bt"] = b1[:, 0::2].T, b1[:, 1::2].T, rows(f["L0_ffn_b2"])
    W = f["L1_attn_W_kqv"].T
    m["a1_Wk"], m["a1_Wq"], m["a1_Wv"] = W[:, :P][:, order], W[:, P:2 * P][:, order], W[:, 2 * P:]
    ws = f["L1_xattn_w_sim"]
    m["x1_w1"], m["x1_w3"], m["x1_w2"] = col(ws[:P]), col(ws[2 * P:]), col(ws[P:2 * P])
    m["x1_bs"], m["x1_Wqv"], m["x1_b"] = bc(f["L1_xattn_b_sim"]), chunked(f["L1_xattn_W_qv"].reshape(4, P, P)), bc(f["L1_xattn_b_qv"])
    m["f1_wg"], m["f1_bg"] = f["L1_ffn_gate_w"], bc(f["L1_ffn_gate_b"])
    for to, n in (("w1", "w1"), ("w3", "w2")):
        m[f"f1_{to}"] = chunked(np.concatenate([f[f"L1_ffn_r{n}"], f[f"L1_ffn_s{n}"]]))
    m["f1_w2"] = chunked(np.concatenate([f["L1_ffn_rw3"], f["L1_ffn_sw3"]]).reshape(CH1, P, P))
    for to, n in (("b1", "b1"), ("b3", "b2")):
        m[f"f1_{to}"] = np.concatenate([f[f"L1_ffn_r{n}"], f[f"L1_ffn_s{n}"]]).reshape(CH1, P).T
    m["f1_bt"] = rows(np.concatenate([f["L1_ffn_rb3"], f["L1_ffn_sb3"]]))
    W, b = f["L2_attn_qkv_w"].T, f["L2_attn_qkv_b"]
    for i, n in enumerate("qkv"):
        m[f"o_W{n}"], m[f"o_b{n}"] = W[:, i * P:(i + 1) * P], col(b[i * P:(i + 1) * P])
    m["o_Wg"], m["o_bg"] = f["L2_attn_gate_w"].T, col(f["L2_attn_gate_b"])
    m["o_Wo"], m["o_bo"], m["o_gain"] = f["L2_attn_out_w"].T, bc(f["L2_attn_out_b"]), bc(f["L2_attn_if_gain"])
    perm = np.array([SORTED.index(o) for o in OFFSETS] + [0] * (4 * NSLOT - NOFF))
    m["o_emb"] = np.tile(f["L2_attn_scale_embed"][perm].T, (H, 1))
    pos_bias = np.ascontiguousarray(bc(f["L2_attn_pos_bias"][perm])).reshape(P, 4 * NSLOT, H)
    for n, t in (("q", "q"), ("k", "k")):
        m[f"a2_W{n}"], m[f"a2_b{n}"] = f[f"L2_xattn_W{n}"].T[:, order], col(f[f"L2_xattn_b{n}"][order])
    m["a2_Wv"], m["a2_bv"] = f["L2_xattn_Wv"].T, bc(f["L2_xattn_bv"])
    m["a2_Wo"], m["a2_bo"] = f["L2_xattn_Wo"].T, bc(f["L2_xattn_bo"])
    m["f2_wg"] = f["L2_ffn_gate_w"][:E2].T
    m["f2_w1"], m["f2_w3"] = chunked(f["L2_ffn_w1"][:E2]), chunked(f["L2_ffn_w3"][:E2])
    m["f2_w2"] = chunked(f["L2_ffn_w2"][:E2].reshape(CH2, P, P))
    W, b = f["L3_attn_qkv_w"], f["L3_attn_qkv_b"]
    for i, n in enumerate("qk"):
        Wn, bn_ = W[:, i * P:(i + 1) * P], b[i * P:(i + 1) * P]
        m[f"a3_W{n}"], m[f"a3_b{n}"] = Wn[:, rotary(pairs)], col(bn_[rotary(pairs)])
        m[f"a3_W{n}s"], m[f"a3_b{n}s"] = Wn[:, rotary(swapped)], col(bn_[rotary(swapped)])
    m["a3_Wv"], m["a3_bv"] = W[:, 2 * P:], bc(b[2 * P:])
    m["a3_Wo"], m["a3_bo"] = f["L3_attn_out_w"], bc(f["L3_attn_out_b"])
    inv_freq = (f32(1.0) / f32(10000.0) ** (np.arange(0, HD, 2, dtype=f32) / f32(HD))).astype(f32)
    freqs = np.arange(SEQ, dtype=f32)[:, None] * inv_freq[None, :]
    table = np.concatenate([np.sin(freqs), np.cos(freqs)], -1).astype(f32)
    sin, cos = table[:, 0::2], table[:, 1::2]
    C = np.concatenate([cos, cos], 1).T
    S = np.concatenate([-sin, sin], 1).T
    at = np.array([d for two in range(2) for d in range(HD) for p in range(H // 2)])
    m["rope"] = np.concatenate([C[at], S[at]], 1).astype(f32)
    for n in "qk":
        m[f"a4_W{n}"] = f[f"L3_xattn_W_{n}"][:, order]
    m["a4_Wv"], m["a4_Wo"], m["a4_bo"] = f["L3_xattn_W_v"], f["L3_xattn_W_o"], bc(f["L3_xattn_b_o"])
    m["f3_wr"], m["f3_br"], m["f3_w1"] = f["L3_ffn_w_r"], bc(f["L3_ffn_b_r"]), f["L3_ffn_W1"]
    m["f3_w2"] = chunked(f["L3_ffn_W2"].reshape(CH3, P, P))
    m["f3_b1"], m["f3_b2"] = f["L3_ffn_b1"].reshape(CH3, P).T, bc(f["L3_ffn_b2"])
    for name, (_, n) in COLS.items():
        assert m[name].shape == (P, n), (name, m[name].shape, n)
    packed = np.concatenate([np.asarray(m[name], f32) for g in LAYOUT for name, _ in g], 1)

    bf = mybir.dt.np(BF16)
    sel = np.zeros((P, H), f32)
    for h in range(H):
        for part in range(3):
            sel[32 * part + h, h] = 1.0
    i = np.arange(P)
    qk_mask = np.where(i[None, :] <= i[:, None], 0.0, NEG)
    zero = np.zeros((P, P))
    packed_bf = np.concatenate([sel.reshape(P, -1), np.eye(P), qk_mask, zero, qk_mask,
                                qk_mask.T, zero, qk_mask.T], 1).astype(bf)
    base = (2 ** 8) ** (1.0 / H)
    slopes = np.array([1.0 / base ** (h + 1) for h in range(H)], f32)
    bias = (slopes[:, None] * np.arange(SEQ, dtype=f32)[None, :]).astype(f32)
    p0 = bias.astype(bf)
    p1 = (bias - p0.astype(f32)).astype(bf)
    p2 = (bias - p0.astype(f32) - p1.astype(f32)).astype(bf)
    rows_q, rows_k = np.zeros((2, 2, HD, H // 2, SEQ), bf), np.zeros((2, 2, HD, H // 2, SEQ), bf)
    rows_q[1, :, 0:3] = 1
    for odd in range(2):
        for part, p in enumerate((p0, p1, p2)):
            rows_k[1, odd, part] = p[odd::2]
    n = B // PAIR
    return {
        "x": np.ascontiguousarray(f["x"]).reshape(n, PAIR, TT, P, P),
        "ctx": np.ascontiguousarray(f["ctx_1024"]).reshape(n, PAIR, CTX, P),
        "mask": np.ascontiguousarray(f["mask_BxS2_bf1"]).view(np.uint8).reshape(n, PAIR, CTX),
        "packed": packed, "packed_bf": packed_bf, "rows_q": rows_q.reshape(2, P, SEQ), "rows_k": rows_k.reshape(2, P, SEQ), "pos_bias": pos_bias,
    }


def build(nc, arrays, **kw):
    aps = [nc.dram_tensor(f"in_{k}", a.shape, mybir.dt.from_np(a.dtype), kind="ExternalInput").ap()
           for k, a in arrays.items()]
    images = [nc.dram_tensor(n, [2, PAIR, SLOTS, P, t], BF16, kind="Internal").ap()
              for n, t in (("image_q", SEQ), ("image_k", SEQ), ("image_kc", CTX))]
    out = nc.dram_tensor("out", [B // PAIR, PAIR, TT, P, P], F32, kind="ExternalOutput").ap()
    build_decoder(nc, *aps, *images, out, **kw)


def kernel(**inputs):
    import concourse.bacc as bacc
    from concourse.bass_utils import run_bass_kernel_spmd

    arrays = layout(inputs)
    nc = bacc.Bacc("TRN2", target_bir_lowering=False, num_devices=1)
    build(nc, arrays)
    r = run_bass_kernel_spmd(nc, [{f"in_{k}": a for k, a in arrays.items()}], core_ids=[0])
    return np.asarray(r.results[0]["out"]).reshape(B, SEQ, P)
```
